# Optimizing a Trainium2 kernel written in Bass

```python
import numpy as np
import jax
import jax.numpy as jnp

def _softmax(x, axis=-1):
    return jax.nn.softmax(x, axis=axis)

def _gelu(x):
    return jax.nn.gelu(x, approximate=True)

def _silu(x):
    return jax.nn.silu(x)

def _sigmoid(x):
    return jax.nn.sigmoid(x)

def _layernorm(x, axis=-1, eps=1e-05):
    m = jnp.mean(x, axis=axis, keepdims=True)
    v = jnp.var(x, axis=axis, keepdims=True)
    return (x - m) / jnp.sqrt(v + eps)

def _scatter_add(tgt, idx, src, axis=0):
    return tgt.at[idx].add(src)

def _segment_sum(src, seg, n):
    return jax.ops.segment_sum(src, seg, n)
kernel_name = 'mk_metaformer_d1_conv_nchw768_r4_6ead0f'

def setup_inputs(seed: int=0):
    np.random.seed(seed)
    _w = jnp.asarray

    def _rec_inputs():
        import jax
        import jax.numpy as jnp
        _gk = jax.random.key(seed)
        x = -0.0002221 + 1 * jax.random.normal(jax.random.fold_in(_gk, 1), (8, 192, 16, 16), jnp.float32)
        return x
    x = _rec_inputs()

    def _L0_conv_setup():
        import jax, jax.numpy as jnp
        import numpy as np
        WS = 8
        NH = 12
        DM = 192
        HD = DM // NH
        SCALE = float(HD) ** 0.5

        def _make_rel_coords():
            coords = np.stack(np.meshgrid(np.arange(WS), np.arange(WS), indexing='ij'))
            coords = coords.reshape(2, -1)
            rel = coords[:, :, None] - coords[:, None, :]
            rel = rel.transpose(1, 2, 0) + (WS - 1)
            rel[:, :, 0] *= 2 * WS - 1
            return jnp.asarray(rel.sum(-1), dtype=jnp.int32)
        key = jax.random.key(seed)
        ks = jax.random.split(key, 7)
        B, H, W = (8, 16, 16)
        return {'x': jax.random.normal(ks[0], (B, DM, H, W), dtype=jnp.float32), 'Wq': jax.random.normal(ks[1], (DM, DM), dtype=jnp.float32) * 0.02, 'Wk': jax.random.normal(ks[2], (DM, DM), dtype=jnp.float32) * 0.02, 'Wv': jax.random.normal(ks[3], (DM, DM), dtype=jnp.float32) * 0.02, 'Wo_w': jax.random.normal(ks[4], (DM, DM), dtype=jnp.float32) * 0.02, 'Wo_b': jax.random.normal(ks[5], (DM,), dtype=jnp.float32) * 0.02, 'rel_pos_bias': jax.random.normal(ks[6], (NH, (2 * WS - 1) ** 2), dtype=jnp.float32) * 0.02, 'rel_coords': _make_rel_coords()}
    _L0_conv_all = _L0_conv_setup()
    _L0_conv_in = {k: v for k, v in _L0_conv_all.items() if k in ('Wq', 'Wk', 'Wv', 'Wo_w', 'Wo_b', 'rel_pos_bias', 'rel_coords')}
    del _L0_conv_all

    def _L0_ffn_setup():
        import jax, jax.numpy as jnp
        import numpy as np
        D_MODEL = 192
        D_FF = 768
        N_EXPERTS = 9
        key = jax.random.key(seed)
        ks = jax.random.split(key, 7)
        scale = 0.02
        return {'x': jax.random.normal(ks[0], (2, 256, D_MODEL), jnp.float32), 'Ws': jax.random.normal(ks[1], (D_MODEL, N_EXPERTS), jnp.float32) * scale, 'bs': jnp.zeros((N_EXPERTS,), jnp.float32), 'W1': jax.random.normal(ks[2], (N_EXPERTS, D_MODEL, D_FF), jnp.float32) * scale, 'b1': jnp.zeros((N_EXPERTS, D_FF), jnp.float32), 'W2': jax.random.normal(ks[3], (N_EXPERTS, D_FF, D_MODEL), jnp.float32) * scale, 'b2': jnp.zeros((N_EXPERTS, D_MODEL), jnp.float32)}
    _L0_ffn_all = _L0_ffn_setup()
    _L0_ffn_in = {k: v for k, v in _L0_ffn_all.items() if k in ('Ws', 'bs', 'W1', 'b1', 'W2', 'b2')}
    del _L0_ffn_all
    return {'x': x, 'L0_conv_Wq': _L0_conv_in['Wq'], 'L0_conv_Wk': _L0_conv_in['Wk'], 'L0_conv_Wv': _L0_conv_in['Wv'], 'L0_conv_Wo_w': _L0_conv_in['Wo_w'], 'L0_conv_Wo_b': _L0_conv_in['Wo_b'], 'L0_conv_rel_pos_bias': _L0_conv_in['rel_pos_bias'], 'L0_conv_rel_coords': _L0_conv_in['rel_coords'], 'L0_ffn_Ws': _L0_ffn_in['Ws'], 'L0_ffn_bs': _L0_ffn_in['bs'], 'L0_ffn_W1': _L0_ffn_in['W1'], 'L0_ffn_b1': _L0_ffn_in['b1'], 'L0_ffn_W2': _L0_ffn_in['W2'], 'L0_ffn_b2': _L0_ffn_in['b2']}

def reference(x, L0_conv_Wq, L0_conv_Wk, L0_conv_Wv, L0_conv_Wo_w, L0_conv_Wo_b, L0_conv_rel_pos_bias, L0_conv_rel_coords, L0_ffn_Ws, L0_ffn_bs, L0_ffn_W1, L0_ffn_b1, L0_ffn_W2, L0_ffn_b2):
    import jax
    import jax.numpy as jnp

    def _L0_conv_ref(x, Wq, Wk, Wv, Wo_w, Wo_b, rel_pos_bias, rel_coords):
        import jax, jax.numpy as jnp
        import numpy as np
        WS = 8
        NH = 12
        DM = 192
        HD = DM // NH
        SCALE = float(HD) ** 0.5

        def _make_rel_coords():
            coords = np.stack(np.meshgrid(np.arange(WS), np.arange(WS), indexing='ij'))
            coords = coords.reshape(2, -1)
            rel = coords[:, :, None] - coords[:, None, :]
            rel = rel.transpose(1, 2, 0) + (WS - 1)
            rel[:, :, 0] *= 2 * WS - 1
            return jnp.asarray(rel.sum(-1), dtype=jnp.int32)
        B, C, H, W = x.shape
        nh, nw = (H // WS, W // WS)
        L = WS * WS
        xw = x.reshape(B, C, nh, WS, nw, WS).transpose(0, 2, 4, 3, 5, 1).reshape(B, nh, nw, L, C)

        def proj(Wm):
            y = jnp.einsum('bhwlc,oc->bhwlo', xw, Wm)
            return y.reshape(B, nh, nw, L, NH, HD).transpose(0, 1, 2, 4, 3, 5)
        q, k, v = (proj(Wq), proj(Wk), proj(Wv))
        bias = rel_pos_bias[:, rel_coords]
        attn = jnp.einsum('bhwnld,bhwnmd->bhwnlm', q, k) / SCALE + bias
        p = jax.nn.softmax(attn, axis=-1)
        o = jnp.einsum('bhwnlm,bhwnmd->bhwnld', p, v)
        o = o.reshape(B, nh, nw, NH, WS, WS, HD)
        o = o.transpose(0, 3, 6, 1, 4, 2, 5).reshape(B, C, H, W)
        return jnp.einsum('bchw,oc->bohw', o, Wo_w) + Wo_b[None, :, None, None]

    def _L0_ffn_ref(x, Ws, bs, W1, b1, W2, b2):
        import jax, jax.numpy as jnp
        import numpy as np
        D_MODEL = 192
        D_FF = 768
        N_EXPERTS = 9
        B, S, d = x.shape
        xt = x.reshape(-1, d)
        route_prob = jax.nn.softmax(xt @ Ws + bs, axis=-1)
        p = jnp.max(route_prob, axis=-1)
        routes = jnp.argmax(route_prob, axis=-1)
        h = jax.nn.gelu(jnp.einsum('td,edf->tef', xt, W1) + b1, approximate=False)
        out = jnp.einsum('tef,efd->ted', h, W2) + b2
        common = out[:, 0, :]
        sel = jnp.take_along_axis(out, routes[:, None, None], axis=1)[:, 0, :]
        scaling = (p / jax.lax.stop_gradient(p))[:, None]
        pe = p[:, None]
        final = jnp.where((routes == 0)[:, None], common * scaling, pe * sel + (1.0 - pe) * common)
        return final.reshape(B, S, d)

    def _gn(v, G=32, eps=1e-05):
        B_, C_, H_, W_ = v.shape
        g = v.reshape(B_, G, C_ // G, H_, W_)
        m = jnp.mean(g, axis=(2, 3, 4), keepdims=True)
        s = jnp.var(g, axis=(2, 3, 4), keepdims=True)
        return ((g - m) / jnp.sqrt(s + eps)).reshape(v.shape)

    def _ln_c(v, eps=1e-06):
        m = jnp.mean(v, axis=1, keepdims=True)
        s = jnp.var(v, axis=1, keepdims=True)
        return (v - m) / jnp.sqrt(s + eps)

    def _ln_t(v, eps=1e-05):
        m = jnp.mean(v, axis=-1, keepdims=True)
        s = jnp.var(v, axis=-1, keepdims=True)
        return (v - m) / jnp.sqrt(s + eps)

    def _to_tokens(v):
        B_, C_, H_, W_ = v.shape
        return v.reshape(B_, C_, H_ * W_).transpose(0, 2, 1)

    def _from_tokens(t, like):
        B_, C_, H_, W_ = like.shape
        return t.transpose(0, 2, 1).reshape(B_, C_, H_, W_)
    x = x + _L0_conv_ref(_ln_c(x), L0_conv_Wq, L0_conv_Wk, L0_conv_Wv, L0_conv_Wo_w, L0_conv_Wo_b, L0_conv_rel_pos_bias, L0_conv_rel_coords)
    t = _to_tokens(x)
    t = t + _L0_ffn_ref(_ln_t(t), L0_ffn_Ws, L0_ffn_bs, L0_ffn_W1, L0_ffn_b1, L0_ffn_W2, L0_ffn_b2)
    x = _from_tokens(t, x)
    return x

_drawn_inputs = setup_inputs


def setup_inputs(seed=0):
    import zlib

    import numpy as np

    out = dict(_drawn_inputs(seed))
    spreads = {'L0_ffn_bs': (0.0, 2.0), 'L0_ffn_b1': (0.0, 0.316), 'L0_ffn_b2': (0.0, 0.1)}
    factors = {'L0_conv_Wq': 8.0,
     'L0_conv_Wk': 8.0,
     'L0_conv_Wv': 5.713,
     'L0_conv_Wo_w': 5.68,
     'L0_conv_rel_pos_bias': 8.0,
     'L0_ffn_Ws': 2.694,
     'L0_conv_Wo_b': 5.44}
    for name, (base, spread) in spreads.items():
        noise = np.random.default_rng([zlib.crc32(name.encode()), seed]).standard_normal(out[name].shape)
        drawn = base * np.exp(spread * noise) if base else spread * noise
        out[name] = jnp.asarray(drawn.astype(out[name].dtype))
    for name, factor in factors.items():
        out[name] = (out[name] * factor).astype(out[name].dtype)
    return out
```

```python
from contextlib import ExitStack

import concourse.bass as bass
from concourse import mybir

F32 = mybir.dt.float32
F16 = mybir.dt.float16
I32 = mybir.dt.int32
U32 = mybir.dt.uint32
ALU = mybir.AluOpType
ACT = mybir.ActivationFunctionType
AX = mybir.AxisListType.X

B, C, IMG = 8, 192, 16
WS, NH = 8, 12
HD = C // NH
L = WS * WS
T = 128
NT = B * IMG * IMG // T
TPI = IMG * IMG // T
CH = 96
NE, FF = 9, 768
NF = FF // 128
NR = (NT * T + NE * (T - 1)) // T
TBL = (2 * WS - 1) ** 2
TH = TBL // 3
HA = 128 // HD
HC = NH - HA
RC = HC * HD
NP = NH // 2
VW = HD + 1

PASSES = ((0, 0), (0, 1), (1, 0))
SA = 16.0
SF = 64.0
S_SCALE = 1.0 / (float(HD) ** 0.5 * SA * SA)


def to_windows(ap):
    return ap.rearrange("p (w i j) -> p i w j", w=2, j=WS)


def to_raster(ap):
    return ap.rearrange("p (i w j) -> p w i j", w=2, j=WS)


def build(nc, x, Wq, Wk, Wv, Wo_w, Wo_b, rpb, rel, Ws, bs, W1, b1, W2, b2, out):
    xs = nc.dram_tensor("sorted_tokens", (NR * T, 2 * C), F16, kind="Internal").ap()
    ys = nc.dram_tensor("sorted_outputs", (NR * T, C), F32, kind="Internal").ap()
    with ExitStack() as whole:
        def sbw(name, shape, dt):
            return whole.enter_context(nc.sbuf_tensor(name, shape, dt))

        def sem(name):
            return whole.enter_context(nc.semaphore(name))

        ident = sbw("ident", [128, 128], F32)
        ident16 = sbw("ident16", [128, 128], F16)
        ones16 = sbw("ones16", [128, 128], F16)
        w1s = sbw("w1s", [CH + 1, NE, 2, 2, FF], F16)
        w2s = sbw("w2s", [128, NE, 2, NF, C], F16)
        x2 = sbw("x2", [128, NT, C], F32)
        xhl = sbw("xhl", [128, NT, 2, C], F16)
        xhT = sbw("xhT", [CH + 1, NT, 2, 2, T], F16)
        pmax = sbw("pmax", [128, NT], F32)
        omp = sbw("omp", [128, NT], F32)
        slot = sbw("slot", [128, NT], U32)
        etile = sbw("etile", [1, NR], I32)

        attention(nc, locals())
        experts(nc, locals())


def attention(nc, g):
    (ident, ident16, ones16, w1s, w2s,  x2, xhl, xhT, pmax, omp, slot, etile, xs) = (
        g[n] for n in ("ident", "ident16", "ones16", "w1s", "w2s", "x2", "xhl", "xhT",
                       "pmax", "omp", "slot", "etile", "xs"))
    x, Wo_b, rpb, rel, Ws, bs, W1, b1, W2, b2 = (
        g[n] for n in ("x", "Wo_b", "rpb", "rel", "Ws", "bs", "W1", "b1", "W2", "b2"))
    mats = [g["Wq"], g["Wk"], g["Wv"], g["Wo_w"]]
    VB = 4
    XI = 2
    with ExitStack() as ctx:
        def sb(name, shape, dt):
            return ctx.enter_context(nc.sbuf_tensor(name, shape, dt))

        def pb(name, cols, dt=F32):
            return ctx.enter_context(nc.psum_tensor(name, [128, cols], dt))

        def sem(name):
            return ctx.enter_context(nc.semaphore(name))

        xin = sb("xin", [CH, XI, 2, IMG * IMG], F32)
        w1stage = sb("w1stage", [CH + 1, 2, FF], F32)
        w2stage = sb("w2stage", [128, NF, C], F32)
        xn = sb("xn", [128, 2, C], F32)
        xnT = sb("xnT", [CH, 2, 2, 2, T], F16)
        qk = sb("qk", [128, 2, 2, 4 * T], F16)
        ka = sb("ka", [128, 2, 2, 2, HA, L], F16)
        kc = sb("kc", [RC, 2, 2, 2, HC, L], F16)
        v2 = sb("v2", [128, VB, 2, 2, NP, 2, VW], F16)
        sc = sb("sc", [128, 2, NH * L], F32)
        pT = sb("pT", [128, 2, 2, NP, T], F16)
        on = sb("on", [128, 2, C], F32)
        oT = sb("oT", [CH + 1, 2, 2, 2, T], F16)
        xhf = sb("xhf", [128, 2, C], F32)
        bias = sb("bias", [128, NH * L], F32)
        wT = sb("wT", [CH, 2, 2, 3 * C], F16)
        woT = sb("woT", [CH + 1, 2, 2, C], F16)
        wob = sb("wob", [CH + 1, C], F32)
        wsr = sb("wsr", [CH + 1, 2, NE], F32)
        ws16 = sb("ws16", [CH + 1, 2, 2, NE], F16)
        mask = sb("mask", [128, HA, L], F16)
        tab = sb("tab", [TH, 3, NH], F32)
        tab16 = sb("tab16", [TH, 2, 3, NH], F16)
        rowid = sb("rowid", [TH, 3], F32)
        stat = sb("stat", [128, 2, 2, 6], F32)
        mv = sb("mv", [128, 2, 2, 2], F32)
        rstd = sb("rstd", [128, 2, 2], F32)
        minus_half = sb("minus_half", [128, 1], F32)
        mx = sb("mx", [128, 2, NH], F32)
        rden = sb("rden", [128, NH], F32)
        lg = sb("lg", [128, NT, NE], F32)
        ex, cand = (b[:, :, :].rearrange("p a c -> p (a c)")[:, 0:NT * NE].rearrange(
            "p (t e) -> p t e", e=NE) for b in (xn, on))
        big = sc[:, 0, :]
        oh = sb("oh", [128, NT, NE], F16)
        r16 = sb("r16", [128, 4, NT], F32)
        tri = sb("tri", [128, 128], F16)
        eio = sb("eio", [128, NE], F32)
        kio = sb("kio", [128, NT], F32)
        jio = sb("jio", [1, NR], F32)
        ltm = sb("ltm", [128, NE, NE], F32)
        cnt = sb("cnt", [128, 4, NE], F32)
        ejf = sb("ejf", [1, 2, NR], F32)
        zeros = sb("zeros", [128, 2 * C], F16)
        late = w1s[:, :, :, :, :].rearrange("p e a k f -> p (e a k f)")
        per_e = 2 * 2 * FF
        idx = late[:, 2 * per_e:2 * per_e + 2 * L * L].bitcast(I32)
        hot = late[:, 2 * per_e + 2 * L * L:2 * per_e + 5 * L * L].rearrange("p (k n) -> p k n", k=3)
        watt = w2s[:, NE - 2:NE, :, :, :].rearrange("p e a f c -> p (e a f c)")[
            0:CH, 0:4 * 2 * C * 2].bitcast(F32).rearrange("p (m r c) -> p m r c", m=4, r=2)

        p_x = pb("p_x", 512)
        p_n = pb("p_n", 512)
        p_qk = pb("p_qk", 512)
        p_v = pb("p_v", 512)
        p_s = pb("p_s", 1024)
        p_t = [pb("p_t0", 512), pb("p_t1", 512)]

        x_loaded = [sem(f"x_loaded{i}") for i in range(XI)]
        watt_loaded = sem("watt_loaded")
        idx_loaded = sem("idx_loaded")
        small_loaded = sem("small_loaded")
        w1_loaded = sem("w1_loaded")
        w2_loaded = sem("w2_loaded")
        xs_zeroed = sem("xs_zeroed")
        consts0 = sem("consts0")
        consts = sem("consts")
        dve_consts = sem("dve_consts")
        wt_mm = sem("wt_mm")
        wt_hi = sem("wt_hi")
        wt_lo = sem("wt_lo")
        small_hi = sem("small_hi")
        small_lo = sem("small_lo")
        hot_ready = sem("hot_ready")
        bias_mm = sem("bias_mm")
        bias_ready = sem("bias_ready")
        w1_scaled = sem("w1_scaled")
        w2_scaled = sem("w2_scaled")
        w1_hi = sem("w1_hi")
        w1_lo = sem("w1_lo")
        w2_hi = sem("w2_hi")
        w2_lo = sem("w2_lo")
        xT_mm = sem("xT_mm")
        x_kept = sem("x_kept")
        stat1 = sem("stat1")
        mv1 = sem("mv1")
        rstd1a = sem("rstd1a")
        rstd1 = sem("rstd1")
        xn_ready = sem("xn_ready")
        xnT_mm = sem("xnT_mm")
        xnT_hi = sem("xnT_hi")
        xnT_lo = sem("xnT_lo")
        qk_mm = sem("qk_mm")
        v_mm = sem("v_mm")
        qk_hi = sem("qk_hi")
        qk_lo = sem("qk_lo")
        kbd_ready = sem("kbd_ready")
        v_hi = sem("v_hi")
        v_lo = sem("v_lo")
        s_mm = sem("s_mm")
        s_biased = sem("s_biased")
        s_max = sem("s_max")
        s_sub = sem("s_sub")
        p_ready = sem("p_ready")
        pT_mm = [sem("pT_mm0"), sem("pT_mm1")]
        pT_hi = [sem("pT_hi0"), sem("pT_hi1")]
        pT_lo = [sem("pT_lo0"), sem("pT_lo1")]
        pv_mm = sem("pv_mm")
        rden_ready = sem("rden_ready")
        o_norm = sem("o_norm")
        oT_mm = sem("oT_mm")
        oT_hi = sem("oT_hi")
        oT_lo = sem("oT_lo")
        wo_mm = sem("wo_mm")
        x2_ready = sem("x2_ready")
        stat2 = sem("stat2")
        mv2 = sem("mv2")
        rstd2a = sem("rstd2a")
        rstd2 = sem("rstd2")
        xh_ready = sem("xh_ready")
        xh_hi = sem("xh_hi")
        xh_lo = sem("xh_lo")
        xhT_mm = sem("xhT_mm")
        xhT_ready = sem("xhT_ready")
        lg_mm = sem("lg_mm")
        lg_kept = sem("lg_kept")
        chain = sem("chain")
        ex_in = sem("ex_in")
        ex_out = sem("ex_out")
        oh_ready = sem("oh_ready")
        rank_mm = sem("rank_mm")

        STEPS = NT + 11
        WINDOW_HEADS = [(w, h) for w in range(2) for h in range(2)]

        def values(w, h):
            return p_v[w * L:(w + 1) * L, 0:C].rearrange("p (n h d) -> p n h d", n=NP, h=2)[:, :, h, :]

        def stages(step, program):
            for stage, lag in program:
                t = step - lag
                if 0 <= t < NT:
                    stage(t)

        block = ctx.enter_context(nc.Block())

        @block.sync
        def _(sp):
            def image(b):
                if b >= XI:
                    sp.wait_ge(xT_mm, TPI * (b - XI + 1))
                sp.dma_start(xin[:, b % XI, :, :],
                             x[b].rearrange("(k c) i j -> c k (i j)", k=2)).then_inc(x_loaded[b % XI], 16)

            for m in range(4):
                sp.dma_start(watt[:, m, :, :],
                             mats[m].rearrange("(r o) c -> o r c", r=2)).then_inc(watt_loaded, 16)
            image(0)
            image(1)
            sp.dma_start(idx[0:TH, :], rel.rearrange("l m -> (l m)").unsqueeze(0).to_broadcast([TH, L * L])
                         ).then_inc(idx_loaded, 16)
            sp.dma_start(wob[CH:CH + 1, :], Wo_b.unsqueeze(0)).then_inc(small_loaded, 16)
            sp.dma_start(wsr[0:CH, :, :], Ws.rearrange("(k c) e -> c k e", k=2)).then_inc(small_loaded, 16)
            sp.dma_start(wsr[CH:CH + 1, 0, :], bs.unsqueeze(0)).then_inc(small_loaded, 16)
            with nc.allow_non_contiguous_dma(reason="small table, transposed once"):
                for k in range(3):
                    sp.dma_start(tab[:, k, :], rpb[:, k * TH:(k + 1) * TH].rearrange("h r -> r h")
                                 ).then_inc(small_loaded, 16)
            image(2)
            sp.wait_ge(dve_consts, 1)
            for e in range(NE):
                if e >= 1:
                    sp.wait_ge(w1_hi, e)
                    sp.wait_ge(w1_lo, e)
                sp.dma_start(w1stage[0:CH, :, :], W1[e].rearrange("(k c) f -> c k f", k=2)).then_inc(w1_loaded, 16)
                sp.dma_start(w1stage[CH:CH + 1, 0, :], b1[e].unsqueeze(0)).then_inc(w1_loaded, 16)
                sp.dma_start(w1stage[CH:CH + 1, 1, 0:C], b2[e].unsqueeze(0)).then_inc(w1_loaded, 16)
                if e >= 1:
                    sp.wait_ge(w2_hi, e)
                    sp.wait_ge(w2_lo, e)
                sp.dma_start(w2stage[:, :, :], W2[e].rearrange("(f p) c -> p f c", p=128)).then_inc(w2_loaded, 16)
                if e % 2 == 1 and (e + 5) // 2 < B:
                    image((e + 5) // 2)
            image(B - 1)
            sp.wait_ge(xs_zeroed, 16)

        @block.gpsimd
        def _(pool):
            pool.memset(ident[:, :], 0.0).then_inc(consts0, 1)
            pool.memset(ident16[:, :], 0.0).then_inc(consts0, 1)
            pool.memset(tri[:, :], 1.0).then_inc(consts0, 1)
            pool.memset(mask[:, :, :], 1.0).then_inc(consts0, 1)
            pool.memset(ltm[:, :, :], 1.0).then_inc(consts0, 1)
            pool.memset(zeros[:, :], 0.0).then_inc(consts0, 1)
            pool.memset(minus_half[:, :], -0.5).then_inc(consts0, 1)
            pool.wait_ge(consts0, 7)
            for m in (ident, ident16):
                pool.affine_select(out=m[:, :], in_=m[:, :], compare_op=ALU.not_equal, fill=1.0, base=0,
                                   pattern=[[-1, 128]], channel_multiplier=1).then_inc(consts0, 1)
            pool.affine_select(out=tri[:, :], in_=tri[:, :], compare_op=ALU.is_gt, fill=0.0, base=0,
                               pattern=[[1, 128]], channel_multiplier=-1).then_inc(consts0, 1)
            pool.affine_select(out=ltm[:, :, :], in_=ltm[:, :, :], compare_op=ALU.is_gt, fill=0.0, base=0,
                               pattern=[[1, NE], [-1, NE]], channel_multiplier=0).then_inc(consts0, 1)
            pool.affine_select(out=mask[:, :, :], in_=mask[:, :, :], compare_op=ALU.is_ge, fill=0.0, base=0,
                               pattern=[[-HD, HA], [0, L]], channel_multiplier=1).then_inc(consts0, 1)
            pool.wait_ge(consts0, 12)
            pool.affine_select(out=mask[:, :, :], in_=mask[:, :, :], compare_op=ALU.is_ge, fill=0.0, base=HD - 1,
                               pattern=[[HD, HA], [0, L]], channel_multiplier=-1).then_inc(consts0, 1)
            pool.iota(rowid[:, :], [[TH, 3]], base=0, channel_multiplier=1,
                      allow_small_or_imprecise_dtypes=True).then_inc(consts0, 1)
            pool.iota(eio[:, :], [[1, NE]], base=0, channel_multiplier=0,
                      allow_small_or_imprecise_dtypes=True).then_inc(consts0, 1)
            pool.iota(kio[:, :], [[T, NT]], base=0, channel_multiplier=0,
                      allow_small_or_imprecise_dtypes=True).then_inc(consts0, 1)
            pool.iota(jio[:, :], [[1, NR]], base=0, channel_multiplier=0,
                      allow_small_or_imprecise_dtypes=True).then_inc(consts0, 1)
            pool.wait_ge(consts0, 17)
            pool.memset(ones16[:, :], 1.0).then_inc(consts, 1)
            pool.dma_start(xs.rearrange("(j p) c -> p j c", p=T),
                           zeros[:, :].unsqueeze(1).to_broadcast([128, NR, 2 * C])).then_inc(xs_zeroed, 16)

            def softmax_shift(t):
                pool.wait_ge(s_max, t + 1)
                s = sc[:, t % 2, :].rearrange("p (h m) -> p h m", h=NH)
                pool.tensor_tensor(s, s, mx[:, t % 2, :].unsqueeze(2).to_broadcast([128, NH, L]),
                                   ALU.subtract).then_inc(s_sub, 1)

            def inverse_deviation(t, ln, eps, ready, shifted, done):
                r = rstd[:, ln, t % 2:t % 2 + 1]
                pool.wait_ge(ready, t + 1)
                pool.tensor_scalar(r, mv[:, ln, t % 2, 1:2], eps, None, ALU.add).then_inc(shifted, 1)
                pool.wait_ge(shifted, t + 1)
                pool.tensor_tensor(r, r, minus_half[:, :], ALU.pow).then_inc(done, 1)

            def rstd_1(t):
                if t >= 2:
                    pool.wait_ge(xn_ready, t - 1)
                inverse_deviation(t, 0, 1e-6, mv1, rstd1a, rstd1)

            def rstd_2(t):
                if t >= 2:
                    pool.wait_ge(xh_ready, t - 1)
                inverse_deviation(t, 1, 1e-5, mv2, rstd2a, rstd2)

            def expert_low(e):
                pool.wait_ge(w1_hi, e + 1)
                pool.tensor_tensor(w1s[:, e, 1, :, :], w1stage[:, :, :], w1s[:, e, 0, :, :], ALU.subtract
                                   ).then_inc(w1_lo, 1)
                pool.wait_ge(w2_hi, e + 1)
                pool.tensor_tensor(w2s[:, e, 1, :, :], w2stage[:, :, :], w2s[:, e, 0, :, :], ALU.subtract
                                   ).then_inc(w2_lo, 1)

            for step in range(STEPS):
                stages(step, ((softmax_shift, 3), (rstd_1, 0), (rstd_2, 7)))
                if 3 <= step < 3 + NE:
                    expert_low(step - 3)

        @block.scalar
        def _(act):
            for m in range(4):
                act.wait_ge(wt_mm, m + 1)
                src = (p_qk if m % 2 == 0 else p_v)[0:CH, 0:2 * C].rearrange("p (k o) -> p k o", k=2)
                dst = wT[:, 0, :, m * C:(m + 1) * C] if m < 3 else woT[0:CH, 0, :, :]
                act.activation(dst, src, ACT.Copy, scale=SA).then_inc(wt_hi, 1)
            def small_weights():
                act.wait_ge(small_loaded, 16 * 6)
                act.wait_ge(dve_consts, 2)
                act.activation(tab16[:, 0, :, :], tab[:, :, :], ACT.Copy).then_inc(small_hi, 1)
                act.activation(woT[CH:CH + 1, 0, 0, :], wob[CH:CH + 1, :], ACT.Copy, scale=SA).then_inc(small_hi, 1)
                act.activation(ws16[:, 0, :, :], wsr[:, :, :], ACT.Copy, scale=SF).then_inc(small_hi, 1)

            def keep_bias():
                act.wait_ge(bias_mm, 1)
                by_key = bias[:, :].rearrange("p (h m) -> p m h", h=NH)
                for half in range(2):
                    keys = slice(half * L // 2, (half + 1) * L // 2)
                    src = p_s[0:L, half * 512:half * 512 + NH * L // 2].rearrange("p (m h) -> p m h", h=NH)
                    for w in range(2):
                        act.activation(by_key[w * L:(w + 1) * L, keys, :], src, ACT.Copy).then_inc(bias_ready, 1)

            def keep_x(t):
                act.wait_ge(xT_mm, t + 1)
                act.activation(x2[:, t, :], p_x[:, 0:C], ACT.Copy).then_inc(x_kept, 1)

            def normed_hi(t):
                act.wait_ge(xnT_mm, t + 1)
                if t >= 2:
                    act.wait_ge(v_mm, t - 1)
                act.activation(xnT[:, t % 2, 0, :, :], p_n[0:CH, 0:2 * T].rearrange("p (k n) -> p k n", k=2),
                               ACT.Copy).then_inc(xnT_hi, 1)

            def qk_high(t):
                act.wait_ge(qk_mm, t + 1)
                if t >= 2:
                    act.wait_ge(s_mm, t - 1)
                    act.wait_ge(kbd_ready, t - 1)
                act.activation(qk[:, t % 2, 0, :], p_qk[:, :], ACT.Copy).then_inc(qk_hi, 1)

            def v_high(t):
                act.wait_ge(v_mm, t + 1)
                if t >= VB:
                    act.wait_ge(pv_mm, t - VB + 1)
                for w, h in WINDOW_HEADS:
                    act.activation(v2[h * L:(h + 1) * L, t % VB, 0, w, :, h, 0:HD], values(w, h), ACT.Copy
                                   ).then_inc(v_hi, 1)

            def exponentials(t):
                act.wait_ge(s_sub, t + 1)
                act.activation(sc[:, t % 2, :], sc[:, t % 2, :], ACT.Exp).then_inc(p_ready, 1)

            def weightsT_hi(t):
                if t >= 2:
                    act.wait_ge(pv_mm, t - 1)
                for h in range(2):
                    act.wait_ge(pT_mm[h], t + 1)
                    act.activation(pT[:, t % 2, 0, 3 * h:3 * h + 3, :],
                                   p_t[h][:, 0:3 * T].rearrange("p (n q) -> p n q", n=3),
                                   ACT.Copy).then_inc(pT_hi[h], 1)

            def attendedT_hi(t):
                act.wait_ge(oT_mm, t + 1)
                if t >= 2:
                    act.wait_ge(wo_mm, t - 1)
                act.activation(oT[0:CH, t % 2, 0, :, :], p_n[0:CH, 0:2 * T].rearrange("p (k n) -> p k n", k=2),
                               ACT.Copy).then_inc(oT_hi, 1)

            def xh_high(t):
                act.wait_ge(xh_ready, t + 1)
                act.activation(xhl[:, t, 0, :], xhf[:, t % 2, :], ACT.Copy).then_inc(xh_hi, 1)

            def keep_xhT(t):
                act.wait_ge(xhT_mm, t + 1)
                act.activation(xhT[0:CH, t, :, :, :],
                               p_n[0:CH, 0:2 * T].bitcast(F16).rearrange("p (a k n) -> p a k n", a=2, k=2),
                               ACT.Copy).then_inc(xhT_ready, 1)

            def expert_high(e):
                act.wait_ge(w1_loaded, 48 * (e + 1))
                if e >= 2:
                    act.wait_ge(bias_mm, 1)
                act.activation(w1stage[:, :, :], w1stage[:, :, :], ACT.Copy, scale=SF).then_inc(w1_scaled, 1)
                act.wait_ge(w2_loaded, 16 * (e + 1))
                if e >= NE - 2:
                    act.wait_ge(wt_mm, 4)
                act.activation(w2stage[:, :, :], w2stage[:, :, :], ACT.Copy, scale=SF).then_inc(w2_scaled, 1)
                act.wait_ge(w1_scaled, e + 1)
                act.activation(w1s[:, e, 0, :, :], w1stage[:, :, :], ACT.Copy).then_inc(w1_hi, 1)
                act.wait_ge(w2_scaled, e + 1)
                act.activation(w2s[:, e, 0, :, :], w2stage[:, :, :], ACT.Copy).then_inc(w2_hi, 1)

            for step in range(STEPS):
                if step == 3:
                    keep_bias()
                stages(step, ((qk_high, 2), (v_high, 2), (normed_hi, 1), (keep_x, 0), (keep_xhT, 9),
                              (xh_high, 8), (exponentials, 3), (attendedT_hi, 6), (weightsT_hi, 4)))
                if step == 1:
                    small_weights()
                if 3 <= step < 3 + NE:
                    expert_high(step - 3)
            act.wait_ge(ex_in, 1)
            act.activation(ex[:, :, :], ex[:, :, :], ACT.Exp).then_inc(ex_out, 1)

        @block.vector
        def _(dve):
            dve.memset(w1stage[CH:CH + 1, 1, :], 0.0).then_inc(dve_consts, 1)
            dve.memset(wsr[CH:CH + 1, 1, :], 0.0).then_inc(dve_consts, 1)
            dve.memset(v2[:, :, 0, :, :, :, :], 0.0).then_inc(dve_consts, 1)
            dve.memset(v2[:, :, 1, :, :, :, :], 0.0).then_inc(dve_consts, 1)
            dve.memset(oT[CH:CH + 1, :, 1, :, :], 0.0).then_inc(dve_consts, 1)
            dve.memset(oT[CH:CH + 1, :, 0, :, :], 1.0).then_inc(dve_consts, 1)
            dve.memset(xhT[CH:CH + 1, :, 1, :, :], 0.0).then_inc(dve_consts, 1)
            dve.memset(xhT[CH:CH + 1, :, 0, :, :], 1.0).then_inc(dve_consts, 1)
            dve.wait_ge(dve_consts, 4)
            for h in range(2):
                for w in range(2):
                    dve.memset(v2[64 * h:64 * h + 64, :, 0, w, :, h, HD], SA).then_inc(dve_consts, 1)
            for m in range(4):
                dve.wait_ge(wt_hi, m + 1)
                src = (p_qk if m % 2 == 0 else p_v)[0:CH, 0:2 * C].rearrange("p (k o) -> p k o", k=2)
                hi, lo = (wT[:, a, :, m * C:(m + 1) * C] if m < 3 else woT[0:CH, a, :, :] for a in range(2))
                dve.scalar_tensor_tensor(out=lo, in0=src, scalar=SA, in1=hi, op0=ALU.mult,
                                         op1=ALU.subtract).then_inc(wt_lo, 1)

            def small_weights():
                dve.wait_ge(small_hi, 3)
                dve.tensor_tensor(tab16[:, 1, :, :], tab[:, :, :], tab16[:, 0, :, :], ALU.subtract
                                  ).then_inc(small_lo, 1)
                for lo, src, hi, scale in (
                        (woT[CH:CH + 1, 1, 0, :], wob[CH:CH + 1, :], woT[CH:CH + 1, 0, 0, :], SA),
                        (ws16[:, 1, :, :], wsr[:, :, :], ws16[:, 0, :, :], SF)):
                    dve.scalar_tensor_tensor(out=lo, in0=src, scalar=scale, in1=hi, op0=ALU.mult,
                                             op1=ALU.subtract).then_inc(small_lo, 1)

            def one_hots():
                dve.wait_ge(idx_loaded, 16)
                dve.wait_ge(consts, 1)
                for k in range(3):
                    dve.tensor_scalar(hot[0:TH, k, :], idx[0:TH, :], rowid[:, k:k + 1], None, ALU.is_equal
                                      ).then_inc(hot_ready, 1)

            def normed(t):
                dve.wait_ge(rstd1, t + 1)
                if t >= 2:
                    dve.wait_ge(xnT_mm, t - 1)
                dve.tensor_scalar(xn[:, t % 2, :], x2[:, t, :], mv[:, 0, t % 2, 0:1], rstd[:, 0, t % 2:t % 2 + 1],
                                  ALU.subtract, ALU.mult).then_inc(xn_ready, 1)

            def statistics_1(t):
                dve.wait_ge(x_kept, t + 1)
                dve.bn_stats(stat[:, 0, t % 2, :], x2[:, t, :]).then_inc(stat1, 1)
                dve.wait_ge(stat1, t + 1)
                dve.bn_aggr(mv[:, 0, t % 2, :], stat[:, 0, t % 2, :]).then_inc(mv1, 1)

            def normed_lo(t):
                dve.wait_ge(xnT_hi, t + 1)
                if t >= 2:
                    dve.wait_ge(v_mm, t - 1)
                dve.tensor_tensor(xnT[:, t % 2, 1, :, :], p_n[0:CH, 0:2 * T].rearrange("p (k n) -> p k n", k=2),
                                  xnT[:, t % 2, 0, :, :], ALU.subtract).then_inc(xnT_lo, 1)

            def qk_low(t):
                dve.wait_ge(qk_hi, t + 1)
                if t >= 2:
                    dve.wait_ge(s_mm, t - 1)
                dve.tensor_tensor(qk[:, t % 2, 1, :], p_qk[:, :], qk[:, t % 2, 0, :], ALU.subtract
                                  ).then_inc(qk_lo, 1)

            def head_blocks(t):
                dve.wait_ge(qk_lo, t + 1)
                if t >= 2:
                    dve.wait_ge(s_mm, t - 1)
                for a in range(2):
                    for dst, rows, heads, chunk in ((ka, 128, HA, 1), (kc, RC, HC, 3)):
                        keys = qk[0:rows, t % 2, a, chunk * T:(chunk + 1) * T].rearrange("p (w m) -> p w m", w=2)
                        blk = dve.tensor_tensor(
                            dst[:, t % 2, a, :, :, :], keys.unsqueeze(2).to_broadcast([rows, 2, heads, L]),
                            mask[0:rows, 0:heads, :].unsqueeze(1).to_broadcast([rows, 2, heads, L]), ALU.mult)
                blk.then_inc(kbd_ready, 1)

            def v_low(t):
                dve.wait_ge(v_hi, 4 * t + 4)
                for w, h in WINDOW_HEADS:
                    hi, lo = (v2[h * L:(h + 1) * L, t % VB, a, w, :, h, 0:HD] for a in range(2))
                    dve.tensor_tensor(lo, values(w, h), hi, ALU.subtract).then_inc(v_lo, 1)

            def add_bias(t):
                dve.wait_ge(s_mm, t + 1)
                dve.wait_ge(bias_ready, 4)
                if t >= 2:
                    dve.wait_ge(pT_mm[1], t - 1)
                dve.scalar_tensor_tensor(out=sc[:, t % 2, :], in0=p_s[:, 0:NH * L], scalar=S_SCALE, in1=bias[:, :],
                                         op0=ALU.mult, op1=ALU.add).then_inc(s_biased, 1)

            def row_max(t):
                dve.wait_ge(s_biased, t + 1)
                if t >= 2:
                    dve.wait_ge(s_sub, t - 1)
                dve.tensor_reduce(mx[:, t % 2, :], sc[:, t % 2, :].rearrange("p (h m) -> p h m", h=NH), AX, ALU.max
                                  ).then_inc(s_max, 1)

            def weightsT_lo(t):
                if t >= 2:
                    dve.wait_ge(pv_mm, t - 1)
                for h in range(2):
                    dve.wait_ge(pT_hi[h], t + 1)
                    dve.tensor_tensor(pT[:, t % 2, 1, 3 * h:3 * h + 3, :],
                                      p_t[h][:, 0:3 * T].rearrange("p (n q) -> p n q", n=3),
                                      pT[:, t % 2, 0, 3 * h:3 * h + 3, :], ALU.subtract).then_inc(pT_lo[h], 1)

            def normalise(t):
                dve.wait_ge(pv_mm, t + 1)
                heads = p_v[:, 0:NH * VW].rearrange("p (h d) -> p h d", h=NH)
                if t >= 1:
                    dve.wait_ge(o_norm, t)
                dve.reciprocal(rden[:, :], heads[:, :, HD]).then_inc(rden_ready, 1)
                dve.wait_ge(rden_ready, t + 1)
                if t >= 2:
                    dve.wait_ge(oT_mm, t - 1)
                dve.tensor_tensor(on[:, t % 2, :].rearrange("p (h d) -> p h d", h=NH), heads[:, :, 0:HD],
                                  rden[:, :].unsqueeze(2).to_broadcast([128, NH, HD]), ALU.mult).then_inc(o_norm, 1)

            def attendedT_lo(t):
                dve.wait_ge(oT_hi, t + 1)
                if t >= 2:
                    dve.wait_ge(wo_mm, t - 1)
                dve.tensor_tensor(oT[0:CH, t % 2, 1, :, :], p_n[0:CH, 0:2 * T].rearrange("p (k n) -> p k n", k=2),
                                  oT[0:CH, t % 2, 0, :, :], ALU.subtract).then_inc(oT_lo, 1)

            def residual(t):
                dve.wait_ge(wo_mm, t + 1)
                dve.scalar_tensor_tensor(out=x2[:, t, :], in0=p_x[:, 0:C], scalar=1.0 / SA, in1=x2[:, t, :],
                                         op0=ALU.mult, op1=ALU.add).then_inc(x2_ready, 1)
                dve.wait_ge(x2_ready, t + 1)
                dve.bn_stats(stat[:, 1, t % 2, :], x2[:, t, :]).then_inc(stat2, 1)
                dve.wait_ge(stat2, t + 1)
                dve.bn_aggr(mv[:, 1, t % 2, :], stat[:, 1, t % 2, :]).then_inc(mv2, 1)

            def xh(t):
                dve.wait_ge(rstd2, t + 1)
                if t >= 2:
                    dve.wait_ge(xh_hi, t - 1)
                    dve.wait_ge(xh_lo, t - 1)
                dve.tensor_scalar(xhf[:, t % 2, :], x2[:, t, :], mv[:, 1, t % 2, 0:1], rstd[:, 1, t % 2:t % 2 + 1],
                                  ALU.subtract, ALU.mult).then_inc(xh_ready, 1)

            def xh_low(t):
                dve.wait_ge(xh_hi, t + 1)
                dve.tensor_tensor(xhl[:, t, 1, :], xhf[:, t % 2, :], xhl[:, t, 0, :], ALU.subtract
                                  ).then_inc(xh_lo, 1)

            def keep_logits(t):
                dve.wait_ge(lg_mm, t + 1)
                dve.tensor_scalar(lg[:, t, :], p_x[:, 0:NE], 1.0 / SF, None, ALU.mult).then_inc(lg_kept, 1)

            for step in range(STEPS):
                if step == 2:
                    small_weights()
                    one_hots()
                stages(step, ((normed, 1), (xh, 8), (add_bias, 3), (row_max, 3), (qk_low, 2), (head_blocks, 2),
                              (v_low, 2), (normed_lo, 1), (statistics_1, 0), (keep_logits, 10), (xh_low, 8),
                              (residual, 7), (attendedT_lo, 6), (normalise, 5), (weightsT_lo, 4)))

            links = [0]

            def link(ins):
                links[0] += 1
                ins.then_inc(chain, 1)
                dve.wait_ge(chain, links[0])

            def by_expert(column):
                return column.unsqueeze(2).to_broadcast([128, NT, NE])

            def over_tiles(row):
                return row.unsqueeze(1).to_broadcast([128, NT, NE])

            top, total, expert, slotf = (r16[:, i, :] for i in range(4))
            dve.wait_ge(lg_kept, NT)
            link(dve.tensor_reduce(top, lg[:, :, :], AX, ALU.max))
            link(dve.tensor_tensor(lg[:, :, :], lg[:, :, :], by_expert(top), ALU.subtract))
            dve.tensor_copy(ex[:, :, :], lg[:, :, :]).then_inc(ex_in, 1)
            link(dve.tensor_scalar(cand[:, :, :], lg[:, :, :], 0.0, float(NE), ALU.is_lt, ALU.mult))
            link(dve.tensor_tensor(cand[:, :, :], cand[:, :, :], over_tiles(eio[:, :]), ALU.add))
            link(dve.tensor_reduce(expert, cand[:, :, :], AX, ALU.min))
            dve.tensor_tensor(oh[:, :, :], over_tiles(eio[:, :]), by_expert(expert), ALU.is_equal
                              ).then_inc(oh_ready, 1)
            dve.wait_ge(ex_out, 1)
            link(dve.tensor_reduce(total, ex[:, :, :], AX, ALU.add))
            link(dve.reciprocal(pmax[:, :], total))
            link(dve.tensor_scalar(omp[:, :], pmax[:, :], -1.0, 1.0, ALU.mult, ALU.add))
            count, tiles, first, end = (cnt[:, i, :] for i in range(4))
            dve.wait_ge(rank_mm, 1)
            link(dve.tensor_copy(count, p_v[:, 0:NE]))
            above = big[:, 0:NE * NT].rearrange("p (e k) -> p e k", e=NE)
            link(dve.tensor_tensor(above, count.unsqueeze(2).to_broadcast([128, NE, NT]),
                                   kio[:, :].unsqueeze(1).to_broadcast([128, NE, NT]), ALU.is_gt))
            link(dve.tensor_reduce(tiles, above, AX, ALU.add))
            before = big[:, 0:NE * NE].rearrange("p (e k) -> p e k", e=NE)
            link(dve.tensor_tensor(before, tiles.unsqueeze(1).to_broadcast([128, NE, NE]), ltm[:, :, :], ALU.mult))
            link(dve.tensor_reduce(first, before, AX, ALU.add))
            link(dve.tensor_tensor(end, first, tiles, ALU.add))
            link(dve.tensor_scalar(first, first, float(T), None, ALU.mult))
            link(dve.tensor_tensor(cand[:, :, :], p_qk[:, 0:NT * NE].rearrange("p (t e) -> p t e", e=NE),
                                   over_tiles(first), ALU.add))
            link(dve.tensor_tensor(cand[:, :, :], cand[:, :, :], oh[:, :, :], ALU.mult))
            link(dve.tensor_reduce(slotf, cand[:, :, :], AX, ALU.add))
            link(dve.tensor_copy(slot[:, :], slotf))
            passed = big[0:1, 0:NR * NE].rearrange("p (j e) -> p j e", e=NE)
            link(dve.tensor_tensor(passed, end[0:1, :].unsqueeze(1).to_broadcast([1, NR, NE]),
                                   jio[:, :].unsqueeze(2).to_broadcast([1, NR, NE]), ALU.is_le))
            link(dve.tensor_reduce(ejf[:, 0, :], passed, AX, ALU.add))
            link(dve.tensor_scalar(ejf[:, 1, :], ejf[:, 0, :], float(NE - 1), None, ALU.min))
            link(dve.tensor_copy(etile[:, :], ejf[:, 1, :]))

        @block.tensor
        def _(pe):
            pe.wait_ge(consts, 1)
            pe.wait_ge(dve_consts, 12)
            for m in range(4):
                pe.wait_ge(watt_loaded, 16 * 4)
                if m >= 2:
                    pe.wait_ge(wt_lo, m - 1)
                bank = p_qk if m % 2 == 0 else p_v
                for k in range(2):
                    for r in range(2):
                        mm = pe.transpose(bank[0:CH, k * C + r * CH:k * C + (r + 1) * CH],
                                          watt[:, m, r, k * CH:(k + 1) * CH], ident[0:CH, 0:CH])
                mm.then_inc(wt_mm, 1)
            pe.wait_ge(wt_lo, 4)

            def position_bias():
                pe.wait_ge(hot_ready, 3)
                pe.wait_ge(small_lo, 3)
                for m in range(L):
                    col = (m // (L // 2)) * 512 + (m % (L // 2)) * NH
                    n = 0
                    for k in range(3):
                        w = hot[0:TH, k, :].rearrange("p (l m) -> p l m", m=L)[:, :, m]
                        for part in range(2):
                            mm = pe.matmul(p_s[0:L, col:col + NH], w, tab16[:, part, k, :], start=(n == 0), stop=(n == 5))
                            n += 1
                mm.then_inc(bias_mm, 1)

            def x_to_tokens(t):
                b = t // TPI
                pe.wait_ge(x_loaded[b % XI], 16 * (b // XI + 1))
                if t >= 1:
                    pe.wait_ge(x_kept, t)
                if t >= 8:
                    pe.wait_ge(x2_ready, t - 7)
                if t >= 11:
                    pe.wait_ge(lg_kept, t - 10)
                for k in range(2):
                    cols = xin[:, b % XI, k, (t % TPI) * T:(t % TPI + 1) * T]
                    mm = pe.transpose(p_x[:, k * CH:(k + 1) * CH], cols, ident[0:CH, 0:CH])
                mm.then_inc(xT_mm, 1)

            def normed_to_channels(t):
                pe.wait_ge(xn_ready, t + 1)
                if t >= 1:
                    pe.wait_ge(xnT_lo, t)
                if t >= 6:
                    pe.wait_ge(oT_lo, t - 5)
                if t >= 9:
                    pe.wait_ge(xhT_ready, t - 8)
                for k in range(2):
                    mm = pe.transpose(to_windows(p_n[0:CH, k * T:(k + 1) * T]), xn[:, t % 2, k * CH:(k + 1) * CH], ident[:, :])
                mm.then_inc(xnT_mm, 1)

            def project(t):
                pe.wait_ge(xnT_lo, t + 1)
                if t >= 1:
                    pe.wait_ge(qk_lo, t)
                for c, row in enumerate((0, C, 128, C + 128)):
                    n = 0
                    for k in range(2):
                        for a, b in PASSES:
                            mm = pe.matmul(p_qk[:, c * T:(c + 1) * T], wT[:, a, k, row:row + 128],
                                           xnT[:, t % 2, b, k, :], start=(n == 0), stop=(n == 5))
                            n += 1
                mm.then_inc(qk_mm, 1)
                if t >= 1:
                    pe.wait_ge(v_lo, 4 * t)
                if t >= 4:
                    pe.wait_ge(o_norm, t - 3)
                n = 0
                for k in range(2):
                    for a, b in PASSES:
                        mm = pe.matmul(p_v[:, 0:C], xnT[:, t % 2, a, k, :], wT[:, b, k, 2 * C:3 * C],
                                       start=(n == 0), stop=(n == 5))
                        n += 1
                mm.then_inc(v_mm, 1)

            def scores(t):
                pe.wait_ge(kbd_ready, t + 1)
                if t == 0:
                    pe.wait_ge(bias_ready, 4)
                else:
                    pe.wait_ge(s_biased, t)
                for w in range(2):
                    r = slice(w * L, (w + 1) * L)
                    for n, (a, b) in enumerate(PASSES):
                        pe.matmul(p_s[r, 0:HA * L], qk[:, t % 2, a, w * L:(w + 1) * L],
                                  ka[:, t % 2, b, w, :, :], start=(n == 0), stop=(n == 2))
                    for n, (a, b) in enumerate(PASSES):
                        mm = pe.matmul(p_s[r, HA * L:NH * L], qk[0:RC, t % 2, a, 2 * T + w * L:2 * T + (w + 1) * L],
                                       kc[:, t % 2, b, w, :, :], start=(n == 0), stop=(n == 2))
                mm.then_inc(s_mm, 1)

            def weights_to_keys(t):
                pe.wait_ge(p_ready, t + 1)
                for h in range(2):
                    if t >= 1:
                        pe.wait_ge(pT_lo[h], t)
                    for n in range(3):
                        pair = 3 * h + n
                        mm = pe.transpose(p_t[h][:, n * T:(n + 1) * T],
                                          sc[:, t % 2, pair * 2 * L:(pair + 1) * 2 * L], ident[:, :])
                    mm.then_inc(pT_mm[h], 1)

            def attend(t):
                pe.wait_ge(pT_lo[0], t + 1)
                pe.wait_ge(pT_lo[1], t + 1)
                pe.wait_ge(v_lo, 4 * min(t + 4, NT))
                if t >= 1:
                    pe.wait_ge(o_norm, t)
                for w in range(2):
                    for pair in range(NP):
                        for n, (a, b) in enumerate(PASSES):
                            mm = pe.matmul(p_v[w * L:(w + 1) * L, pair * 2 * VW:(pair + 1) * 2 * VW],
                                           pT[:, t % 2, a, pair, w * L:(w + 1) * L], v2[:, t % VB, b, w, pair, :, :],
                                           start=(n == 0), stop=(n == 2))
                mm.then_inc(pv_mm, 1)

            def attended_to_channels(t):
                pe.wait_ge(o_norm, t + 1)
                pe.wait_ge(xnT_lo, min(t + 6, NT))
                if t >= 1:
                    pe.wait_ge(oT_lo, t)
                if t >= 3:
                    pe.wait_ge(xhT_ready, t - 2)
                for k in range(2):
                    mm = pe.transpose(to_raster(p_n[0:CH, k * T:(k + 1) * T]), on[:, t % 2, k * CH:(k + 1) * CH], ident[:, :])
                mm.then_inc(oT_mm, 1)

            def output_projection(t):
                pe.wait_ge(oT_lo, t + 1)
                pe.wait_ge(x_kept, min(t + 8, NT))
                if t >= 1:
                    pe.wait_ge(x2_ready, t)
                if t >= 3:
                    pe.wait_ge(lg_kept, t - 2)
                n = 0
                for k in range(2):
                    for a, b in PASSES:
                        mm = pe.matmul(p_x[:, 0:C], oT[0:CH + 1 - k, t % 2, a, k, :], woT[0:CH + 1 - k, b, k, :],
                                       start=(n == 0), stop=(n == 5))
                        n += 1
                mm.then_inc(wo_mm, 1)

            def xh_to_channels(t):
                pe.wait_ge(xh_lo, t + 1)
                pe.wait_ge(xnT_lo, min(t + 9, NT))
                pe.wait_ge(oT_lo, min(t + 3, NT))
                if t >= 1:
                    pe.wait_ge(xhT_ready, t)
                bank = p_n[0:CH, 0:2 * T].bitcast(F16).rearrange("p (a k n) -> p a k n", a=2, k=2)
                for a in range(2):
                    for k in range(2):
                        mm = pe.transpose(bank[:, a, k, :], xhl[:, t, a, k * CH:(k + 1) * CH], ident16[:, :])
                mm.then_inc(xhT_mm, 1)

            def logits(t):
                pe.wait_ge(xhT_ready, t + 1)
                pe.wait_ge(x_kept, min(t + 11, NT))
                pe.wait_ge(x2_ready, min(t + 3, NT))
                if t >= 1:
                    pe.wait_ge(lg_kept, t)
                n = 0
                for k in range(2):
                    for a, b in PASSES:
                        mm = pe.matmul(p_x[:, 0:NE], xhT[0:CH + 1 - k, t, a, k, :], ws16[0:CH + 1 - k, b, k, :],
                                       start=(n == 0), stop=(n == 5))
                        n += 1
                mm.then_inc(lg_mm, 1)

            for step in range(STEPS):
                if step == 3:
                    position_bias()
                stages(step, ((scores, 3), (project, 2), (normed_to_channels, 1), (x_to_tokens, 0), (logits, 10),
                              (xh_to_channels, 9), (output_projection, 7), (attended_to_channels, 6),
                              (attend, 5), (weights_to_keys, 4)))
            pe.wait_ge(oh_ready, 1)
            flat = oh[:, :, :].rearrange("p t e -> p (t e)")
            pe.matmul(p_qk[:, 0:NT * NE], tri[:, :], flat, start=True, stop=False, skip_group_check=True)
            for d in range(1, NT):
                pe.matmul(p_qk[:, d * NE:NT * NE], ones16[:, :], flat[:, 0:(NT - d) * NE], start=False,
                          stop=(d == NT - 1), skip_group_check=True)
            for t in range(NT):
                mm = pe.matmul(p_v[:, 0:NE], ones16[:, :], oh[:, t, :], start=(t == 0), stop=(t == NT - 1))
            mm.then_inc(rank_mm, 1)



def experts(nc, g):
    (ident, ident16, ones16, w1s, w2s,  x2, xhl, xhT, pmax, omp, slot, etile, xs, ys, out) = (
        g[n] for n in ("ident", "ident16", "ones16", "w1s", "w2s", "x2", "xhl", "xhT",
                       "pmax", "omp", "slot", "etile", "xs", "ys", "out"))
    HF = NF // 2
    YB, GB = 4, 8
    FIRST = NT // 2
    TILES = ([("common", t) for t in range(FIRST)] + [("routed", j) for j in range(NR)]
             + [("common", t) for t in range(FIRST, NT)])
    N = len(TILES)
    MIX = FIRST + NR + 3

    def common_at(t):
        return t if t < FIRST else t + NR

    def routed_at(j):
        return FIRST + j

    def next_routed(n):
        return TILES[n + 1][1] if n + 1 < N and TILES[n + 1][0] == "routed" else None

    def mixes(step):
        last = 2 * (step - MIX) + 2
        if step == N:
            return range(max(0, last - 2), NT)
        return range(max(0, last - 2), max(0, min(last, NT)))

    with ExitStack() as ctx:
        def sb(name, shape, dt):
            return ctx.enter_context(nc.sbuf_tensor(name, shape, dt))

        def pb(name):
            return ctx.enter_context(nc.psum_tensor(name, [128, 512], F32))

        def sem(name):
            return ctx.enter_context(nc.semaphore(name))

        base = sb("base", [128, NT, C], F32)
        hf = sb("hf", [128, 2, 2, HF * T], F32)
        hp = sb("hp", [128, 2, 2, NF, T], F16)
        w1d = sb("w1d", [CH + 1, 2, 2, 2, FF], F16)
        w2d = sb("w2d", [128, 2, 2, NF, C], F16)
        b2d = sb("b2d", [CH + 1, 2, 2, C], F16)
        tok = sb("tok", [128, YB, 2 * C], F16)
        tokT = sb("tokT", [CH + 1, 2, 2, 2, T], F16)
        yo = sb("yo", [128, YB, C], F32)
        sel = sb("sel", [128, GB, C], F32)
        fin = sb("fin", [128, 2, C], F32)
        outc = sb("outc", [CH, 2, 2, IMG * IMG], F32)

        p_h = [[pb(f"p_h{i}{j}") for j in range(2)] for i in range(2)]
        p_y = [pb(f"p_y{i}") for i in range(2)]
        p_k = pb("p_k")
        p_f = [pb("p_f"), p_k]

        consts = sem("f_consts")
        scattered = sem("scattered")
        tok_loaded = [sem(f"tok_loaded{i}") for i in range(YB)]
        tokT_mm = sem("tokT_mm")
        tokT_ready = sem("tokT_ready")
        w1_copied = sem("w1_copied")
        w2_copied = sem("w2_copied")
        h_mm = [sem("h_mm0"), sem("h_mm1")]
        h_act = [sem("h_act0"), sem("h_act1")]
        h_hi = [sem("h_hi0"), sem("h_hi1")]
        h_lo = [sem("h_lo0"), sem("h_lo1")]
        y_mm = sem("y_mm")
        y_kept = sem("y_kept")
        base_ready = sem("base_ready")
        y_stored = [sem(f"y_stored{i}") for i in range(YB)]
        gathered = [sem(f"gathered{i}") for i in range(GB)]
        mixed = sem("mixed")
        fin_mm = sem("fin_mm")
        fin_kept = sem("fin_kept")
        out_stored = [sem("out_stored0"), sem("out_stored1")]

        block = ctx.enter_context(nc.Block())

        @block.gpsimd
        def _(pool):
            for t in range(NT):
                pool.indirect_dma_start(out=xs, out_offset=bass.IndirectOffsetOnAxis(ap=slot[:, t:t + 1], axis=0),
                                        in_=xhl[:, t, :, :].rearrange("p a c -> p (a c)"), in_offset=None
                                        ).then_inc(scattered, 16)
            for i in range(YB):
                pool.wait_ge(y_stored[i], 16 * len(range(i, NR, YB)))
            for t in range(NT):
                if t >= GB:
                    pool.wait_ge(mixed, t - GB + 1)
                pool.indirect_dma_start(out=sel[:, t % GB, :], out_offset=None, in_=ys,
                                        in_offset=bass.IndirectOffsetOnAxis(ap=slot[:, t:t + 1], axis=0)
                                        ).then_inc(gathered[t % GB], 16)

        @block.sync
        def _(sp):
            def load(j):
                if j >= YB:
                    sp.wait_ge(tokT_mm, j - YB + 1)
                sp.dma_start(tok[:, j % YB, :], xs[j * T:(j + 1) * T, :]).then_inc(tok_loaded[j % YB], 16)

            sp.wait_ge(scattered, 16 * NT)
            for j in range(YB):
                load(j)
            for j in range(NR):
                if j + YB < NR:
                    load(j + YB)
                sp.wait_ge(y_kept, routed_at(j) + 1)
                sp.dma_start(ys[j * T:(j + 1) * T, :], yo[:, j % YB, :]).then_inc(y_stored[j % YB], 16)
            for b in range(B):
                sp.wait_ge(fin_kept, TPI * (b + 1))
                sp.dma_start(out[b].rearrange("(k c) i j -> c k (i j)", k=2), outc[:, b % 2, :, :]
                             ).then_inc(out_stored[b % 2], 16)
            for i in range(2):
                sp.wait_ge(out_stored[i], 16 * B // 2)

        @block.scalar
        def _(act):
            def hidden(n):
                for h in range(2):
                    act.wait_ge(h_mm[h], n + 1)
                    if n >= 2:
                        act.wait_ge(h_lo[h], n - 1)
                        act.wait_ge(y_mm, n - 1)
                    act.activation(hp[:, n % 2, 0, HF * h:HF * h + HF, :],
                                   p_h[n % 2][h][:, 0:HF * T].rearrange("p (f t) -> p f t", f=HF), ACT.Gelu,
                                   scale=1.0 / SF).then_inc(h_hi[h], 1)
                    act.activation(hf[:, n % 2, h, :], p_h[n % 2][h][:, 0:HF * T], ACT.Gelu, scale=1.0 / SF
                                   ).then_inc(h_act[h], 1)

            def tokens(j):
                act.wait_ge(tokT_mm, j + 1)
                if j >= 2:
                    act.wait_ge(h_mm[1], routed_at(j - 2) + 1)
                act.activation(tokT[0:CH, j % 2, :, :, :],
                               p_k[0:CH, 0:2 * T].bitcast(F16).rearrange("p (a k n) -> p a k n", a=2, k=2),
                               ACT.Copy).then_inc(tokT_ready, 1)

            def keep_result(t):
                b = t // TPI
                act.wait_ge(fin_mm, t + 1)
                if b >= 2 and t % TPI == 0:
                    act.wait_ge(out_stored[b % 2], 16 * (b // 2))
                act.activation(outc[:, b % 2, :, (t % TPI) * T:(t % TPI + 1) * T],
                               p_f[t % 2][0:CH, 0:2 * T].rearrange("p (k n) -> p k n", k=2), ACT.Copy
                               ).then_inc(fin_kept, 1)

            act.wait_ge(consts, 1)
            for n in range(N + 1):
                j = next_routed(n)
                if j is not None:
                    tokens(j)
                if n < N:
                    hidden(n)
                for t in mixes(n):
                    keep_result(t)

        @block.vector
        def _(dve):
            dve.memset(tokT[CH:CH + 1, :, 1, :, :], 0.0)
            dve.memset(tokT[CH:CH + 1, :, 0, :, :], 1.0).then_inc(consts, 1)

            def weights_1(j):
                e = dve.value_load(etile[0:1, j:j + 1], min_val=0, max_val=NE - 1)
                if j >= 2:
                    dve.wait_ge(h_mm[1], routed_at(j - 2) + 1)
                dve.tensor_copy(w1d[:, j % 2, :, :, :], w1s[:, e, :, :, :]).then_inc(w1_copied, 1)
                return e

            def weights_2(j, e):
                if j >= 2:
                    dve.wait_ge(y_mm, routed_at(j - 2) + 1)
                dve.tensor_copy(b2d[CH:CH + 1, j % 2, :, :], w1s[CH:CH + 1, e, :, 1, 0:C])
                dve.tensor_copy(w2d[:, j % 2, :, :, :], w2s[:, e, :, :, :]).then_inc(w2_copied, 1)

            def hidden_lo(n):
                for h in range(2):
                    dve.wait_ge(h_act[h], n + 1)
                    if n >= 2:
                        dve.wait_ge(y_mm, n - 1)
                    dve.tensor_tensor(hp[:, n % 2, 1, HF * h:HF * h + HF, :],
                                      hf[:, n % 2, h, :].rearrange("p (f t) -> p f t", f=HF),
                                      hp[:, n % 2, 0, HF * h:HF * h + HF, :], ALU.subtract).then_inc(h_lo[h], 1)

            def keep_y(n):
                kind, i = TILES[n]
                dve.wait_ge(y_mm, n + 1)
                if kind == "common":
                    dve.tensor_scalar(base[:, i, :], p_y[n % 2][:, 0:C], omp[:, i:i + 1], 1.0 / SF,
                                      ALU.mult, ALU.mult).then_inc(y_kept, 1)
                    dve.wait_ge(y_kept, n + 1)
                    dve.tensor_tensor(base[:, i, :], base[:, i, :], x2[:, i, :], ALU.add).then_inc(base_ready, 1)
                else:
                    if i >= YB:
                        dve.wait_ge(y_stored[i % YB], 16 * (i // YB))
                    dve.tensor_scalar(yo[:, i % YB, :], p_y[n % 2][:, 0:C], 1.0 / SF, None, ALU.mult
                                      ).then_inc(y_kept, 1)

            def mix(t):
                dve.wait_ge(gathered[t % GB], 16 * (t // GB + 1))
                dve.wait_ge(base_ready, t + 1)
                if t >= 2:
                    dve.wait_ge(fin_mm, t - 1)
                dve.scalar_tensor_tensor(out=fin[:, t % 2, :], in0=sel[:, t % GB, :], scalar=pmax[:, t:t + 1],
                                         in1=base[:, t, :], op0=ALU.mult, op1=ALU.add).then_inc(mixed, 1)

            for n in range(N + 1):
                j = next_routed(n)
                if j is not None:
                    e = weights_1(j)
                if n < N:
                    hidden_lo(n)
                if n >= 1:
                    keep_y(n - 1)
                if j is not None:
                    weights_2(j, e)
                for t in mixes(n):
                    mix(t)

        @block.tensor
        def _(pe):
            pe.wait_ge(consts, 1)

            def tokens(j):
                pe.wait_ge(tok_loaded[j % YB], 16 * (j // YB + 1))
                if j >= 1:
                    pe.wait_ge(tokT_ready, j)
                bank = p_k[0:CH, 0:2 * T].bitcast(F16).rearrange("p (a k n) -> p a k n", a=2, k=2)
                for a in range(2):
                    for k in range(2):
                        col = a * C + k * CH
                        mm = pe.transpose(bank[:, a, k, :], tok[:, j % YB, col:col + CH], ident16[:, :])
                mm.then_inc(tokT_mm, 1)

            def hidden(n):
                kind, i = TILES[n]
                if n >= 2:
                    for h in range(2):
                        pe.wait_ge(h_act[h], n - 1)
                if kind == "common":
                    w, xT = w1s[:, 0, :, :, :], xhT[:, i, :, :, :]
                else:
                    pe.wait_ge(w1_copied, i + 1)
                    pe.wait_ge(tokT_ready, i + 1)
                    w, xT = w1d[:, i % 2, :, :, :], tokT[:, i % 2, :, :, :]
                for f in range(NF):
                    m = 0
                    for k in range(2):
                        for a, b in PASSES:
                            mm = pe.matmul(p_h[n % 2][f // HF][:, (f % HF) * T:(f % HF + 1) * T],
                                           w[0:CH + 1 - k, a, k, f * 128:(f + 1) * 128], xT[0:CH + 1 - k, b, k, :],
                                           start=(m == 0), stop=(m == 5))
                            m += 1
                    if f % HF == HF - 1:
                        mm.then_inc(h_mm[f // HF], 1)

            def outputs(n):
                kind, i = TILES[n]
                if n >= 2:
                    pe.wait_ge(y_kept, n - 1)
                if kind == "common":
                    w, b2 = w2s[:, 0, :, :, :], w1s[CH:CH + 1, 0, :, 1, 0:C]
                else:
                    pe.wait_ge(w2_copied, i + 1)
                    w, b2 = w2d[:, i % 2, :, :, :], b2d[CH:CH + 1, i % 2, :, :]
                y = p_y[n % 2][:, 0:C]
                for a in range(2):
                    pe.matmul(y, ones16[CH:CH + 1, :], b2[:, a, :], start=(a == 0), stop=False)
                for f in range(NF):
                    if f % HF == 0:
                        pe.wait_ge(h_lo[f // HF], n + 1)
                    for m, (a, b) in enumerate(PASSES):
                        mm = pe.matmul(y, hp[:, n % 2, a, f, :], w[:, b, f, :], start=False,
                                       stop=(f == NF - 1 and m == 2))
                mm.then_inc(y_mm, 1)

            def result_to_channels(t):
                pe.wait_ge(mixed, t + 1)
                if t >= 2:
                    pe.wait_ge(fin_kept, t - 1)
                elif t == 1:
                    pe.wait_ge(tokT_ready, NR)
                for k in range(2):
                    mm = pe.transpose(p_f[t % 2][0:CH, k * T:(k + 1) * T], fin[:, t % 2, k * CH:(k + 1) * CH],
                                      ident[:, :])
                mm.then_inc(fin_mm, 1)

            for n in range(N + 1):
                j = next_routed(n)
                if j is not None:
                    tokens(j)
                if n < N:
                    hidden(n)
                if n >= 1:
                    outputs(n - 1)
                for t in mixes(n):
                    result_to_channels(t)


_INS = ['x', 'L0_conv_Wq', 'L0_conv_Wk', 'L0_conv_Wv', 'L0_conv_Wo_w', 'L0_conv_Wo_b', 'L0_conv_rel_pos_bias',
        'L0_conv_rel_coords', 'L0_ffn_Ws', 'L0_ffn_bs', 'L0_ffn_W1', 'L0_ffn_b1', 'L0_ffn_W2', 'L0_ffn_b2']
_OUTS = [((B, C, IMG, IMG), 'float32')]


def kernel(**inputs):
    import numpy as _np
    import concourse.bacc as _bacc
    from concourse import mybir as _mybir
    from concourse.bass_utils import run_bass_kernel_spmd as _run

    nc = _bacc.Bacc("TRN2", target_bir_lowering=False, num_devices=1)
    arrays, args = {}, []
    for name in _INS:
        a = _np.ascontiguousarray(inputs[name])
        arrays[f"in_{name}_dram"] = a
        args.append(nc.dram_tensor(f"in_{name}_dram", a.shape, _mybir.dt.from_np(a.dtype), kind="ExternalInput").ap())
    for i, (shape, dtype) in enumerate(_OUTS):
        dt = _mybir.dt.from_np(_np.dtype(dtype))
        args.append(nc.dram_tensor(f"out_{i}_dram", shape, dt, kind="ExternalOutput").ap())
    build(nc, *args)
    r = _run(nc, [arrays], core_ids=[0])
    got = tuple(r.results[0][f"out_{i}_dram"] for i in range(len(_OUTS)))
    return got[0]
```

```python
from contextlib import ExitStack

import concourse.bass as bass
from concourse import mybir

F32 = mybir.dt.float32
F16 = mybir.dt.float16
I32 = mybir.dt.int32
U32 = mybir.dt.uint32
ALU = mybir.AluOpType
ACT = mybir.ActivationFunctionType
AX = mybir.AxisListType.X

B, C, IMG = 8, 192, 16
WS, NH = 8, 12
HD = C // NH
L = WS * WS
T = 128
NT = B * IMG * IMG // T
TPI = IMG * IMG // T
CH = 96
NE, FF = 9, 768
NF = FF // 128
NR = (NT * T + NE * (T - 1)) // T
TBL = (2 * WS - 1) ** 2
TH = TBL // 3
HA = 128 // HD
HC = NH - HA
RC = HC * HD
NP = NH // 2
VW = HD + 1

PASSES = ((0, 0), (0, 1), (1, 0))
SV = 16.0
SF = 64.0
S_SCALE = 1.0 / float(HD) ** 0.5


def to_windows(ap):
    return ap.rearrange("p (w i j) -> p i w j", w=2, j=WS)


def to_raster(ap):
    return ap.rearrange("p (i w j) -> p w i j", w=2, j=WS)


def build(nc, x, Wq, Wk, Wv, Wo_w, Wo_b, rpb, rel, Ws, bs, W1, b1, W2, b2, out):
    xs = nc.dram_tensor("sorted_tokens", (NR * T, 2 * C), F16, kind="Internal").ap()
    ys = nc.dram_tensor("sorted_outputs", (NR * T, C), F32, kind="Internal").ap()
    with ExitStack() as whole:
        def sbw(name, shape, dt):
            return whole.enter_context(nc.sbuf_tensor(name, shape, dt))

        def sem(name):
            return whole.enter_context(nc.semaphore(name))

        ident = sbw("ident", [128, 128], F32)
        ident16 = sbw("ident16", [128, 128], F16)
        ones16 = sbw("ones16", [128, 128], F16)
        w1s = sbw("w1s", [CH + 1, NE, 2, 2, FF], F16)
        w2s = sbw("w2s", [128, NE, 2, NF, C], F16)
        x2 = sbw("x2", [128, NT, C], F32)
        xhl = sbw("xhl", [128, NT, 2, C], F16)
        xhT = sbw("xhT", [CH + 1, NT, 2, 2, T], F16)
        pmax = sbw("pmax", [128, NT], F32)
        omp = sbw("omp", [128, NT], F32)
        slot = sbw("slot", [128, NT], U32)
        etile = sbw("etile", [1, NR], I32)

        attention(nc, locals())
        experts(nc, locals())


def attention(nc, g):
    (ident, ident16, ones16, w1s, w2s,  x2, xhl, xhT, pmax, omp, slot, etile, xs) = (
        g[n] for n in ("ident", "ident16", "ones16", "w1s", "w2s", "x2", "xhl", "xhT",
                       "pmax", "omp", "slot", "etile", "xs"))
    x, Wo_b, rpb, rel, Ws, bs, W1, b1, W2, b2 = (
        g[n] for n in ("x", "Wo_b", "rpb", "rel", "Ws", "bs", "W1", "b1", "W2", "b2"))
    mats = [g["Wq"], g["Wk"], g["Wv"], g["Wo_w"]]
    VB = 4
    XI = 2
    SB = 3
    with ExitStack() as ctx:
        def sb(name, shape, dt):
            return ctx.enter_context(nc.sbuf_tensor(name, shape, dt))

        def pb(name, cols, dt=F32):
            return ctx.enter_context(nc.psum_tensor(name, [128, cols], dt))

        def sem(name):
            return ctx.enter_context(nc.semaphore(name))

        xin = sb("xin", [CH, XI, 2, IMG * IMG], F32)
        w1stage = sb("w1stage", [CH + 1, 2, FF], F32)
        w2stage = sb("w2stage", [128, NF, C], F32)
        xn = sb("xn", [128, 2, C], F32)
        xnT = sb("xnT", [CH, 2, 2, T], F32)
        q = sb("q", [128, 2, 2, T], F32)
        ka = sb("ka", [128, 2, 2, HA, L], F32)
        kc = sb("kc", [RC, 2, 2, HC, L], F32)
        v2 = sb("v2", [128, VB, 2, 2, NP, 2, VW], F16)
        sc = sb("sc", [128, SB, NH * L], F32)
        pT = sb("pT", [128, 2, 2, NP, T], F16)
        on = sb("on", [128, 2, C], F32)
        oT = sb("oT", [CH + 1, 2, 2, T], F32)
        xhf = sb("xhf", [128, 2, C], F32)
        bias = sb("bias", [128, NH * L], F32)
        wT = sb("wT", [CH, 2, 3 * C], F32)
        woT = sb("woT", [CH + 1, 2, C], F32)
        wsr = sb("wsr", [CH + 1, 2, NE], F32)
        ws16 = sb("ws16", [CH + 1, 2, 2, NE], F16)
        mask = sb("mask", [128, HA], F32)
        tab = sb("tab", [TH, 3, NH], F32)
        tab16 = sb("tab16", [TH, 2, 3, NH], F16)
        rowid = sb("rowid", [TH, 3], F32)
        stat = sb("stat", [128, 2, 2, 6], F32)
        mv = sb("mv", [128, 2, 2, 2], F32)
        rstd = sb("rstd", [128, 2, 2], F32)
        minus_half = sb("minus_half", [128, 1], F32)
        mx = sb("mx", [128, 2, NH], F32)
        rden = sb("rden", [128, NH], F32)
        lg = sb("lg", [128, NT, NE], F32)
        ex, cand = (b[:, :, :].rearrange("p a c -> p (a c)")[:, 0:NT * NE].rearrange(
            "p (t e) -> p t e", e=NE) for b in (xn, on))
        big = sc[:, 0, :]
        oh = sb("oh", [128, NT, NE], F16)
        r16 = sb("r16", [128, 4, NT], F32)
        tri = sb("tri", [128, 128], F16)
        eio = sb("eio", [128, NE], F32)
        kio = sb("kio", [128, NT], F32)
        jio = sb("jio", [1, NR], F32)
        ltm = sb("ltm", [128, NE, NE], F32)
        cnt = sb("cnt", [128, 4, NE], F32)
        ejf = sb("ejf", [1, 2, NR], F32)
        zeros = sb("zeros", [128, 2 * C], F16)
        late = w1s[:, :, :, :, :].rearrange("p e a k f -> p (e a k f)")
        per_e = 2 * 2 * FF
        idx = late[:, 2 * per_e:2 * per_e + 2 * L * L].bitcast(I32)
        hot = late[:, 2 * per_e + 2 * L * L:2 * per_e + 5 * L * L].rearrange("p (k n) -> p k n", k=3)
        watt = w2s[:, NE - 2:NE, :, :, :].rearrange("p e a f c -> p (e a f c)")[
            0:CH, 0:4 * 2 * C * 2].bitcast(F32).rearrange("p (m r c) -> p m r c", m=4, r=2)

        p_x = pb("p_x", 512)
        p_n = pb("p_n", 512)
        p_qk = pb("p_qk", 512)
        p_v = pb("p_v", 512)
        p_s = pb("p_s", 1024)
        p_t = [pb("p_t0", 512), pb("p_t1", 512)]

        x_loaded = [sem(f"x_loaded{i}") for i in range(XI)]
        watt_loaded = sem("watt_loaded")
        idx_loaded = sem("idx_loaded")
        small_loaded = sem("small_loaded")
        w1_loaded = sem("w1_loaded")
        w2_loaded = sem("w2_loaded")
        xs_zeroed = sem("xs_zeroed")
        consts0 = sem("consts0")
        consts = sem("consts")
        dve_consts = sem("dve_consts")
        wt_mm = sem("wt_mm")
        wt_kept = sem("wt_kept")
        small_hi = sem("small_hi")
        small_lo = sem("small_lo")
        hot_ready = sem("hot_ready")
        bias_mm = sem("bias_mm")
        bias_ready = sem("bias_ready")
        w1_scaled = sem("w1_scaled")
        w2_scaled = sem("w2_scaled")
        w1_hi = sem("w1_hi")
        w1_lo = sem("w1_lo")
        w2_hi = sem("w2_hi")
        w2_lo = sem("w2_lo")
        xT_mm = sem("xT_mm")
        x_kept = sem("x_kept")
        stat1 = sem("stat1")
        mv1 = sem("mv1")
        rstd1a = sem("rstd1a")
        rstd1 = sem("rstd1")
        xn_ready = sem("xn_ready")
        xnT_mm = sem("xnT_mm")
        xnT_ready = sem("xnT_ready")
        qk_mm = sem("qk_mm")
        v_mm = sem("v_mm")
        q_kept = sem("q_kept")
        kbd_ready = sem("kbd_ready")
        v_hi = sem("v_hi")
        v_lo = sem("v_lo")
        s_mm = [sem("s_mm0"), sem("s_mm1")]
        s_biased = [sem("s_biased0"), sem("s_biased1")]
        s_max = sem("s_max")
        s_sub = sem("s_sub")
        p_ready = sem("p_ready")
        pT_mm = [sem("pT_mm0"), sem("pT_mm1")]
        pT_hi = [sem("pT_hi0"), sem("pT_hi1")]
        pT_lo = [sem("pT_lo0"), sem("pT_lo1")]
        pv_mm = sem("pv_mm")
        rden_ready = sem("rden_ready")
        o_norm = sem("o_norm")
        oT_mm = sem("oT_mm")
        oT_ready = sem("oT_ready")
        wo_mm = sem("wo_mm")
        x2_ready = sem("x2_ready")
        stat2 = sem("stat2")
        mv2 = sem("mv2")
        rstd2a = sem("rstd2a")
        rstd2 = sem("rstd2")
        xh_ready = sem("xh_ready")
        xh_hi = sem("xh_hi")
        xh_lo = sem("xh_lo")
        xhT_mm = sem("xhT_mm")
        xhT_ready = sem("xhT_ready")
        lg_mm = sem("lg_mm")
        lg_kept = sem("lg_kept")
        chain = sem("chain")
        ex_in = sem("ex_in")
        ex_out = sem("ex_out")
        oh_ready = sem("oh_ready")
        rank_mm = sem("rank_mm")

        PE_PROGRAM = (("x_to_tokens", 0), ("attend", 5), ("logits", 7), ("project", 1),
                      ("attended_to_channels", 5), ("project_values", 1), ("output_projection", 5),
                      ("normed_to_channels", 0), ("scores_0", 2), ("scores_1", 1), ("xh_to_channels", 6),
                      ("weights_to_keys_0", 3), ("weights_to_keys_1", 3))
        ACT_PROGRAM = (("keep_x", 0), ("weightsT_hi_1", 4), ("split", 0), ("keep_queries", 1),
                       ("keep_attendedT", 5), ("xh_high", 6), ("v_high", 1), ("split", 0), ("keep_normedT", 0),
                       ("exponentials", 3), ("keep_xhT", 6), ("weightsT_hi_0", 3))
        DVE_PROGRAM = (("statistics_1", 0), ("weightsT_lo_0", 4), ("weightsT_lo_1", 4), ("normed", 0),
                       ("normalise", 5), ("keep_logits", 7), ("xh", 6), ("head_blocks", 1), ("v_low", 1),
                       ("residual", 5), ("add_bias_0", 2), ("add_bias_1", 1), ("row_max", 2))
        POOL_PROGRAM = (("rstd_1", 0), ("split", 0), ("softmax_shift", 3), ("xh_low", 6), ("split", 0),
                        ("rstd_2", 5))
        STEPS = NT + 1 + max(lag for program in (PE_PROGRAM, ACT_PROGRAM, DVE_PROGRAM, POOL_PROGRAM)
                             for _, lag in program)
        BIAS_STEP = 1
        FIRST_SCORES = 1
        QUARTERS = 4 * NE
        FIRST_SPLIT = 2
        STEPS = max(STEPS, FIRST_SPLIT + QUARTERS // 2)
        SCORE_COLS = (slice(0, HA * L), slice(HA * L, NH * L))
        WINDOW_HEADS = [(w, h) for w in range(2) for h in range(2)]

        def values(w, h):
            return p_v[w * L:(w + 1) * L, 0:C].rearrange("p (n h d) -> p n h d", n=NP, h=2)[:, :, h, :]

        def stages(step, program, functions, split):
            by_name = {f.__name__: f for f in functions}
            quarter = 2 * (step - FIRST_SPLIT)
            for name, lag in program:
                if name == "split":
                    if 0 <= quarter < QUARTERS:
                        split(quarter // 4, quarter % 4)
                        quarter += 1
                elif 0 <= step - lag < NT:
                    by_name[name](step - lag)

        def ahead(stage, t, other):
            names = [name for name, _ in PE_PROGRAM]
            lags = dict(PE_PROGRAM)
            n = t + lags[stage] - lags[other] + (names.index(other) < names.index(stage))
            return max(0, min(n, NT))

        block = ctx.enter_context(nc.Block())

        @block.sync
        def _(sp):
            def image(b):
                if b >= XI:
                    sp.wait_ge(xT_mm, TPI * (b - XI + 1))
                sp.dma_start(xin[:, b % XI, :, :],
                             x[b].rearrange("(k c) i j -> c k (i j)", k=2)).then_inc(x_loaded[b % XI], 16)

            image(0)
            for m in range(4):
                sp.dma_start(watt[:, m, :, :],
                             mats[m].rearrange("(r o) c -> o r c", r=2)).then_inc(watt_loaded, 16)
            image(1)
            sp.dma_start(idx[0:TH, :], rel.rearrange("l m -> (l m)").unsqueeze(0).to_broadcast([TH, L * L])
                         ).then_inc(idx_loaded, 16)
            sp.dma_start(woT[CH:CH + 1, 0, :], Wo_b.unsqueeze(0)).then_inc(small_loaded, 16)
            sp.dma_start(wsr[0:CH, :, :], Ws.rearrange("(k c) e -> c k e", k=2)).then_inc(small_loaded, 16)
            sp.dma_start(wsr[CH:CH + 1, 0, :], bs.unsqueeze(0)).then_inc(small_loaded, 16)
            with nc.allow_non_contiguous_dma(reason="small table, transposed once"):
                for k in range(3):
                    sp.dma_start(tab[:, k, :], rpb[:, k * TH:(k + 1) * TH].rearrange("h r -> r h")
                                 ).then_inc(small_loaded, 16)
            sp.wait_ge(dve_consts, 1)
            for e in range(NE):
                if e >= 1:
                    sp.wait_ge(w1_hi, 2 * e)
                    sp.wait_ge(w1_lo, 2 * e)
                sp.dma_start(w1stage[0:CH, :, :], W1[e].rearrange("(k c) f -> c k f", k=2)).then_inc(w1_loaded, 16)
                sp.dma_start(w1stage[CH:CH + 1, 0, :], b1[e].unsqueeze(0)).then_inc(w1_loaded, 16)
                sp.dma_start(w1stage[CH:CH + 1, 1, 0:C], b2[e].unsqueeze(0)).then_inc(w1_loaded, 16)
                if e >= 1:
                    sp.wait_ge(w2_hi, 2 * e)
                    sp.wait_ge(w2_lo, 2 * e)
                sp.dma_start(w2stage[:, :, :], W2[e].rearrange("(f p) c -> p f c", p=128)).then_inc(w2_loaded, 16)
                if e + 2 < B:
                    image(e + 2)
            sp.wait_ge(xs_zeroed, 16)

        @block.gpsimd
        def _(pool):
            pool.memset(ident[:, :], 0.0).then_inc(consts0, 1)
            pool.memset(ident16[:, :], 0.0).then_inc(consts0, 1)
            pool.memset(tri[:, :], 1.0).then_inc(consts0, 1)
            pool.memset(mask[:, :], 1.0).then_inc(consts0, 1)
            pool.memset(ltm[:, :, :], 1.0).then_inc(consts0, 1)
            pool.memset(zeros[:, :], 0.0).then_inc(consts0, 1)
            pool.memset(minus_half[:, :], -0.5).then_inc(consts0, 1)
            pool.wait_ge(consts0, 7)
            for m in (ident, ident16):
                pool.affine_select(out=m[:, :], in_=m[:, :], compare_op=ALU.not_equal, fill=1.0, base=0,
                                   pattern=[[-1, 128]], channel_multiplier=1).then_inc(consts0, 1)
            pool.affine_select(out=tri[:, :], in_=tri[:, :], compare_op=ALU.is_gt, fill=0.0, base=0,
                               pattern=[[1, 128]], channel_multiplier=-1).then_inc(consts0, 1)
            pool.affine_select(out=ltm[:, :, :], in_=ltm[:, :, :], compare_op=ALU.is_gt, fill=0.0, base=0,
                               pattern=[[1, NE], [-1, NE]], channel_multiplier=0).then_inc(consts0, 1)
            pool.affine_select(out=mask[:, :], in_=mask[:, :], compare_op=ALU.is_ge, fill=0.0, base=0,
                               pattern=[[-HD, HA]], channel_multiplier=1).then_inc(consts0, 1)
            pool.wait_ge(consts0, 12)
            pool.affine_select(out=mask[:, :], in_=mask[:, :], compare_op=ALU.is_ge, fill=0.0, base=HD - 1,
                               pattern=[[HD, HA]], channel_multiplier=-1).then_inc(consts0, 1)
            pool.iota(rowid[:, :], [[TH, 3]], base=0, channel_multiplier=1,
                      allow_small_or_imprecise_dtypes=True).then_inc(consts0, 1)
            pool.iota(eio[:, :], [[1, NE]], base=0, channel_multiplier=0,
                      allow_small_or_imprecise_dtypes=True).then_inc(consts0, 1)
            pool.iota(kio[:, :], [[T, NT]], base=0, channel_multiplier=0,
                      allow_small_or_imprecise_dtypes=True).then_inc(consts0, 1)
            pool.iota(jio[:, :], [[1, NR]], base=0, channel_multiplier=0,
                      allow_small_or_imprecise_dtypes=True).then_inc(consts0, 1)
            pool.wait_ge(consts0, 17)
            pool.memset(ones16[:, :], 1.0).then_inc(consts, 1)
            pool.dma_start(xs.rearrange("(j p) c -> p j c", p=T),
                           zeros[:, :].unsqueeze(1).to_broadcast([128, NR, 2 * C])).then_inc(xs_zeroed, 16)

            def softmax_shift(t):
                pool.wait_ge(s_max, t + 1)
                s = sc[:, t % SB, :].rearrange("p (h m) -> p h m", h=NH)
                pool.tensor_tensor(s, s, mx[:, t % 2, :].unsqueeze(2).to_broadcast([128, NH, L]),
                                   ALU.subtract).then_inc(s_sub, 1)

            def inverse_deviation(t, ln, eps, ready, shifted, done):
                r = rstd[:, ln, t % 2:t % 2 + 1]
                pool.wait_ge(ready, t + 1)
                pool.tensor_scalar(r, mv[:, ln, t % 2, 1:2], eps, None, ALU.add).then_inc(shifted, 1)
                pool.wait_ge(shifted, t + 1)
                pool.tensor_tensor(r, r, minus_half[:, :], ALU.pow).then_inc(done, 1)

            def rstd_1(t):
                if t >= 2:
                    pool.wait_ge(xn_ready, t - 1)
                inverse_deviation(t, 0, 1e-6, mv1, rstd1a, rstd1)

            def rstd_2(t):
                if t >= 2:
                    pool.wait_ge(xh_ready, t - 1)
                inverse_deviation(t, 1, 1e-5, mv2, rstd2a, rstd2)

            def xh_low(t):
                pool.wait_ge(xh_hi, t + 1)
                pool.tensor_tensor(xhl[:, t, 1, :], xhf[:, t % 2, :], xhl[:, t, 0, :], ALU.subtract
                                   ).then_inc(xh_lo, 1)

            def split_low(e, k):
                if k < 2:
                    pool.wait_ge(w1_hi, 2 * e + k + 1)
                    pool.tensor_tensor(w1s[:, e, 1, k, :], w1stage[:, k, :], w1s[:, e, 0, k, :], ALU.subtract
                                       ).then_inc(w1_lo, 1)
                else:
                    r = slice((k - 2) * NF // 2, (k - 1) * NF // 2)
                    pool.wait_ge(w2_hi, 2 * e + k - 1)
                    pool.tensor_tensor(w2s[:, e, 1, r, :], w2stage[:, r, :], w2s[:, e, 0, r, :], ALU.subtract
                                       ).then_inc(w2_lo, 1)

            for step in range(STEPS):
                stages(step, POOL_PROGRAM, (rstd_1, softmax_shift, rstd_2, xh_low), split_low)

        @block.scalar
        def _(act):
            def keep_weights():
                for m, bank in enumerate((p_qk, p_v, p_t[0], p_t[1])):
                    act.wait_ge(wt_mm, m + 1)
                    act.activation(wT[:, :, m * C:(m + 1) * C] if m < 3 else woT[0:CH, :, :],
                                   bank[0:CH, 0:2 * C].rearrange("p (k o) -> p k o", k=2), ACT.Copy,
                                   scale=SV if m == 2 else 1.0).then_inc(wt_kept, 1)

            def small_weights():
                act.wait_ge(small_loaded, 16 * 6)
                act.wait_ge(dve_consts, 2)
                act.activation(tab16[:, 0, :, :], tab[:, :, :], ACT.Copy).then_inc(small_hi, 1)
                act.activation(ws16[:, 0, :, :], wsr[:, :, :], ACT.Copy, scale=SF).then_inc(small_hi, 1)

            def keep_bias():
                act.wait_ge(bias_mm, 1)
                by_key = bias[:, :].rearrange("p (h m) -> p m h", h=NH)
                for half in range(2):
                    keys = slice(half * L // 2, (half + 1) * L // 2)
                    src = p_s[0:L, half * 512:half * 512 + NH * L // 2].rearrange("p (m h) -> p m h", h=NH)
                    for w in range(2):
                        act.activation(by_key[w * L:(w + 1) * L, keys, :], src, ACT.Copy).then_inc(bias_ready, 1)

            def keep_x(t):
                act.wait_ge(xT_mm, t + 1)
                act.activation(x2[:, t, :], p_x[:, 0:C], ACT.Copy).then_inc(x_kept, 1)

            def keep_normedT(t):
                act.wait_ge(xnT_mm, t + 1)
                if t >= 2:
                    act.wait_ge(qk_mm, t - 1)
                    act.wait_ge(v_mm, t - 1)
                act.activation(xnT[:, t % 2, :, :], p_n[0:CH, 0:2 * T].rearrange("p (k n) -> p k n", k=2),
                               ACT.Copy).then_inc(xnT_ready, 1)

            def keep_queries(t):
                act.wait_ge(qk_mm, t + 1)
                if t >= 2:
                    act.wait_ge(s_mm[0], t - 1)
                    act.wait_ge(s_mm[1], t - 1)
                act.activation(q[:, t % 2, :, :], p_qk[:, 0:2 * T].rearrange("p (c n) -> p c n", c=2), ACT.Copy
                               ).then_inc(q_kept, 1)

            def v_high(t):
                act.wait_ge(v_mm, t + 1)
                if t >= VB:
                    act.wait_ge(pv_mm, t - VB + 1)
                for w, h in WINDOW_HEADS:
                    act.activation(v2[h * L:(h + 1) * L, t % VB, 0, w, :, h, 0:HD], values(w, h), ACT.Copy
                                   ).then_inc(v_hi, 1)

            def exponentials(t):
                act.wait_ge(s_sub, t + 1)
                act.activation(sc[:, t % SB, :], sc[:, t % SB, :], ACT.Exp).then_inc(p_ready, 1)

            def weightsT_hi(t, h):
                act.wait_ge(pT_mm[h], t + 1)
                if t >= 2:
                    act.wait_ge(pv_mm, t - 1)
                act.activation(pT[:, t % 2, 0, 3 * h:3 * h + 3, :],
                               p_t[h][:, 0:3 * T].rearrange("p (n q) -> p n q", n=3), ACT.Copy).then_inc(pT_hi[h], 1)

            def weightsT_hi_0(t):
                weightsT_hi(t, 0)

            def weightsT_hi_1(t):
                weightsT_hi(t, 1)

            def keep_attendedT(t):
                act.wait_ge(oT_mm, t + 1)
                if t >= 2:
                    act.wait_ge(wo_mm, t - 1)
                act.activation(oT[0:CH, t % 2, :, :], p_n[0:CH, 0:2 * T].rearrange("p (k n) -> p k n", k=2),
                               ACT.Copy).then_inc(oT_ready, 1)

            def xh_high(t):
                act.wait_ge(xh_ready, t + 1)
                act.activation(xhl[:, t, 0, :], xhf[:, t % 2, :], ACT.Copy).then_inc(xh_hi, 1)

            def keep_xhT(t):
                act.wait_ge(xhT_mm, t + 1)
                act.activation(xhT[0:CH, t, :, :, :],
                               p_n[0:CH, 0:2 * T].bitcast(F16).rearrange("p (a k n) -> p a k n", a=2, k=2),
                               ACT.Copy).then_inc(xhT_ready, 1)

            def split_high(e, k):
                if k < 2:
                    if k == 0:
                        act.wait_ge(w1_loaded, 48 * (e + 1))
                        if e >= 2:
                            act.wait_ge(bias_mm, 1)
                    act.activation(w1stage[:, k, :], w1stage[:, k, :], ACT.Copy, scale=SF).then_inc(w1_scaled, 1)
                    act.wait_ge(w1_scaled, 2 * e + k + 1)
                    act.activation(w1s[:, e, 0, k, :], w1stage[:, k, :], ACT.Copy).then_inc(w1_hi, 1)
                else:
                    if k == 2:
                        act.wait_ge(w2_loaded, 16 * (e + 1))
                        if e >= NE - 2:
                            act.wait_ge(wt_mm, 4)
                    r = slice((k - 2) * NF // 2, (k - 1) * NF // 2)
                    act.activation(w2stage[:, r, :], w2stage[:, r, :], ACT.Copy, scale=SF).then_inc(w2_scaled, 1)
                    act.wait_ge(w2_scaled, 2 * e + k - 1)
                    act.activation(w2s[:, e, 0, r, :], w2stage[:, r, :], ACT.Copy).then_inc(w2_hi, 1)

            for step in range(STEPS):
                if step == 1:
                    keep_weights()
                    small_weights()
                stages(step, ACT_PROGRAM, (keep_x, keep_normedT, keep_queries, v_high, exponentials, weightsT_hi_0,
                                           weightsT_hi_1, keep_attendedT, xh_high, keep_xhT), split_high)
                if step == BIAS_STEP:
                    keep_bias()
            act.wait_ge(ex_in, 1)
            act.activation(ex[:, :, :], ex[:, :, :], ACT.Exp).then_inc(ex_out, 1)

        @block.vector
        def _(dve):
            dve.memset(w1stage[CH:CH + 1, 1, :], 0.0).then_inc(dve_consts, 1)
            dve.memset(wsr[CH:CH + 1, 1, :], 0.0).then_inc(dve_consts, 1)
            dve.memset(v2[:, :, 0, :, :, :, :], 0.0).then_inc(dve_consts, 1)

            def more_constants():
                dve.memset(v2[:, :, 1, :, :, :, :], 0.0).then_inc(dve_consts, 1)
                dve.memset(oT[CH:CH + 1, :, 0, :], 1.0).then_inc(dve_consts, 1)
                dve.wait_ge(dve_consts, 5)
                for h in range(2):
                    for w in range(2):
                        dve.memset(v2[64 * h:64 * h + 64, :, 0, w, :, h, HD], SV).then_inc(dve_consts, 1)

            def ones_rows():
                dve.memset(xhT[CH:CH + 1, :, 1, 0, :], 0.0).then_inc(dve_consts, 1)
                dve.memset(xhT[CH:CH + 1, :, 0, 0, :], 1.0).then_inc(dve_consts, 1)

            def small_weights():
                dve.wait_ge(small_hi, 2)
                dve.tensor_tensor(tab16[:, 1, :, :], tab[:, :, :], tab16[:, 0, :, :], ALU.subtract
                                  ).then_inc(small_lo, 1)
                dve.scalar_tensor_tensor(out=ws16[:, 1, :, :], in0=wsr[:, :, :], scalar=SF, in1=ws16[:, 0, :, :],
                                         op0=ALU.mult, op1=ALU.subtract).then_inc(small_lo, 1)

            def one_hots():
                dve.wait_ge(idx_loaded, 16)
                dve.wait_ge(consts, 1)
                for k in range(3):
                    dve.tensor_scalar(hot[0:TH, k, :], idx[0:TH, :], rowid[:, k:k + 1], None, ALU.is_equal
                                      ).then_inc(hot_ready, 1)

            def normed(t):
                dve.wait_ge(rstd1, t + 1)
                if t >= 2:
                    dve.wait_ge(xnT_mm, t - 1)
                dve.tensor_scalar(xn[:, t % 2, :], x2[:, t, :], mv[:, 0, t % 2, 0:1], rstd[:, 0, t % 2:t % 2 + 1],
                                  ALU.subtract, ALU.mult).then_inc(xn_ready, 1)

            def statistics_1(t):
                dve.wait_ge(x_kept, t + 1)
                dve.bn_stats(stat[:, 0, t % 2, :], x2[:, t, :]).then_inc(stat1, 1)
                dve.wait_ge(stat1, t + 1)
                dve.bn_aggr(mv[:, 0, t % 2, :], stat[:, 0, t % 2, :]).then_inc(mv1, 1)

            def head_blocks(t):
                dve.wait_ge(qk_mm, t + 1)
                dve.wait_ge(q_kept, t + 1)
                if t >= 2:
                    dve.wait_ge(s_mm[0], t - 1)
                    dve.wait_ge(s_mm[1], t - 1)
                for dst, rows, heads, chunk in ((ka, 128, HA, 2), (kc, RC, HC, 3)):
                    keys = p_qk[0:rows, chunk * T:(chunk + 1) * T].rearrange("p (w m) -> p w m", w=2)
                    shape = [rows, 2, heads, L]
                    blk = dve.tensor_tensor(
                        dst[:, t % 2, :, :, :], keys.unsqueeze(2).to_broadcast(shape),
                        mask[0:rows, 0:heads].unsqueeze(1).unsqueeze(3).to_broadcast(shape), ALU.mult)
                blk.then_inc(kbd_ready, 1)

            def v_low(t):
                dve.wait_ge(v_hi, 4 * t + 4)
                for w, h in WINDOW_HEADS:
                    hi, lo = (v2[h * L:(h + 1) * L, t % VB, a, w, :, h, 0:HD] for a in range(2))
                    dve.tensor_tensor(lo, values(w, h), hi, ALU.subtract).then_inc(v_lo, 1)

            def add_bias(t, h):
                cols = SCORE_COLS[h]
                dve.wait_ge(s_mm[h], t + 1)
                dve.wait_ge(bias_ready, 4)
                if t >= SB:
                    dve.wait_ge(pT_mm[0], t - SB + 1)
                    dve.wait_ge(pT_mm[1], t - SB + 1)
                dve.scalar_tensor_tensor(out=sc[:, t % SB, cols], in0=p_s[:, cols], scalar=S_SCALE,
                                         in1=bias[:, cols], op0=ALU.mult, op1=ALU.add).then_inc(s_biased[h], 1)

            def add_bias_0(t):
                add_bias(t, 0)

            def add_bias_1(t):
                add_bias(t, 1)

            def row_max(t):
                dve.wait_ge(s_biased[0], t + 1)
                dve.wait_ge(s_biased[1], t + 1)
                if t >= 2:
                    dve.wait_ge(s_sub, t - 1)
                dve.tensor_reduce(mx[:, t % 2, :], sc[:, t % SB, :].rearrange("p (h m) -> p h m", h=NH), AX, ALU.max
                                  ).then_inc(s_max, 1)

            def weightsT_lo(t, h):
                dve.wait_ge(pT_hi[h], t + 1)
                if t >= 2:
                    dve.wait_ge(pv_mm, t - 1)
                dve.tensor_tensor(pT[:, t % 2, 1, 3 * h:3 * h + 3, :],
                                  p_t[h][:, 0:3 * T].rearrange("p (n q) -> p n q", n=3),
                                  pT[:, t % 2, 0, 3 * h:3 * h + 3, :], ALU.subtract).then_inc(pT_lo[h], 1)

            def weightsT_lo_0(t):
                weightsT_lo(t, 0)

            def weightsT_lo_1(t):
                weightsT_lo(t, 1)

            def normalise(t):
                dve.wait_ge(pv_mm, t + 1)
                heads = p_v[:, 0:NH * VW].rearrange("p (h d) -> p h d", h=NH)
                if t >= 1:
                    dve.wait_ge(o_norm, t)
                dve.reciprocal(rden[:, :], heads[:, :, HD]).then_inc(rden_ready, 1)
                dve.wait_ge(rden_ready, t + 1)
                if t >= 2:
                    dve.wait_ge(oT_mm, t - 1)
                dve.tensor_tensor(on[:, t % 2, :].rearrange("p (h d) -> p h d", h=NH), heads[:, :, 0:HD],
                                  rden[:, :].unsqueeze(2).to_broadcast([128, NH, HD]), ALU.mult).then_inc(o_norm, 1)

            def residual(t):
                dve.wait_ge(wo_mm, t + 1)
                dve.scalar_tensor_tensor(out=x2[:, t, :], in0=p_x[:, 0:C], scalar=1.0, in1=x2[:, t, :],
                                         op0=ALU.mult, op1=ALU.add).then_inc(x2_ready, 1)
                dve.wait_ge(x2_ready, t + 1)
                dve.bn_stats(stat[:, 1, t % 2, :], x2[:, t, :]).then_inc(stat2, 1)
                dve.wait_ge(stat2, t + 1)
                dve.bn_aggr(mv[:, 1, t % 2, :], stat[:, 1, t % 2, :]).then_inc(mv2, 1)

            def xh(t):
                dve.wait_ge(rstd2, t + 1)
                if t >= 2:
                    dve.wait_ge(xh_hi, t - 1)
                    dve.wait_ge(xh_lo, t - 1)
                dve.tensor_scalar(xhf[:, t % 2, :], x2[:, t, :], mv[:, 1, t % 2, 0:1], rstd[:, 1, t % 2:t % 2 + 1],
                                  ALU.subtract, ALU.mult).then_inc(xh_ready, 1)

            def keep_logits(t):
                dve.wait_ge(lg_mm, t + 1)
                dve.tensor_scalar(lg[:, t, :], p_x[:, 0:NE], 1.0 / SF, None, ALU.mult).then_inc(lg_kept, 1)

            for step in range(STEPS):
                if step == 1:
                    more_constants()
                    small_weights()
                    one_hots()
                if step == 4:
                    ones_rows()
                stages(step, DVE_PROGRAM, (statistics_1, normed, head_blocks, v_low, add_bias_0, add_bias_1, row_max,
                                           weightsT_lo_0, weightsT_lo_1, normalise, residual, xh, keep_logits), None)

            links = [0]

            def link(ins):
                links[0] += 1
                ins.then_inc(chain, 1)
                dve.wait_ge(chain, links[0])

            def by_expert(column):
                return column.unsqueeze(2).to_broadcast([128, NT, NE])

            def over_tiles(row):
                return row.unsqueeze(1).to_broadcast([128, NT, NE])

            top, total, expert, slotf = (r16[:, i, :] for i in range(4))
            dve.wait_ge(lg_kept, NT)
            link(dve.tensor_reduce(top, lg[:, :, :], AX, ALU.max))
            link(dve.tensor_tensor(lg[:, :, :], lg[:, :, :], by_expert(top), ALU.subtract))
            dve.tensor_copy(ex[:, :, :], lg[:, :, :]).then_inc(ex_in, 1)
            link(dve.tensor_scalar(cand[:, :, :], lg[:, :, :], 0.0, float(NE), ALU.is_lt, ALU.mult))
            link(dve.tensor_tensor(cand[:, :, :], cand[:, :, :], over_tiles(eio[:, :]), ALU.add))
            link(dve.tensor_reduce(expert, cand[:, :, :], AX, ALU.min))
            dve.tensor_tensor(oh[:, :, :], over_tiles(eio[:, :]), by_expert(expert), ALU.is_equal
                              ).then_inc(oh_ready, 1)
            dve.wait_ge(ex_out, 1)
            link(dve.tensor_reduce(total, ex[:, :, :], AX, ALU.add))
            link(dve.reciprocal(pmax[:, :], total))
            link(dve.tensor_scalar(omp[:, :], pmax[:, :], -1.0, 1.0, ALU.mult, ALU.add))
            count, tiles, first, end = (cnt[:, i, :] for i in range(4))
            dve.wait_ge(rank_mm, 1)
            link(dve.tensor_copy(count, p_v[:, 0:NE]))
            above = big[:, 0:NE * NT].rearrange("p (e k) -> p e k", e=NE)
            link(dve.tensor_tensor(above, count.unsqueeze(2).to_broadcast([128, NE, NT]),
                                   kio[:, :].unsqueeze(1).to_broadcast([128, NE, NT]), ALU.is_gt))
            link(dve.tensor_reduce(tiles, above, AX, ALU.add))
            before = big[:, 0:NE * NE].rearrange("p (e k) -> p e k", e=NE)
            link(dve.tensor_tensor(before, tiles.unsqueeze(1).to_broadcast([128, NE, NE]), ltm[:, :, :], ALU.mult))
            link(dve.tensor_reduce(first, before, AX, ALU.add))
            link(dve.tensor_tensor(end, first, tiles, ALU.add))
            link(dve.tensor_scalar(first, first, float(T), None, ALU.mult))
            link(dve.tensor_tensor(cand[:, :, :], p_qk[:, 0:NT * NE].rearrange("p (t e) -> p t e", e=NE),
                                   over_tiles(first), ALU.add))
            link(dve.tensor_tensor(cand[:, :, :], cand[:, :, :], oh[:, :, :], ALU.mult))
            link(dve.tensor_reduce(slotf, cand[:, :, :], AX, ALU.add))
            link(dve.tensor_copy(slot[:, :], slotf))
            passed = big[0:1, 0:NR * NE].rearrange("p (j e) -> p j e", e=NE)
            link(dve.tensor_tensor(passed, end[0:1, :].unsqueeze(1).to_broadcast([1, NR, NE]),
                                   jio[:, :].unsqueeze(2).to_broadcast([1, NR, NE]), ALU.is_le))
            link(dve.tensor_reduce(ejf[:, 0, :], passed, AX, ALU.add))
            link(dve.tensor_scalar(ejf[:, 1, :], ejf[:, 0, :], float(NE - 1), None, ALU.min))
            link(dve.tensor_copy(etile[:, :], ejf[:, 1, :]))

        @block.tensor
        def _(pe):
            pe.wait_ge(consts, 1)

            def transpose_weights():
                pe.wait_ge(watt_loaded, 16 * 4)
                for m, bank in enumerate((p_qk, p_v, p_t[0], p_t[1])):
                    for k in range(2):
                        for r in range(2):
                            mm = pe.transpose(bank[0:CH, k * C + r * CH:k * C + (r + 1) * CH],
                                              watt[:, m, r, k * CH:(k + 1) * CH], ident[0:CH, 0:CH])
                    mm.then_inc(wt_mm, 1)

            def position_bias():
                pe.wait_ge(hot_ready, 3)
                pe.wait_ge(small_lo, 2)
                for m in range(L):
                    col = (m // (L // 2)) * 512 + (m % (L // 2)) * NH
                    n = 0
                    for k in range(3):
                        w = hot[0:TH, k, :].rearrange("p (l m) -> p l m", m=L)[:, :, m]
                        for part in range(2):
                            mm = pe.matmul(p_s[0:L, col:col + NH], w, tab16[:, part, k, :], start=(n == 0), stop=(n == 5))
                            n += 1
                mm.then_inc(bias_mm, 1)

            def bank_read(stage, t, readers):
                for other, read, per_tile in readers:
                    n = ahead(stage, t, other)
                    if n >= 1:
                        pe.wait_ge(read, per_tile * n)

            def x_to_tokens(t):
                b = t // TPI
                pe.wait_ge(x_loaded[b % XI], 16 * (b // XI + 1))
                bank_read("x_to_tokens", t, P_X_READ)
                for k in range(2):
                    cols = xin[:, b % XI, k, (t % TPI) * T:(t % TPI + 1) * T]
                    mm = pe.transpose(p_x[:, k * CH:(k + 1) * CH], cols, ident[0:CH, 0:CH])
                mm.then_inc(xT_mm, 1)

            def normed_to_channels(t):
                pe.wait_ge(xn_ready, t + 1)
                bank_read("normed_to_channels", t, P_N_READ)
                for k in range(2):
                    mm = pe.transpose(to_windows(p_n[0:CH, k * T:(k + 1) * T]), xn[:, t % 2, k * CH:(k + 1) * CH],
                                      ident[:, :])
                mm.then_inc(xnT_mm, 1)

            def project(t):
                pe.wait_ge(xnT_ready, t + 1)
                if t == 0:
                    pe.wait_ge(wt_kept, 4)
                if t >= 1:
                    pe.wait_ge(q_kept, t)
                    pe.wait_ge(kbd_ready, t)
                for c, row in enumerate((0, 128, C, C + 128)):
                    for k in range(2):
                        mm = pe.matmul(p_qk[:, c * T:(c + 1) * T], wT[:, k, row:row + 128], xnT[:, t % 2, k, :],
                                       start=(k == 0), stop=(k == 1))
                mm.then_inc(qk_mm, 1)

            def project_values(t):
                pe.wait_ge(xnT_ready, t + 1)
                if t == 0:
                    pe.wait_ge(wt_kept, 4)
                bank_read("project_values", t, P_V_READ)
                for k in range(2):
                    mm = pe.matmul(p_v[:, 0:C], xnT[:, t % 2, k, :], wT[:, k, 2 * C:3 * C],
                                   start=(k == 0), stop=(k == 1))
                mm.then_inc(v_mm, 1)

            def scores(t, h):
                pe.wait_ge(q_kept, t + 1)
                pe.wait_ge(kbd_ready, t + 1)
                if t == 0:
                    if h == FIRST_SCORES:
                        position_bias()
                    pe.wait_ge(bias_ready, 4)
                else:
                    pe.wait_ge(s_biased[h], t)
                rows, keys = ((128, ka), (RC, kc))[h]
                for w in range(2):
                    mm = pe.matmul(p_s[w * L:(w + 1) * L, SCORE_COLS[h]], q[0:rows, t % 2, h, w * L:(w + 1) * L],
                                   keys[:, t % 2, w, :, :], start=True, stop=True)
                mm.then_inc(s_mm[h], 1)

            def scores_0(t):
                scores(t, 0)

            def scores_1(t):
                scores(t, 1)

            def weights_to_keys(t, h):
                pe.wait_ge(p_ready, t + 1)
                if t == 0:
                    pe.wait_ge(wt_kept, 4)
                if t >= 1:
                    pe.wait_ge(pT_lo[h], t)
                for n in range(3):
                    pair = 3 * h + n
                    mm = pe.transpose(p_t[h][:, n * T:(n + 1) * T],
                                      sc[:, t % SB, pair * 2 * L:(pair + 1) * 2 * L], ident[:, :])
                mm.then_inc(pT_mm[h], 1)

            def weights_to_keys_0(t):
                weights_to_keys(t, 0)

            def weights_to_keys_1(t):
                weights_to_keys(t, 1)

            def attend(t):
                pe.wait_ge(pT_lo[0], t + 1)
                pe.wait_ge(pT_lo[1], t + 1)
                pe.wait_ge(v_lo, 4 * t + 4)
                bank_read("attend", t, P_V_READ)
                for w in range(2):
                    for pair in range(NP):
                        for n, (a, b) in enumerate(PASSES):
                            mm = pe.matmul(p_v[w * L:(w + 1) * L, pair * 2 * VW:(pair + 1) * 2 * VW],
                                           pT[:, t % 2, a, pair, w * L:(w + 1) * L], v2[:, t % VB, b, w, pair, :, :],
                                           start=(n == 0), stop=(n == 2))
                mm.then_inc(pv_mm, 1)

            def attended_to_channels(t):
                pe.wait_ge(o_norm, t + 1)
                bank_read("attended_to_channels", t, P_N_READ)
                for k in range(2):
                    mm = pe.transpose(to_raster(p_n[0:CH, k * T:(k + 1) * T]), on[:, t % 2, k * CH:(k + 1) * CH],
                                      ident[:, :])
                mm.then_inc(oT_mm, 1)

            def output_projection(t):
                pe.wait_ge(oT_ready, t + 1)
                bank_read("output_projection", t, P_X_READ)
                for k in range(2):
                    mm = pe.matmul(p_x[:, 0:C], oT[0:CH + 1 - k, t % 2, k, :], woT[0:CH + 1 - k, k, :],
                                   start=(k == 0), stop=(k == 1))
                mm.then_inc(wo_mm, 1)

            def xh_to_channels(t):
                pe.wait_ge(xh_lo, t + 1)
                bank_read("xh_to_channels", t, P_N_READ)
                bank = p_n[0:CH, 0:2 * T].bitcast(F16).rearrange("p (a k n) -> p a k n", a=2, k=2)
                for a in range(2):
                    for k in range(2):
                        mm = pe.transpose(bank[:, a, k, :], xhl[:, t, a, k * CH:(k + 1) * CH], ident16[:, :])
                mm.then_inc(xhT_mm, 1)

            def logits(t):
                pe.wait_ge(xhT_ready, t + 1)
                bank_read("logits", t, P_X_READ)
                n = 0
                for k in range(2):
                    for a, b in PASSES:
                        mm = pe.matmul(p_x[:, 0:NE], xhT[0:CH + 1 - k, t, a, k, :], ws16[0:CH + 1 - k, b, k, :],
                                       start=(n == 0), stop=(n == 5))
                        n += 1
                mm.then_inc(lg_mm, 1)

            P_X_READ = (("x_to_tokens", x_kept, 1), ("output_projection", x2_ready, 1), ("logits", lg_kept, 1))
            P_N_READ = (("normed_to_channels", xnT_ready, 1), ("attended_to_channels", oT_ready, 1),
                        ("xh_to_channels", xhT_ready, 1))
            P_V_READ = (("project_values", v_lo, 4), ("attend", o_norm, 1))

            for step in range(STEPS):
                if step == 1:
                    transpose_weights()
                stages(step, PE_PROGRAM, (x_to_tokens, normed_to_channels, project, project_values, scores_0, scores_1,
                                          weights_to_keys_0, weights_to_keys_1, attend, attended_to_channels,
                                          output_projection, xh_to_channels, logits), None)
            pe.wait_ge(dve_consts, 11)
            pe.wait_ge(oh_ready, 1)
            flat = oh[:, :, :].rearrange("p t e -> p (t e)")
            pe.matmul(p_qk[:, 0:NT * NE], tri[:, :], flat, start=True, stop=False, skip_group_check=True)
            for d in range(1, NT):
                pe.matmul(p_qk[:, d * NE:NT * NE], ones16[:, :], flat[:, 0:(NT - d) * NE], start=False,
                          stop=(d == NT - 1), skip_group_check=True)
            for t in range(NT):
                mm = pe.matmul(p_v[:, 0:NE], ones16[:, :], oh[:, t, :], start=(t == 0), stop=(t == NT - 1))
            mm.then_inc(rank_mm, 1)



def experts(nc, g):
    (ident, ident16, ones16, w1s, w2s,  x2, xhl, xhT, pmax, omp, slot, etile, xs, ys, out) = (
        g[n] for n in ("ident", "ident16", "ones16", "w1s", "w2s", "x2", "xhl", "xhT",
                       "pmax", "omp", "slot", "etile", "xs", "ys", "out"))
    HF = NF // 2
    YB, GB = 4, 8
    FIRST = NT // 2
    TILES = ([("common", t) for t in range(FIRST)] + [("routed", j) for j in range(NR)]
             + [("common", t) for t in range(FIRST, NT)])
    N = len(TILES)
    MIX = FIRST + NR + 3

    def common_at(t):
        return t if t < FIRST else t + NR

    def routed_at(j):
        return FIRST + j

    def next_routed(n):
        return TILES[n + 1][1] if n + 1 < N and TILES[n + 1][0] == "routed" else None

    def mixes(step):
        last = 2 * (step - MIX) + 2
        if step == N:
            return range(max(0, last - 2), NT)
        return range(max(0, last - 2), max(0, min(last, NT)))

    with ExitStack() as ctx:
        def sb(name, shape, dt):
            return ctx.enter_context(nc.sbuf_tensor(name, shape, dt))

        def pb(name):
            return ctx.enter_context(nc.psum_tensor(name, [128, 512], F32))

        def sem(name):
            return ctx.enter_context(nc.semaphore(name))

        base = sb("base", [128, NT, C], F32)
        hf = sb("hf", [128, 2, 2, HF * T], F32)
        hp = sb("hp", [128, 2, 2, NF, T], F16)
        w1d = sb("w1d", [CH + 1, 2, 2, 2, FF], F16)
        w2d = sb("w2d", [128, 2, 2, NF, C], F16)
        b2d = sb("b2d", [CH + 1, 2, 2, C], F16)
        tok = sb("tok", [128, YB, 2 * C], F16)
        tokT = sb("tokT", [CH + 1, 2, 2, 2, T], F16)
        yo = sb("yo", [128, YB, C], F32)
        sel = sb("sel", [128, GB, C], F32)
        fin = sb("fin", [128, 2, C], F32)
        outc = sb("outc", [CH, 2, 2, IMG * IMG], F32)

        p_h = [[pb(f"p_h{i}{j}") for j in range(2)] for i in range(2)]
        p_y = [pb(f"p_y{i}") for i in range(2)]
        p_k = pb("p_k")
        p_f = [pb("p_f"), p_k]

        consts = sem("f_consts")
        scattered = sem("scattered")
        tok_loaded = [sem(f"tok_loaded{i}") for i in range(YB)]
        tokT_mm = sem("tokT_mm")
        tokT_ready = sem("tokT_ready")
        w1_copied = sem("w1_copied")
        w2_copied = sem("w2_copied")
        h_mm = [sem("h_mm0"), sem("h_mm1")]
        h_act = [sem("h_act0"), sem("h_act1")]
        h_hi = [sem("h_hi0"), sem("h_hi1")]
        h_lo = [sem("h_lo0"), sem("h_lo1")]
        y_mm = sem("y_mm")
        y_kept = sem("y_kept")
        base_ready = sem("base_ready")
        y_stored = [sem(f"y_stored{i}") for i in range(YB)]
        gathered = [sem(f"gathered{i}") for i in range(GB)]
        mixed = sem("mixed")
        fin_mm = sem("fin_mm")
        fin_kept = sem("fin_kept")
        out_stored = [sem("out_stored0"), sem("out_stored1")]

        block = ctx.enter_context(nc.Block())

        @block.gpsimd
        def _(pool):
            for t in range(NT):
                pool.indirect_dma_start(out=xs, out_offset=bass.IndirectOffsetOnAxis(ap=slot[:, t:t + 1], axis=0),
                                        in_=xhl[:, t, :, :].rearrange("p a c -> p (a c)"), in_offset=None
                                        ).then_inc(scattered, 16)
            for i in range(YB):
                pool.wait_ge(y_stored[i], 16 * len(range(i, NR, YB)))
            for t in range(NT):
                if t >= GB:
                    pool.wait_ge(mixed, t - GB + 1)
                pool.indirect_dma_start(out=sel[:, t % GB, :], out_offset=None, in_=ys,
                                        in_offset=bass.IndirectOffsetOnAxis(ap=slot[:, t:t + 1], axis=0)
                                        ).then_inc(gathered[t % GB], 16)

        @block.sync
        def _(sp):
            def load(j):
                if j >= YB:
                    sp.wait_ge(tokT_mm, j - YB + 1)
                sp.dma_start(tok[:, j % YB, :], xs[j * T:(j + 1) * T, :]).then_inc(tok_loaded[j % YB], 16)

            sp.wait_ge(scattered, 16 * NT)
            for j in range(YB):
                load(j)
            for j in range(NR):
                if j + YB < NR:
                    load(j + YB)
                sp.wait_ge(y_kept, routed_at(j) + 1)
                sp.dma_start(ys[j * T:(j + 1) * T, :], yo[:, j % YB, :]).then_inc(y_stored[j % YB], 16)
            for b in range(B):
                sp.wait_ge(fin_kept, TPI * (b + 1))
                sp.dma_start(out[b].rearrange("(k c) i j -> c k (i j)", k=2), outc[:, b % 2, :, :]
                             ).then_inc(out_stored[b % 2], 16)
            for i in range(2):
                sp.wait_ge(out_stored[i], 16 * B // 2)

        @block.scalar
        def _(act):
            def hidden(n):
                for h in range(2):
                    act.wait_ge(h_mm[h], n + 1)
                    if n >= 2:
                        act.wait_ge(h_lo[h], n - 1)
                        act.wait_ge(y_mm, n - 1)
                    act.activation(hp[:, n % 2, 0, HF * h:HF * h + HF, :],
                                   p_h[n % 2][h][:, 0:HF * T].rearrange("p (f t) -> p f t", f=HF), ACT.Gelu,
                                   scale=1.0 / SF).then_inc(h_hi[h], 1)
                    act.activation(hf[:, n % 2, h, :], p_h[n % 2][h][:, 0:HF * T], ACT.Gelu, scale=1.0 / SF
                                   ).then_inc(h_act[h], 1)

            def tokens(j):
                act.wait_ge(tokT_mm, j + 1)
                if j >= 2:
                    act.wait_ge(h_mm[1], routed_at(j - 2) + 1)
                act.activation(tokT[0:CH, j % 2, :, :, :],
                               p_k[0:CH, 0:2 * T].bitcast(F16).rearrange("p (a k n) -> p a k n", a=2, k=2),
                               ACT.Copy).then_inc(tokT_ready, 1)

            def keep_result(t):
                b = t // TPI
                act.wait_ge(fin_mm, t + 1)
                if b >= 2 and t % TPI == 0:
                    act.wait_ge(out_stored[b % 2], 16 * (b // 2))
                act.activation(outc[:, b % 2, :, (t % TPI) * T:(t % TPI + 1) * T],
                               p_f[t % 2][0:CH, 0:2 * T].rearrange("p (k n) -> p k n", k=2), ACT.Copy
                               ).then_inc(fin_kept, 1)

            act.wait_ge(consts, 1)
            for n in range(N + 1):
                j = next_routed(n)
                if j is not None:
                    tokens(j)
                if n < N:
                    hidden(n)
                for t in mixes(n):
                    keep_result(t)

        @block.vector
        def _(dve):
            dve.memset(tokT[CH:CH + 1, :, 1, :, :], 0.0)
            dve.memset(tokT[CH:CH + 1, :, 0, :, :], 1.0).then_inc(consts, 1)

            def weights_1(j):
                e = dve.value_load(etile[0:1, j:j + 1], min_val=0, max_val=NE - 1)
                if j >= 2:
                    dve.wait_ge(h_mm[1], routed_at(j - 2) + 1)
                dve.tensor_copy(w1d[:, j % 2, :, :, :], w1s[:, e, :, :, :]).then_inc(w1_copied, 1)
                return e

            def weights_2(j, e):
                if j >= 2:
                    dve.wait_ge(y_mm, routed_at(j - 2) + 1)
                dve.tensor_copy(b2d[CH:CH + 1, j % 2, :, :], w1s[CH:CH + 1, e, :, 1, 0:C])
                dve.tensor_copy(w2d[:, j % 2, :, :, :], w2s[:, e, :, :, :]).then_inc(w2_copied, 1)

            def hidden_lo(n):
                for h in range(2):
                    dve.wait_ge(h_act[h], n + 1)
                    if n >= 2:
                        dve.wait_ge(y_mm, n - 1)
                    dve.tensor_tensor(hp[:, n % 2, 1, HF * h:HF * h + HF, :],
                                      hf[:, n % 2, h, :].rearrange("p (f t) -> p f t", f=HF),
                                      hp[:, n % 2, 0, HF * h:HF * h + HF, :], ALU.subtract).then_inc(h_lo[h], 1)

            def keep_y(n):
                kind, i = TILES[n]
                dve.wait_ge(y_mm, n + 1)
                if kind == "common":
                    dve.tensor_scalar(base[:, i, :], p_y[n % 2][:, 0:C], omp[:, i:i + 1], 1.0 / SF,
                                      ALU.mult, ALU.mult).then_inc(y_kept, 1)
                    dve.wait_ge(y_kept, n + 1)
                    dve.tensor_tensor(base[:, i, :], base[:, i, :], x2[:, i, :], ALU.add).then_inc(base_ready, 1)
                else:
                    if i >= YB:
                        dve.wait_ge(y_stored[i % YB], 16 * (i // YB))
                    dve.tensor_scalar(yo[:, i % YB, :], p_y[n % 2][:, 0:C], 1.0 / SF, None, ALU.mult
                                      ).then_inc(y_kept, 1)

            def mix(t):
                dve.wait_ge(gathered[t % GB], 16 * (t // GB + 1))
                dve.wait_ge(base_ready, t + 1)
                if t >= 2:
                    dve.wait_ge(fin_mm, t - 1)
                dve.scalar_tensor_tensor(out=fin[:, t % 2, :], in0=sel[:, t % GB, :], scalar=pmax[:, t:t + 1],
                                         in1=base[:, t, :], op0=ALU.mult, op1=ALU.add).then_inc(mixed, 1)

            for n in range(N + 1):
                j = next_routed(n)
                if j is not None:
                    e = weights_1(j)
                if n < N:
                    hidden_lo(n)
                if n >= 1:
                    keep_y(n - 1)
                if j is not None:
                    weights_2(j, e)
                for t in mixes(n):
                    mix(t)

        @block.tensor
        def _(pe):
            pe.wait_ge(consts, 1)

            def tokens(j):
                pe.wait_ge(tok_loaded[j % YB], 16 * (j // YB + 1))
                if j >= 1:
                    pe.wait_ge(tokT_ready, j)
                bank = p_k[0:CH, 0:2 * T].bitcast(F16).rearrange("p (a k n) -> p a k n", a=2, k=2)
                for a in range(2):
                    for k in range(2):
                        col = a * C + k * CH
                        mm = pe.transpose(bank[:, a, k, :], tok[:, j % YB, col:col + CH], ident16[:, :])
                mm.then_inc(tokT_mm, 1)

            def hidden(n):
                kind, i = TILES[n]
                if n >= 2:
                    for h in range(2):
                        pe.wait_ge(h_act[h], n - 1)
                if kind == "common":
                    w, xT = w1s[:, 0, :, :, :], xhT[:, i, :, :, :]
                else:
                    pe.wait_ge(w1_copied, i + 1)
                    pe.wait_ge(tokT_ready, i + 1)
                    w, xT = w1d[:, i % 2, :, :, :], tokT[:, i % 2, :, :, :]
                for f in range(NF):
                    m = 0
                    for k in range(2):
                        for a, b in PASSES:
                            mm = pe.matmul(p_h[n % 2][f // HF][:, (f % HF) * T:(f % HF + 1) * T],
                                           w[0:CH + 1 - k, a, k, f * 128:(f + 1) * 128], xT[0:CH + 1 - k, b, k, :],
                                           start=(m == 0), stop=(m == 5))
                            m += 1
                    if f % HF == HF - 1:
                        mm.then_inc(h_mm[f // HF], 1)

            def outputs(n):
                kind, i = TILES[n]
                if n >= 2:
                    pe.wait_ge(y_kept, n - 1)
                if kind == "common":
                    w, b2 = w2s[:, 0, :, :, :], w1s[CH:CH + 1, 0, :, 1, 0:C]
                else:
                    pe.wait_ge(w2_copied, i + 1)
                    w, b2 = w2d[:, i % 2, :, :, :], b2d[CH:CH + 1, i % 2, :, :]
                y = p_y[n % 2][:, 0:C]
                for a in range(2):
                    pe.matmul(y, ones16[CH:CH + 1, :], b2[:, a, :], start=(a == 0), stop=False)
                for f in range(NF):
                    if f % HF == 0:
                        pe.wait_ge(h_lo[f // HF], n + 1)
                    for m, (a, b) in enumerate(PASSES):
                        mm = pe.matmul(y, hp[:, n % 2, a, f, :], w[:, b, f, :], start=False,
                                       stop=(f == NF - 1 and m == 2))
                mm.then_inc(y_mm, 1)

            def result_to_channels(t):
                pe.wait_ge(mixed, t + 1)
                if t >= 2:
                    pe.wait_ge(fin_kept, t - 1)
                elif t == 1:
                    pe.wait_ge(tokT_ready, NR)
                for k in range(2):
                    mm = pe.transpose(p_f[t % 2][0:CH, k * T:(k + 1) * T], fin[:, t % 2, k * CH:(k + 1) * CH],
                                      ident[:, :])
                mm.then_inc(fin_mm, 1)

            for n in range(N + 1):
                j = next_routed(n)
                if j is not None:
                    tokens(j)
                if n < N:
                    hidden(n)
                if n >= 1:
                    outputs(n - 1)
                for t in mixes(n):
                    result_to_channels(t)


_INS = ['x', 'L0_conv_Wq', 'L0_conv_Wk', 'L0_conv_Wv', 'L0_conv_Wo_w', 'L0_conv_Wo_b', 'L0_conv_rel_pos_bias',
        'L0_conv_rel_coords', 'L0_ffn_Ws', 'L0_ffn_bs', 'L0_ffn_W1', 'L0_ffn_b1', 'L0_ffn_W2', 'L0_ffn_b2']
_OUTS = [((B, C, IMG, IMG), 'float32')]


def kernel(**inputs):
    import numpy as _np
    import concourse.bacc as _bacc
    from concourse import mybir as _mybir
    from concourse.bass_utils import run_bass_kernel_spmd as _run

    nc = _bacc.Bacc("TRN2", target_bir_lowering=False, num_devices=1)
    arrays, args = {}, []
    for name in _INS:
        a = _np.ascontiguousarray(inputs[name])
        arrays[f"in_{name}_dram"] = a
        args.append(nc.dram_tensor(f"in_{name}_dram", a.shape, _mybir.dt.from_np(a.dtype), kind="ExternalInput").ap())
    for i, (shape, dtype) in enumerate(_OUTS):
        dt = _mybir.dt.from_np(_np.dtype(dtype))
        args.append(nc.dram_tensor(f"out_{i}_dram", shape, dt, kind="ExternalOutput").ap())
    build(nc, *args)
    r = _run(nc, [arrays], core_ids=[0])
    got = tuple(r.results[0][f"out_{i}_dram"] for i in range(len(_OUTS)))
    return got[0]
```

```python
from contextlib import ExitStack

import concourse.bass as bass
from concourse import mybir

F32 = mybir.dt.float32
F16 = mybir.dt.float16
I32 = mybir.dt.int32
U32 = mybir.dt.uint32
ALU = mybir.AluOpType
ACT = mybir.ActivationFunctionType
AX = mybir.AxisListType.X

B, C, IMG = 8, 192, 16
WS, NH = 8, 12
HD = C // NH
L = WS * WS
T = 128
NT = B * IMG * IMG // T
TPI = IMG * IMG // T
CH = 96
NE, FF = 9, 768
NF = FF // 128
NR = (NT * T + NE * (T - 1)) // T
TBL = (2 * WS - 1) ** 2
TH = (TBL + 1) // 2
HA = 128 // HD
HC = NH - HA
RC = HC * HD
NP = NH // 2
VW = HD + 1

PASSES = ((0, 0), (0, 1), (1, 0))
SV = 16.0
SF = 64.0
S_SCALE = 1.0 / float(HD) ** 0.5


LC = C - 128
TAIL = 128 - LC
XW = 2 * C + TAIL
KB = LC + 33
ER = 32
HI, MIX, BIAS, LO = range(4)
X_HI, X_LO, X_MIX, X_BIAS = range(4)
PACKED = ((HI, X_HI, 128), (LO, X_HI, 128), (HI, X_LO, 128), (MIX, X_MIX, 128), (BIAS, X_BIAS, KB))


def packed_transposes(pe, bank, rows, ident16):
    for block, col in ((X_HI, 0), (X_LO, C), (X_BIAS, C + 128)):
        pe.transpose(bank[:, block, :], rows[:, col:col + 128], ident16[:, :])
    for half in range(2):
        mm = pe.transpose(bank[half * LC:(half + 1) * LC, X_MIX, :], rows[:, 128:C], ident16[:, :])
    return mm


def to_windows(ap):
    return ap.rearrange("p (w i j) -> p i w j", w=2, j=WS)


def to_raster(ap):
    return ap.rearrange("p (i w j) -> p w i j", w=2, j=WS)


def build(nc, x, Wq, Wk, Wv, Wo_w, Wo_b, rpb, rel, Ws, bs, W1, b1, W2, b2, out):
    xs = nc.dram_tensor("sorted_tokens", (NR * T, 2 * C), F16, kind="Internal").ap()
    ys = nc.dram_tensor("sorted_outputs", (NR * T, C), F32, kind="Internal").ap()
    with ExitStack() as whole:
        def sbw(name, shape, dt):
            return whole.enter_context(nc.sbuf_tensor(name, shape, dt))

        def sem(name):
            return whole.enter_context(nc.semaphore(name))

        ident = sbw("ident", [128, 128], F32)
        ident16 = sbw("ident16", [128, 128], F16)
        ones16 = sbw("ones16", [128, 128], F16)
        w1s = sbw("w1s", [128, NE, 4, FF], F16)
        w1stage = sbw("w1stage", [128, 2, FF], F32)
        w2stage = sbw("w2stage", [128, NF, C], F32)
        b2s = sbw("b2s", [2 * ER, C], F16)
        pid = sbw("pid", [2 * ER, 1], F32)
        w2s = sbw("w2s", [128, NE, 2, NF, C], F16)
        x2 = sbw("x2", [128, NT, C], F32)
        xhl = sbw("xhl", [128, NT, XW], F16)
        xhT = sbw("xhT", [128, NT, 4, T], F16)
        lg = sbw("lg", [128, NT, NE], F32)
        tri = sbw("tri", [128, 128], F16)
        ltm = sbw("ltm", [128, NE, NE], F32)
        eio = sbw("eio", [128, NE], F32)
        kio = sbw("kio", [128, NT], F32)
        jio = sbw("jio", [2 * ER, NR], F32)
        pmax = sbw("pmax", [128, NT], F32)
        omp = sbw("omp", [128, NT], F32)
        slot = sbw("slot", [128, NT], U32)
        etile = sbw("etile", [1, NR], I32)

        attention(nc, locals())
        experts(nc, locals())


def attention(nc, g):
    (ident, ident16, ones16, w1s, w2s,  x2, xhl, xhT, lg, tri, ltm, eio, kio, jio, xs) = (
        g[n] for n in ("ident", "ident16", "ones16", "w1s", "w2s", "x2", "xhl", "xhT",
                       "lg", "tri", "ltm", "eio", "kio", "jio", "xs"))
    b2s, pid, w1stage, w2stage = (g[n] for n in ("b2s", "pid", "w1stage", "w2stage"))
    x, Wo_b, rpb, rel, Ws, bs, W1, b1, W2, b2 = (
        g[n] for n in ("x", "Wo_b", "rpb", "rel", "Ws", "bs", "W1", "b1", "W2", "b2"))
    mats = [g["Wq"], g["Wk"], g["Wv"], g["Wo_w"]]
    VB = 4
    XI = 2
    HOT_E, WATT_E = NE - 6, NE - 2
    SB = 3
    with ExitStack() as ctx:
        def sb(name, shape, dt):
            return ctx.enter_context(nc.sbuf_tensor(name, shape, dt))

        def pb(name, cols, dt=F32):
            return ctx.enter_context(nc.psum_tensor(name, [128, cols], dt))

        def sem(name):
            return ctx.enter_context(nc.semaphore(name))

        xin = sb("xin", [CH, XI, 2, IMG * IMG], F32)
        xn = sb("xn", [128, C], F32)
        xnT = sb("xnT", [CH, 2, 2, T], F32)
        q = sb("q", [128, 2, 2, T], F32)
        ka = sb("ka", [128, 2, 2, HA, L], F32)
        kc = sb("kc", [RC, 2, 2, HC, L], F32)
        v2 = sb("v2", [128, VB, 2, 2, NP, 2, VW], F16)
        sc = sb("sc", [128, SB, NH * L], F32)
        pT = sb("pT", [128, 2, 2, NP, T], F16)
        on = sb("on", [128, C], F32)
        oT = sb("oT", [CH + 1, 2, T], F32)
        xhf = sb("xhf", [128, C], F32)
        bias = sb("bias", [128, NH * L], F32)
        wT = sb("wT", [CH, 2, 3 * C], F32)
        woT = sb("woT", [CH + 1, 2, C], F32)
        ws16 = sb("ws16", [128, 4, NE], F16)
        mask = sb("mask", [128, HA], F32)
        tab16 = sb("tab16", [TH, 2, 2, NH], F16)
        rowid = sb("rowid", [TH, 2], F32)
        stat = sb("stat", [128, 2, 2, 6], F32)
        mv = sb("mv", [128, 2, 2, 2], F32)
        rstd = sb("rstd", [128, 2, 2], F32)
        minus_half = sb("minus_half", [128, 1], F32)
        mx = sb("mx", [128, 2, NH], F32)
        rden = sb("rden", [128, NH], F32)
        zeros = xhT[:, NT - 1, :, :].rearrange("p b n -> p (b n)")[:, 0:2 * C]
        HL = L // 2
        idx = [xhl[:, :, :].rearrange("p t c -> p (t c)")[0:TH, 0:2 * HL * L].bitcast(I32),
            x2[:, :, :].rearrange("p t c -> p (t c)")[0:TH, NT * C - HL * L:NT * C].bitcast(I32)]
        room = xhT[:, :, :, :].rearrange("p t b n -> p (t b n)").bitcast(F32)
        tab = room[0:NH, 0:2 * TH]
        wsr = room[:, 256:256 + 3 * NE].rearrange("p (b e) -> p b e", b=3)
        b2stage = room[0:2 * ER, 512:512 + C]
        b1stage = room[0:NE, 1024:1024 + FF]
        B1_TILE = 8
        b1hl = xhT[0:NE, B1_TILE:, :, :].rearrange("p t b n -> p (t b n)")[:, 0:2 * FF].rearrange(
            "p (a f) -> p a f", a=2)
        w2flat = w2s[:, :, :, :, :].rearrange("p e a f c -> p (e a f c)")
        per_e = 2 * NF * C
        hot = w2flat[0:TH, HOT_E * per_e:HOT_E * per_e + 2 * L * L].rearrange("p (k l m) -> p k l m", k=2, l=L)
        watt = w2flat[0:CH, WATT_E * per_e:WATT_E * per_e + 4 * 2 * C * 2].bitcast(F32).rearrange(
            "p (m r c) -> p m r c", m=4, r=2)

        p_x = pb("p_x", 512)
        p_n = pb("p_n", 512)
        p_qk = pb("p_qk", 512)
        p_v = pb("p_v", 512)
        p_s = pb("p_s", 1024)
        p_t = [pb("p_t0", 512), pb("p_t1", 512)]

        x_loaded = [sem(f"x_loaded{i}") for i in range(XI)]
        watt_loaded = sem("watt_loaded")
        idx_loaded = [sem("idx_loaded0"), sem("idx_loaded1")]
        tab_mm = sem("tab_mm")
        small_loaded = sem("small_loaded")
        tab_loaded = sem("tab_loaded")
        w1_loaded = sem("w1_loaded")
        w2_loaded = sem("w2_loaded")
        xs_zeroed = sem("xs_zeroed")
        consts0 = sem("consts0")
        consts = sem("consts")
        dve_consts = sem("dve_consts")
        tails_ready = sem("tails_ready")
        wt_mm = sem("wt_mm")
        wt_kept = sem("wt_kept")
        small_hi = sem("small_hi")
        small_lo = sem("small_lo")
        hot_ready = sem("hot_ready")
        bias_mm = sem("bias_mm")
        bias_hi = sem("bias_hi")
        bias_ready = sem("bias_ready")
        w1_scaled = sem("w1_scaled")
        w2_scaled = sem("w2_scaled")
        w1_hi = sem("w1_hi")
        w1_low0 = sem("w1_low0")
        w1_zeroed = sem("w1_zeroed")
        b1_stored = sem("b1_stored")
        w1_lo = sem("w1_lo")
        w2_hi = sem("w2_hi")
        w2_lo = sem("w2_lo")
        xT_mm = sem("xT_mm")
        x_kept = sem("x_kept")
        stat1 = sem("stat1")
        mv1 = sem("mv1")
        rstd1a = sem("rstd1a")
        rstd1 = sem("rstd1")
        xn_ready = sem("xn_ready")
        xnT_mm = sem("xnT_mm")
        xnT_ready = sem("xnT_ready")
        qk_mm = sem("qk_mm")
        v_mm = sem("v_mm")
        q_kept = sem("q_kept")
        kbd_ready = sem("kbd_ready")
        v_hi = sem("v_hi")
        v_lo = sem("v_lo")
        s_mm = [sem("s_mm0"), sem("s_mm1")]
        s_biased = [sem("s_biased0"), sem("s_biased1")]
        s_max = sem("s_max")
        s_sub = sem("s_sub")
        p_ready = sem("p_ready")
        pT_mm = [sem("pT_mm0"), sem("pT_mm1")]
        pT_hi = [sem("pT_hi0"), sem("pT_hi1")]
        pT_lo = [sem("pT_lo0"), sem("pT_lo1")]
        pv_mm = sem("pv_mm")
        rden_ready = sem("rden_ready")
        o_norm = sem("o_norm")
        oT_mm = sem("oT_mm")
        oT_ready = sem("oT_ready")
        wo_mm = sem("wo_mm")
        x2_ready = sem("x2_ready")
        stat2 = sem("stat2")
        mv2 = sem("mv2")
        rstd2a = sem("rstd2a")
        rstd2 = sem("rstd2")
        xh_ready = sem("xh_ready")
        xh_hi = sem("xh_hi")
        xh_lo = sem("xh_lo")
        xhT_mm = sem("xhT_mm")
        xhT_ready = sem("xhT_ready")
        lg_mm = sem("lg_mm")
        lg_kept = sem("lg_kept")

        PE_PROGRAM = (("x_to_tokens", 0), ("project_values", 1), ("weights_to_keys_1", 4),
                      ("output_projection", 5), ("xh_to_channels", 7), ("project", 1), ("scores_0", 2),
                      ("attend", 4), ("logits", 7), ("normed_to_channels", 0), ("scores_1", 1),
                      ("weights_to_keys_0", 3), ("attended_to_channels", 4))
        ACT_PROGRAM = (("keep_x", 0), ("keep_attendedT", 5), ("v_high", 1), ("weightsT_hi_1", 4), ("split", 0),
                       ("keep_queries", 1), ("keep_xhT", 7), ("exponentials", 3), ("xh_high", 6), ("split", 0),
                       ("keep_normedT", 0), ("weightsT_hi_0", 3))
        DVE_PROGRAM = (("statistics_1", 0), ("weightsT_lo_0", 4), ("v_low", 1), ("weightsT_lo_1", 4),
                       ("residual", 5), ("xh", 6), ("normed", 0), ("head_blocks", 1), ("add_bias_0", 2),
                       ("normalise", 4), ("keep_logits", 7), ("add_bias_1", 1), ("row_max", 2))
        POOL_PROGRAM = (("rstd_1", 0), ("softmax_shift", 3), ("split", 0), ("rstd_2", 5), ("xh_low", 6),
                        ("split", 0))
        STEPS = NT + 1 + max(lag for program in (PE_PROGRAM, ACT_PROGRAM, DVE_PROGRAM, POOL_PROGRAM)
                             for _, lag in program)
        FIRST_SCORES = 1
        QUARTERS = 4 * (NE - 1)
        FIRST_SPLIT = 2
        STEPS = max(STEPS, FIRST_SPLIT + QUARTERS // 2)
        KQ = L // 4
        BIAS_BANKS = (p_s[:, 0:512], p_s[:, 512:1024], p_t[0][:, :], p_t[1][:, :])
        BIAS_BY_KEY = bias[:, :].rearrange("p (h m) -> p m h", h=NH)
        SCORE_COLS = (slice(0, HA * L), slice(HA * L, NH * L))
        WINDOW_HEADS = [(w, h) for w in range(2) for h in range(2)]

        def values(w, h):
            return p_v[w * L:(w + 1) * L, 0:C].rearrange("p (n h d) -> p n h d", n=NP, h=2)[:, :, h, :]

        def stages(step, program, functions, split):
            by_name = {f.__name__: f for f in functions}
            quarter = 2 * (step - FIRST_SPLIT)
            for name, lag in program:
                if name == "split":
                    if 0 <= quarter < QUARTERS:
                        split(quarter // 4, (0, 2, 1, 3)[quarter % 4])
                        quarter += 1
                elif 0 <= step - lag < NT:
                    by_name[name](step - lag)

        def ahead(stage, t, other):
            names = [name for name, _ in PE_PROGRAM]
            lags = dict(PE_PROGRAM)
            n = t + lags[stage] - lags[other] + (names.index(other) < names.index(stage))
            return max(0, min(n, NT))

        block = ctx.enter_context(nc.Block())

        @block.sync
        def _(sp):
            def packed(stage, weights, loaded):
                sp.dma_start(stage[:, HI, :], weights[0:128]).then_inc(loaded, 16)
                for half in range(2):
                    sp.dma_start(stage[half * LC:(half + 1) * LC, MIX, :], weights[128:C]).then_inc(loaded, 16)

            def image(b):
                if b >= XI:
                    sp.wait_ge(xT_mm, TPI * (b - XI + 1))
                sp.dma_start(xin[:, b % XI, :, :],
                             x[b].rearrange("(k c) i j -> c k (i j)", k=2)).then_inc(x_loaded[b % XI], 16)

            image(0)
            for m in range(4):
                sp.dma_start(watt[:, m, :, :],
                             mats[m].rearrange("(r o) c -> o r c", r=2)).then_inc(watt_loaded, 16)
            sp.dma_start(woT[CH:CH + 1, 0, :], Wo_b.unsqueeze(0)).then_inc(small_loaded, 16)
            sp.wait_ge(dve_consts, 3)
            sp.dma_start(tab[:, 0:TBL], rpb).then_inc(tab_loaded, 16)
            packed(wsr, Ws, small_loaded)
            sp.dma_start(wsr[0:LC, BIAS, :], Ws[128:C]).then_inc(small_loaded, 16)
            for place in (LC, LC + 32):
                sp.dma_start(wsr[place:place + 1, BIAS, :], bs.unsqueeze(0)).then_inc(small_loaded, 16)
            sp.dma_start(b1stage, b1).then_inc(small_loaded, 16)
            for half in range(2):
                sp.dma_start(b2stage[half * ER:half * ER + NE, :], b2).then_inc(small_loaded, 16)
            image(1)
            for e in range(NE):
                if e >= 1:
                    sp.wait_ge(w1_hi, 2 * e)
                    sp.wait_ge(w1_lo, 2 * e)
                packed(w1stage, W1[e], w1_loaded)
                if e >= 1:
                    sp.wait_ge(w2_hi, 2 * e)
                    sp.wait_ge(w2_lo, 2 * e)
                sp.dma_start(w2stage[:, :, :], W2[e].rearrange("(f p) c -> p f c", p=128)).then_inc(w2_loaded, 16)
                if e + 2 < B:
                    image(e + 2)
                if e == 0:
                    sp.wait_ge(small_lo, 6)
                    sp.wait_ge(w1_zeroed, 1)
                for i in range(3 * e, min(3 * e + 3, NE)):
                    for half in range(2):
                        sp.dma_start(w1s[LC + 32 * half:LC + 32 * half + 1, i, BIAS, :], b1hl[i:i + 1, 1 - half, :]
                                     ).then_inc(b1_stored, 16)
            sp.wait_ge(xs_zeroed, 16)
            sp.wait_ge(b1_stored, 16 * 2 * NE)
            sp.wait_ge(w1_loaded, 16 * 3 * NE)
            sp.wait_ge(w2_loaded, 16 * NE)

        @block.gpsimd
        def _(pool):
            pool.memset(ident[:, :], 0.0).then_inc(consts0, 1)
            pool.memset(ident16[:, :], 0.0).then_inc(consts0, 1)
            pool.memset(tri[:, :], 1.0).then_inc(consts0, 1)
            pool.memset(mask[:, :], 1.0).then_inc(consts0, 1)
            pool.memset(ltm[:, :, :], 1.0).then_inc(consts0, 1)
            pool.memset(zeros, 0.0).then_inc(consts0, 1)
            pool.memset(minus_half[:, :], -0.5).then_inc(consts0, 1)
            pool.wait_ge(consts0, 7)
            for m in (ident, ident16):
                pool.affine_select(out=m[:, :], in_=m[:, :], compare_op=ALU.not_equal, fill=1.0, base=0,
                                   pattern=[[-1, 128]], channel_multiplier=1).then_inc(consts0, 1)
            pool.affine_select(out=tri[:, :], in_=tri[:, :], compare_op=ALU.is_gt, fill=0.0, base=0,
                               pattern=[[1, 128]], channel_multiplier=-1).then_inc(consts0, 1)
            pool.affine_select(out=ltm[:, :, :], in_=ltm[:, :, :], compare_op=ALU.is_gt, fill=0.0, base=0,
                               pattern=[[1, NE], [-1, NE]], channel_multiplier=0).then_inc(consts0, 1)
            pool.affine_select(out=mask[:, :], in_=mask[:, :], compare_op=ALU.is_ge, fill=0.0, base=0,
                               pattern=[[-HD, HA]], channel_multiplier=1).then_inc(consts0, 1)
            pool.wait_ge(consts0, 12)
            pool.affine_select(out=mask[:, :], in_=mask[:, :], compare_op=ALU.is_ge, fill=0.0, base=HD - 1,
                               pattern=[[HD, HA]], channel_multiplier=-1).then_inc(consts0, 1)
            pool.iota(rowid[:, :], [[TH, 2]], base=0, channel_multiplier=1,
                      allow_small_or_imprecise_dtypes=True).then_inc(consts0, 1)
            pool.iota(eio[:, :], [[1, NE]], base=0, channel_multiplier=0,
                      allow_small_or_imprecise_dtypes=True).then_inc(consts0, 1)
            pool.iota(kio[:, :], [[T, NT]], base=0, channel_multiplier=0,
                      allow_small_or_imprecise_dtypes=True).then_inc(consts0, 1)
            pool.iota(jio[:, :], [[1, NR]], base=0, channel_multiplier=0,
                      allow_small_or_imprecise_dtypes=True).then_inc(consts0, 1)
            pool.iota(pid[:, :], [[0, 1]], base=0, channel_multiplier=1,
                      allow_small_or_imprecise_dtypes=True).then_inc(consts0, 1)
            pool.wait_ge(consts0, 18)
            pool.memset(ones16[:, :], 1.0).then_inc(consts, 1)

            def softmax_shift(t):
                pool.wait_ge(s_max, t + 1)
                s = sc[:, t % SB, :].rearrange("p (h m) -> p h m", h=NH)
                pool.tensor_tensor(s, s, mx[:, t % 2, :].unsqueeze(2).to_broadcast([128, NH, L]),
                                   ALU.subtract).then_inc(s_sub, 1)

            def inverse_deviation(t, ln, eps, ready, shifted, done):
                r = rstd[:, ln, t % 2:t % 2 + 1]
                pool.wait_ge(ready, t + 1)
                pool.tensor_scalar(r, mv[:, ln, t % 2, 1:2], eps, None, ALU.add).then_inc(shifted, 1)
                pool.wait_ge(shifted, t + 1)
                pool.tensor_tensor(r, r, minus_half[:, :], ALU.pow).then_inc(done, 1)

            def rstd_1(t):
                if t >= 2:
                    pool.wait_ge(xn_ready, t - 1)
                inverse_deviation(t, 0, 1e-6, mv1, rstd1a, rstd1)

            def rstd_2(t):
                if t >= 2:
                    pool.wait_ge(xh_ready, t - 1)
                inverse_deviation(t, 1, 1e-5, mv2, rstd2a, rstd2)

            def xh_low(t):
                pool.wait_ge(xh_hi, t + 1)
                pool.tensor_tensor(xhl[:, t, C:2 * C], xhf[:, :], xhl[:, t, 0:C], ALU.subtract
                                   ).then_inc(xh_lo, 1)

            def split_low(e, k):
                if k < 2:
                    pool.wait_ge(w1_hi, 2 * e + k + 1)
                    c = slice(k * FF // 2, (k + 1) * FF // 2)
                    pool.tensor_tensor(w1s[:, e, LO, c], w1stage[:, HI, c], w1s[:, e, HI, c], ALU.subtract
                                       ).then_inc(w1_low0, 1)
                    pool.wait_ge(w1_low0, 2 * e + k + 1)
                    mix = w1s[LC:128, e, MIX, c]
                    pool.tensor_tensor(mix, w1stage[LC:128, MIX, c], mix, ALU.subtract).then_inc(w1_lo, 1)
                    pool.wait_ge(w1_lo, 2 * e + k + 1)
                else:
                    r = slice((k - 2) * NF // 2, (k - 1) * NF // 2)
                    pool.wait_ge(w2_hi, 2 * e + k - 1)
                    pool.tensor_tensor(w2s[:, e, 1, r, :], w2stage[:, r, :], w2s[:, e, 0, r, :], ALU.subtract
                                       ).then_inc(w2_lo, 1)

            for step in range(STEPS):
                if step == 4:
                    pool.dma_start(xs.rearrange("(j p) c -> p j c", p=T),
                                   zeros.unsqueeze(1).to_broadcast([128, NR, 2 * C])).then_inc(xs_zeroed, 16)
                if step == 1:
                    pool.wait_ge(rstd1, 1)
                    pool.memset(w1s[LC:128, :, BIAS, :], 0.0).then_inc(w1_zeroed, 1)
                    pool.wait_ge(w1_zeroed, 1)
                stages(step, POOL_PROGRAM, (rstd_1, softmax_shift, rstd_2, xh_low), split_low)

        @block.scalar
        def _(act):
            for i in range(2):
                act.dma_start(idx[i], rel.rearrange("l m -> (l m)")[i * HL * L:(i + 1) * HL * L].unsqueeze(0)
                              .to_broadcast([TH, HL * L])).then_inc(idx_loaded[i], 16)

            def keep_weights():
                for m, bank in enumerate((p_qk, p_v, p_t[0], p_t[1])):
                    act.wait_ge(wt_mm, m + 1)
                    act.activation(wT[:, :, m * C:(m + 1) * C] if m < 3 else woT[0:CH, :, :],
                                   bank[0:CH, 0:2 * C].rearrange("p (k o) -> p k o", k=2), ACT.Copy,
                                   scale=SV if m == 2 else 1.0).then_inc(wt_kept, 1)

            def small_weights():
                act.wait_ge(tab_mm, 1)
                act.activation(tab16[:, :, 0, :], p_s[0:TH, 0:2 * NH].rearrange("p (k h) -> p k h", k=2), ACT.Copy
                               ).then_inc(small_hi, 1)
                act.wait_ge(small_loaded, 16 * 10)
                act.activation(ws16[:, HI:BIAS + 1, :], wsr[:, :, :], ACT.Copy, scale=SF).then_inc(small_hi, 1)
                act.activation(b2s[:, :], b2stage[:, :], ACT.Copy, scale=SF).then_inc(small_hi, 1)
                act.activation(b1hl[:, 0, :], b1stage, ACT.Copy, scale=SF).then_inc(small_hi, 1)

            def keep_bias():
                act.wait_ge(bias_mm, 1)
                for i, bank in enumerate(BIAS_BANKS):
                    for w in range(2):
                        act.activation(BIAS_BY_KEY[w * L:(w + 1) * L, i * KQ:(i + 1) * KQ, :],
                                       bank[0:L, 0:KQ * 2 * NH].rearrange("p (m a h) -> p m a h", a=2, h=NH)[:, :, 0, :],
                                       ACT.Copy).then_inc(bias_hi, 1)

            def keep_x(t):
                act.wait_ge(xT_mm, t + 1)
                act.activation(x2[:, t, :], p_x[:, 0:C], ACT.Copy).then_inc(x_kept, 1)

            def keep_normedT(t):
                act.wait_ge(xnT_mm, t + 1)
                if t >= 2:
                    act.wait_ge(qk_mm, t - 1)
                    act.wait_ge(v_mm, t - 1)
                act.activation(xnT[:, t % 2, :, :], p_n[0:CH, 0:2 * T].rearrange("p (k n) -> p k n", k=2),
                               ACT.Copy).then_inc(xnT_ready, 1)

            def keep_queries(t):
                act.wait_ge(qk_mm, t + 1)
                if t >= 2:
                    act.wait_ge(s_mm[0], t - 1)
                    act.wait_ge(s_mm[1], t - 1)
                act.activation(q[:, t % 2, :, :], p_qk[:, 0:2 * T].rearrange("p (c n) -> p c n", c=2), ACT.Copy
                               ).then_inc(q_kept, 1)
                if t == 0:
                    keep_bias()

            def v_high(t):
                act.wait_ge(v_mm, t + 1)
                if t >= VB:
                    act.wait_ge(pv_mm, t - VB + 1)
                for w, h in WINDOW_HEADS:
                    act.activation(v2[h * L:(h + 1) * L, t % VB, 0, w, :, h, 0:HD], values(w, h), ACT.Copy
                                   ).then_inc(v_hi, 1)

            def exponentials(t):
                act.wait_ge(s_sub, t + 1)
                act.activation(sc[:, t % SB, :], sc[:, t % SB, :], ACT.Exp).then_inc(p_ready, 1)

            def weightsT_hi(t, h):
                act.wait_ge(pT_mm[h], t + 1)
                if t >= 2:
                    act.wait_ge(pv_mm, t - 1)
                act.activation(pT[:, t % 2, 0, 3 * h:3 * h + 3, :],
                               p_t[h][:, 0:3 * T].rearrange("p (n q) -> p n q", n=3), ACT.Copy).then_inc(pT_hi[h], 1)

            def weightsT_hi_0(t):
                weightsT_hi(t, 0)

            def weightsT_hi_1(t):
                weightsT_hi(t, 1)

            def keep_attendedT(t):
                act.wait_ge(oT_mm, t + 1)
                if t >= 1:
                    act.wait_ge(wo_mm, t)
                act.activation(oT[0:CH, :, :], p_n[0:CH, 0:2 * T].rearrange("p (k n) -> p k n", k=2),
                               ACT.Copy).then_inc(oT_ready, 1)

            def xh_high(t):
                act.wait_ge(xh_ready, t + 1)
                act.activation(xhl[:, t, 0:C], xhf[:, :], ACT.Copy).then_inc(xh_hi, 1)

            def keep_xhT(t):
                act.wait_ge(xhT_mm, t + 1)
                if t == B1_TILE:
                    act.wait_ge(b1_stored, 16 * 2 * NE)
                if t == NT - 1:
                    act.wait_ge(xs_zeroed, 16)
                act.activation(xhT[:, t, :, :], p_n[:, 0:2 * T].bitcast(F16).rearrange("p (b n) -> p b n", b=4),
                               ACT.Copy).then_inc(xhT_ready, 1)

            def split_high(e, k):
                if k < 2:
                    if k == 0:
                        act.wait_ge(w1_loaded, 16 * 3 * (e + 1))
                    c = slice(k * FF // 2, (k + 1) * FF // 2)
                    act.activation(w1stage[:, :, c], w1stage[:, :, c], ACT.Copy, scale=SF).then_inc(w1_scaled, 1)
                    act.wait_ge(w1_scaled, 2 * e + k + 1)
                    act.activation(w1s[0:LC, e, BIAS, c], w1stage[0:LC, MIX, c], ACT.Copy)
                    act.activation(w1s[:, e, HI:MIX + 1, c], w1stage[:, :, c], ACT.Copy).then_inc(w1_hi, 1)
                else:
                    if k == 2:
                        act.wait_ge(w2_loaded, 16 * (e + 1))
                        if e >= HOT_E:
                            act.wait_ge(bias_mm, 1)
                            act.wait_ge(wt_mm, 4)
                    r = slice((k - 2) * NF // 2, (k - 1) * NF // 2)
                    act.activation(w2stage[:, r, :], w2stage[:, r, :], ACT.Copy, scale=SF).then_inc(w2_scaled, 1)
                    act.wait_ge(w2_scaled, 2 * e + k - 1)
                    act.activation(w2s[:, e, 0, r, :], w2stage[:, r, :], ACT.Copy).then_inc(w2_hi, 1)

            for step in range(STEPS):
                if step == 1:
                    keep_weights()
                    small_weights()
                stages(step, ACT_PROGRAM, (keep_x, keep_normedT, keep_queries, v_high, exponentials, weightsT_hi_0,
                                           weightsT_hi_1, keep_attendedT, xh_high, keep_xhT), split_high)

        @block.vector
        def _(dve):
            dve.memset(tab[:, :], 0.0).then_inc(dve_consts, 1)
            dve.memset(wsr[LC:128, BIAS, :], 0.0).then_inc(dve_consts, 1)
            dve.memset(b2stage[:, :], 0.0).then_inc(dve_consts, 1)
            dve.memset(v2[:, :, 0, :, :, :, :], 0.0).then_inc(dve_consts, 1)

            def more_constants():
                dve.memset(v2[:, :, 1, :, :, :, :], 0.0).then_inc(dve_consts, 1)
                dve.memset(oT[CH:CH + 1, 0, :], 1.0).then_inc(dve_consts, 1)
                dve.wait_ge(dve_consts, 6)
                for h in range(2):
                    for w in range(2):
                        dve.memset(v2[64 * h:64 * h + 64, :, 0, w, :, h, HD], SV).then_inc(dve_consts, 1)

            def tails():
                dve.wait_ge(hot_ready, 4)
                dve.memset(xhl[:, :, 2 * C:XW], 0.0).then_inc(tails_ready, 1)
                dve.wait_ge(tails_ready, 1)
                for one in (0, 32):
                    dve.memset(xhl[:, :, 2 * C + one], 1.0).then_inc(tails_ready, 1)

            def small_weights():
                dve.wait_ge(small_hi, 1)
                dve.tensor_tensor(tab16[:, :, 1, :], p_s[0:TH, 0:2 * NH].rearrange("p (k h) -> p k h", k=2),
                                  tab16[:, :, 0, :], ALU.subtract).then_inc(small_lo, 1)
                dve.wait_ge(small_hi, 4)
                dve.wait_ge(consts, 1)
                for lo, src, hi in (
                        (ws16[:, LO, :], wsr[:, HI, :], ws16[:, HI, :]),
                        (ws16[LC:128, MIX, :], wsr[LC:128, MIX, :], ws16[LC:128, MIX, :]),
                        (ws16[LC:LC + 1, BIAS, :], wsr[LC:LC + 1, BIAS, :], ws16[LC:LC + 1, BIAS, :]),
                        (b2s[ER:2 * ER, :], b2stage[ER:2 * ER, :], b2s[ER:2 * ER, :]),
                        (b1hl[:, 1, :], b1stage, b1hl[:, 0, :])):
                    dve.scalar_tensor_tensor(out=lo, in0=src, scalar=SF, in1=hi, op0=ALU.mult,
                                             op1=ALU.subtract).then_inc(small_lo, 1)
                dve.tensor_scalar(pid[ER:2 * ER, :], pid[ER:2 * ER, :], float(-ER), None, ALU.add)

            def one_hots():
                dve.wait_ge(consts, 1)
                for i in range(2):
                    dve.wait_ge(idx_loaded[i], 16)
                    for k in range(2):
                        dve.tensor_scalar(hot[:, k, i * HL:(i + 1) * HL, :].rearrange("p l m -> p (l m)"), idx[i],
                                          rowid[:, k:k + 1], None, ALU.is_equal).then_inc(hot_ready, 1)

            def bias_low():
                for i, bank in enumerate(BIAS_BANKS):
                    dve.wait_ge(bias_hi, 2 * (i + 1))
                    for w in range(2):
                        part = BIAS_BY_KEY[w * L:(w + 1) * L, i * KQ:(i + 1) * KQ, :]
                        dve.tensor_tensor(part, bank[0:L, 0:KQ * 2 * NH].rearrange("p (m a h) -> p m a h", a=2, h=NH)
                                          [:, :, 1, :], part, ALU.add).then_inc(bias_ready, 1)

            def normed(t):
                dve.wait_ge(rstd1, t + 1)
                if t >= 1:
                    dve.wait_ge(xnT_mm, t)
                dve.tensor_scalar(xn[:, :], x2[:, t, :], mv[:, 0, t % 2, 0:1], rstd[:, 0, t % 2:t % 2 + 1],
                                  ALU.subtract, ALU.mult).then_inc(xn_ready, 1)

            def statistics_1(t):
                dve.wait_ge(x_kept, t + 1)
                dve.bn_stats(stat[:, 0, t % 2, :], x2[:, t, :]).then_inc(stat1, 1)
                dve.wait_ge(stat1, t + 1)
                dve.bn_aggr(mv[:, 0, t % 2, :], stat[:, 0, t % 2, :]).then_inc(mv1, 1)

            def head_blocks(t):
                dve.wait_ge(qk_mm, t + 1)
                dve.wait_ge(q_kept, t + 1)
                if t >= 2:
                    dve.wait_ge(s_mm[0], t - 1)
                    dve.wait_ge(s_mm[1], t - 1)
                for dst, rows, heads, chunk in ((ka, 128, HA, 2), (kc, RC, HC, 3)):
                    keys = p_qk[0:rows, chunk * T:(chunk + 1) * T].rearrange("p (w m) -> p w m", w=2)
                    shape = [rows, 2, heads, L]
                    blk = dve.tensor_tensor(
                        dst[:, t % 2, :, :, :], keys.unsqueeze(2).to_broadcast(shape),
                        mask[0:rows, 0:heads].unsqueeze(1).unsqueeze(3).to_broadcast(shape), ALU.mult)
                blk.then_inc(kbd_ready, 1)

            def v_low(t):
                dve.wait_ge(v_hi, 4 * t + 4)
                for w, h in WINDOW_HEADS:
                    hi, lo = (v2[h * L:(h + 1) * L, t % VB, a, w, :, h, 0:HD] for a in range(2))
                    dve.tensor_tensor(lo, values(w, h), hi, ALU.subtract).then_inc(v_lo, 1)

            def add_bias(t, h):
                cols = SCORE_COLS[h]
                if t == 0 and h == FIRST_SCORES:
                    bias_low()
                    dve.wait_ge(bias_ready, 8)
                dve.wait_ge(s_mm[h], t + 1)
                if t >= SB:
                    dve.wait_ge(pT_mm[0], t - SB + 1)
                    dve.wait_ge(pT_mm[1], t - SB + 1)
                dve.scalar_tensor_tensor(out=sc[:, t % SB, cols], in0=p_s[:, cols], scalar=S_SCALE,
                                         in1=bias[:, cols], op0=ALU.mult, op1=ALU.add).then_inc(s_biased[h], 1)

            def add_bias_0(t):
                add_bias(t, 0)

            def add_bias_1(t):
                add_bias(t, 1)

            def row_max(t):
                dve.wait_ge(s_biased[0], t + 1)
                dve.wait_ge(s_biased[1], t + 1)
                if t >= 2:
                    dve.wait_ge(s_sub, t - 1)
                dve.tensor_reduce(mx[:, t % 2, :], sc[:, t % SB, :].rearrange("p (h m) -> p h m", h=NH), AX, ALU.max
                                  ).then_inc(s_max, 1)

            def weightsT_lo(t, h):
                dve.wait_ge(pT_hi[h], t + 1)
                if t >= 2:
                    dve.wait_ge(pv_mm, t - 1)
                dve.tensor_tensor(pT[:, t % 2, 1, 3 * h:3 * h + 3, :],
                                  p_t[h][:, 0:3 * T].rearrange("p (n q) -> p n q", n=3),
                                  pT[:, t % 2, 0, 3 * h:3 * h + 3, :], ALU.subtract).then_inc(pT_lo[h], 1)

            def weightsT_lo_0(t):
                weightsT_lo(t, 0)

            def weightsT_lo_1(t):
                weightsT_lo(t, 1)

            def normalise(t):
                dve.wait_ge(pv_mm, t + 1)
                heads = p_v[:, 0:NH * VW].rearrange("p (h d) -> p h d", h=NH)
                if t >= 1:
                    dve.wait_ge(o_norm, t)
                dve.reciprocal(rden[:, :], heads[:, :, HD]).then_inc(rden_ready, 1)
                dve.wait_ge(rden_ready, t + 1)
                if t >= 1:
                    dve.wait_ge(oT_mm, t)
                dve.tensor_tensor(on[:, :].rearrange("p (h d) -> p h d", h=NH), heads[:, :, 0:HD],
                                  rden[:, :].unsqueeze(2).to_broadcast([128, NH, HD]), ALU.mult).then_inc(o_norm, 1)

            def residual(t):
                dve.wait_ge(wo_mm, t + 1)
                dve.scalar_tensor_tensor(out=x2[:, t, :], in0=p_x[:, 0:C], scalar=1.0, in1=x2[:, t, :],
                                         op0=ALU.mult, op1=ALU.add).then_inc(x2_ready, 1)
                dve.wait_ge(x2_ready, t + 1)
                dve.bn_stats(stat[:, 1, t % 2, :], x2[:, t, :]).then_inc(stat2, 1)
                dve.wait_ge(stat2, t + 1)
                dve.bn_aggr(mv[:, 1, t % 2, :], stat[:, 1, t % 2, :]).then_inc(mv2, 1)

            def xh(t):
                dve.wait_ge(rstd2, t + 1)
                if t >= 1:
                    dve.wait_ge(xh_hi, t)
                    dve.wait_ge(xh_lo, t)
                dve.tensor_scalar(xhf[:, :], x2[:, t, :], mv[:, 1, t % 2, 0:1], rstd[:, 1, t % 2:t % 2 + 1],
                                  ALU.subtract, ALU.mult).then_inc(xh_ready, 1)

            def keep_logits(t):
                dve.wait_ge(lg_mm, t + 1)
                dve.tensor_scalar(lg[:, t, :], p_x[:, 0:NE], 1.0 / SF, None, ALU.mult).then_inc(lg_kept, 1)

            for step in range(STEPS):
                if step == 1:
                    more_constants()
                    one_hots()
                    small_weights()
                    tails()
                stages(step, DVE_PROGRAM, (statistics_1, normed, head_blocks, v_low, add_bias_0, add_bias_1, row_max,
                                           weightsT_lo_0, weightsT_lo_1, normalise, residual, xh, keep_logits), None)

        @block.tensor
        def _(pe):
            pe.wait_ge(consts, 1)

            def transpose_weights():
                pe.wait_ge(watt_loaded, 16 * 4)
                for m, bank in enumerate((p_qk, p_v, p_t[0], p_t[1])):
                    for k in range(2):
                        for r in range(2):
                            mm = pe.transpose(bank[0:CH, k * C + r * CH:k * C + (r + 1) * CH],
                                              watt[:, m, r, k * CH:(k + 1) * CH], ident[0:CH, 0:CH])
                    mm.then_inc(wt_mm, 1)
                pe.wait_ge(tab_loaded, 16)
                for k in range(2):
                    mm = pe.transpose(p_s[0:TH, k * NH:(k + 1) * NH], tab[:, k * TH:(k + 1) * TH],
                                      ident[0:NH, 0:NH])
                mm.then_inc(tab_mm, 1)

            def position_bias():
                pe.wait_ge(hot_ready, 4)
                pe.wait_ge(small_lo, 1)
                pe.wait_ge(wt_kept, 4)
                for m in range(L):
                    col = (m % KQ) * 2 * NH
                    for k in range(2):
                        mm = pe.matmul(BIAS_BANKS[m // KQ][0:L, col:col + 2 * NH], hot[:, k, :, m],
                                       tab16[:, k, :, :].rearrange("p a h -> p (a h)"), start=(k == 0), stop=(k == 1))
                mm.then_inc(bias_mm, 1)

            def bank_read(stage, t, readers):
                for other, read, per_tile in readers:
                    n = ahead(stage, t, other)
                    if n >= 1:
                        pe.wait_ge(read, per_tile * n)

            def x_to_tokens(t):
                b = t // TPI
                pe.wait_ge(x_loaded[b % XI], 16 * (b // XI + 1))
                bank_read("x_to_tokens", t, P_X_READ)
                for k in range(2):
                    cols = xin[:, b % XI, k, (t % TPI) * T:(t % TPI + 1) * T]
                    mm = pe.transpose(p_x[:, k * CH:(k + 1) * CH], cols, ident[0:CH, 0:CH])
                mm.then_inc(xT_mm, 1)

            def normed_to_channels(t):
                pe.wait_ge(xn_ready, t + 1)
                bank_read("normed_to_channels", t, P_N_READ)
                for k in range(2):
                    mm = pe.transpose(to_windows(p_n[0:CH, k * T:(k + 1) * T]), xn[:, k * CH:(k + 1) * CH],
                                      ident[:, :])
                mm.then_inc(xnT_mm, 1)

            def project(t):
                pe.wait_ge(xnT_ready, t + 1)
                if t == 0:
                    pe.wait_ge(wt_kept, 4)
                if t >= 1:
                    pe.wait_ge(q_kept, t)
                    pe.wait_ge(kbd_ready, t)
                for c, row in enumerate((0, 128, C, C + 128)):
                    for k in range(2):
                        mm = pe.matmul(p_qk[:, c * T:(c + 1) * T], wT[:, k, row:row + 128], xnT[:, t % 2, k, :],
                                       start=(k == 0), stop=(k == 1))
                mm.then_inc(qk_mm, 1)
                if t == 0:
                    position_bias()

            def project_values(t):
                pe.wait_ge(xnT_ready, t + 1)
                if t == 0:
                    pe.wait_ge(wt_kept, 4)
                bank_read("project_values", t, P_V_READ)
                for k in range(2):
                    mm = pe.matmul(p_v[:, 0:C], xnT[:, t % 2, k, :], wT[:, k, 2 * C:3 * C],
                                   start=(k == 0), stop=(k == 1))
                mm.then_inc(v_mm, 1)

            def scores(t, h):
                pe.wait_ge(q_kept, t + 1)
                pe.wait_ge(kbd_ready, t + 1)
                if t == 0:
                    pe.wait_ge(bias_ready, 8)
                else:
                    pe.wait_ge(s_biased[h], t)
                rows, keys = ((128, ka), (RC, kc))[h]
                for w in range(2):
                    mm = pe.matmul(p_s[w * L:(w + 1) * L, SCORE_COLS[h]], q[0:rows, t % 2, h, w * L:(w + 1) * L],
                                   keys[:, t % 2, w, :, :], start=True, stop=True)
                mm.then_inc(s_mm[h], 1)

            def scores_0(t):
                scores(t, 0)

            def scores_1(t):
                scores(t, 1)

            def weights_to_keys(t, h):
                pe.wait_ge(p_ready, t + 1)
                if t >= 1:
                    pe.wait_ge(pT_lo[h], t)
                for n in range(3):
                    pair = 3 * h + n
                    mm = pe.transpose(p_t[h][:, n * T:(n + 1) * T],
                                      sc[:, t % SB, pair * 2 * L:(pair + 1) * 2 * L], ident[:, :])
                mm.then_inc(pT_mm[h], 1)

            def weights_to_keys_0(t):
                weights_to_keys(t, 0)

            def weights_to_keys_1(t):
                weights_to_keys(t, 1)

            def attend(t):
                pe.wait_ge(pT_lo[0], t + 1)
                pe.wait_ge(pT_lo[1], t + 1)
                pe.wait_ge(v_lo, 4 * t + 4)
                bank_read("attend", t, P_V_READ)
                for w in range(2):
                    for pair in range(NP):
                        for n, (a, b) in enumerate(PASSES):
                            mm = pe.matmul(p_v[w * L:(w + 1) * L, pair * 2 * VW:(pair + 1) * 2 * VW],
                                           pT[:, t % 2, a, pair, w * L:(w + 1) * L], v2[:, t % VB, b, w, pair, :, :],
                                           start=(n == 0), stop=(n == 2))
                mm.then_inc(pv_mm, 1)

            def attended_to_channels(t):
                pe.wait_ge(o_norm, t + 1)
                bank_read("attended_to_channels", t, P_N_READ)
                for k in range(2):
                    mm = pe.transpose(to_raster(p_n[0:CH, k * T:(k + 1) * T]), on[:, k * CH:(k + 1) * CH],
                                      ident[:, :])
                mm.then_inc(oT_mm, 1)

            def output_projection(t):
                pe.wait_ge(oT_ready, t + 1)
                bank_read("output_projection", t, P_X_READ)
                for k in range(2):
                    mm = pe.matmul(p_x[:, 0:C], oT[0:CH + 1 - k, k, :], woT[0:CH + 1 - k, k, :],
                                   start=(k == 0), stop=(k == 1))
                mm.then_inc(wo_mm, 1)

            def xh_to_channels(t):
                pe.wait_ge(xh_lo, t + 1)
                bank_read("xh_to_channels", t, P_N_READ)
                if t == 0:
                    pe.wait_ge(tails_ready, 3)
                bank = p_n[:, 0:2 * T].bitcast(F16).rearrange("p (b n) -> p b n", b=4)
                packed_transposes(pe, bank, xhl[:, t, :], ident16).then_inc(xhT_mm, 1)

            def logits(t):
                pe.wait_ge(xhT_ready, t + 1)
                bank_read("logits", t, P_X_READ)
                if t == 0:
                    pe.wait_ge(small_lo, 6)
                for n, (w, b, rows) in enumerate(PACKED):
                    mm = pe.matmul(p_x[:, 0:NE], xhT[0:rows, t, b, :], ws16[0:rows, w, :], start=(n == 0),
                                   stop=(n == len(PACKED) - 1))
                mm.then_inc(lg_mm, 1)

            P_X_READ = (("x_to_tokens", x_kept, 1), ("output_projection", x2_ready, 1), ("logits", lg_kept, 1))
            P_N_READ = (("normed_to_channels", xnT_ready, 1), ("attended_to_channels", oT_ready, 1),
                        ("xh_to_channels", xhT_ready, 1))
            P_V_READ = (("project_values", v_lo, 4), ("attend", o_norm, 1))

            for step in range(STEPS):
                if step == 1:
                    transpose_weights()
                stages(step, PE_PROGRAM, (x_to_tokens, normed_to_channels, project, project_values, scores_0, scores_1,
                                          weights_to_keys_0, weights_to_keys_1, attend, attended_to_channels,
                                          output_projection, xh_to_channels, logits), None)


def experts(nc, g):
    (ident, ident16, ones16, w1s, w2s,  x2, xhl, xhT, lg, tri, ltm, eio, kio, jio, pmax, omp, slot, etile, xs,
     ys, out) = (
        g[n] for n in ("ident", "ident16", "ones16", "w1s", "w2s", "x2", "xhl", "xhT",
                       "lg", "tri", "ltm", "eio", "kio", "jio", "pmax", "omp", "slot", "etile", "xs", "ys", "out"))
    b2s, pid, w1stage, w2stage = (g[n] for n in ("b2s", "pid", "w1stage", "w2stage"))
    HF = NF // 2
    YB, GB, FB = 4, 7, 4
    FIRST = NT // 2 + 1
    TILES = ([("common", t) for t in range(FIRST)] + [("routed", j) for j in range(NR)]
             + [("common", t) for t in range(FIRST, NT)])
    N = len(TILES)
    MIX_STEP = FIRST + NR + 3

    def common_at(t):
        return t if t < FIRST else t + NR

    def routed_at(j):
        return FIRST + j

    def next_routed(n):
        return TILES[n + 1][1] if n + 1 < N and TILES[n + 1][0] == "routed" else None

    def mixes(step):
        first = 3 * (step - MIX_STEP)
        if step < MIX_STEP or step > N:
            return range(0)
        return range(min(first, NT), NT if step == N else min(first + 3, NT))

    with ExitStack() as ctx:
        def sb(name, shape, dt):
            return ctx.enter_context(nc.sbuf_tensor(name, shape, dt))

        def pb(name):
            return ctx.enter_context(nc.psum_tensor(name, [128, 512], F32))

        def sem(name):
            return ctx.enter_context(nc.semaphore(name))

        ex = sb("ex", [128, NT, NE], F32)
        cand = sb("cand", [128, NT, NE], F32)
        oh = sb("oh", [128, NT, NE], F16)
        big = sb("big", [128, NE * NR], F32)
        r16 = sb("r16", [128, 4, NT], F32)
        cnt = sb("cnt", [128, 4, NE], F32)
        ejf = sb("ejf", [2 * ER, 2, NR], F32)
        hf = sb("hf", [128, 2, 2, HF * T], F32)
        hp = sb("hp", [128, 2, 2, NF, T], F16)
        w1d = sb("w1d", [128, 2, 4, FF], F16)
        w2d = sb("w2d", [128, 2, 2, NF, C], F16)
        ohe = sb("ohe", [2 * ER, NR], F16)
        ohd = sb("ohd", [2 * ER, 2, T], F16)
        ohc = sb("ohc", [2 * ER, T], F16)
        tok = sb("tok", [128, YB, XW], F16)
        tokT = sb("tokT", [128, 2, 4, T], F16)
        yo = sb("yo", [128, YB, C], F32)
        sel = sb("sel", [128, GB, C], F32)
        fin = sb("fin", [128, FB, C], F32)
        outc = sb("outc", [CH, 2, 2, IMG * IMG], F32)

        p_h = [[pb(f"p_h{i}{j}") for j in range(2)] for i in range(2)]
        p_y = [pb(f"p_y{i}") for i in range(2)]
        p_k = pb("p_k")
        p_f = [pb("p_f"), p_k]

        chain = sem("chain")
        ex_in = sem("ex_in")
        ex_out = sem("ex_out")
        oh_ready = sem("oh_ready")
        rank_mm = sem("rank_mm")
        slots_ready = sem("slots_ready")
        last_scaled = sem("last_scaled")
        last_hi = sem("last_hi")
        last_lo = sem("last_lo")
        consts = sem("f_consts")
        scattered = sem("scattered")
        tok_loaded = [sem(f"tok_loaded{i}") for i in range(YB)]
        tokT_mm = sem("tokT_mm")
        tokT_ready = sem("tokT_ready")
        w1_copied = sem("w1_copied")
        w2_copied = sem("w2_copied")
        h_mm = [sem("h_mm0"), sem("h_mm1")]
        h_act = [sem("h_act0"), sem("h_act1")]
        h_hi = [sem("h_hi0"), sem("h_hi1")]
        h_lo = [sem("h_lo0"), sem("h_lo1")]
        y_mm = sem("y_mm")
        y_kept = sem("y_kept")
        y_stored = [sem(f"y_stored{i}") for i in range(YB)]
        gathered = [sem(f"gathered{i}") for i in range(GB)]
        mixed = sem("mixed")
        fin_mm = sem("fin_mm")
        fin_kept = sem("fin_kept")
        out_stored = [sem("out_stored0"), sem("out_stored1")]

        block = ctx.enter_context(nc.Block())

        @block.gpsimd
        def _(pool):
            e = NE - 1

            def last_expert(half):
                c = slice(half * FF // 2, (half + 1) * FF // 2)
                r = slice(half * NF // 2, (half + 1) * NF // 2)
                pool.wait_ge(last_hi, 2 * half + 2)
                pool.tensor_tensor(w1s[:, e, LO, c], w1stage[:, HI, c], w1s[:, e, HI, c], ALU.subtract
                                   ).then_inc(last_lo, 1)
                pool.tensor_tensor(w2s[:, e, 1, r, :], w2stage[:, r, :], w2s[:, e, 0, r, :], ALU.subtract
                                   ).then_inc(last_lo, 1)
                pool.wait_ge(last_lo, 3 * half + 2)
                if half == 1:
                    pool.wait_ge(scattered, 16 * NT)
                mix = w1s[LC:128, e, MIX, c]
                pool.tensor_tensor(mix, w1stage[LC:128, MIX, c], mix, ALU.subtract).then_inc(last_lo, 1)
                pool.wait_ge(last_lo, 3 * half + 3)

            last_expert(0)
            pool.wait_ge(slots_ready, 1)
            for t in range(NT):
                pool.indirect_dma_start(out=xs, out_offset=bass.IndirectOffsetOnAxis(ap=slot[:, t:t + 1], axis=0),
                                        in_=xhl[:, t, 0:2 * C], in_offset=None
                                        ).then_inc(scattered, 16)
            last_expert(1)
            for i in range(YB):
                pool.wait_ge(y_stored[i], 16 * len(range(i, NR, YB)))
            for t in range(NT):
                if t >= GB:
                    pool.wait_ge(mixed, t - GB + 1)
                pool.indirect_dma_start(out=sel[:, t % GB, :], out_offset=None, in_=ys,
                                        in_offset=bass.IndirectOffsetOnAxis(ap=slot[:, t:t + 1], axis=0)
                                        ).then_inc(gathered[t % GB], 16)

        @block.sync
        def _(sp):
            def load(j):
                if j >= YB:
                    sp.wait_ge(tokT_mm, j - YB + 1)
                sp.dma_start(tok[:, j % YB, 0:2 * C], xs[j * T:(j + 1) * T, :]).then_inc(tok_loaded[j % YB], 16)

            sp.wait_ge(scattered, 16 * NT)
            for j in range(YB):
                load(j)
            for j in range(NR):
                if j + YB < NR:
                    load(j + YB)
                sp.wait_ge(y_kept, routed_at(j) + 1)
                sp.dma_start(ys[j * T:(j + 1) * T, :], yo[:, j % YB, :]).then_inc(y_stored[j % YB], 16)
            for b in range(B):
                sp.wait_ge(fin_kept, TPI * (b + 1))
                sp.dma_start(out[b].rearrange("(k c) i j -> c k (i j)", k=2), outc[:, b % 2, :, :]
                             ).then_inc(out_stored[b % 2], 16)
            for i in range(2):
                sp.wait_ge(out_stored[i], 16 * B // 2)

        @block.scalar
        def _(act):
            def hidden(n):
                for h in range(2):
                    act.wait_ge(h_mm[h], n + 1)
                    if n >= 2:
                        act.wait_ge(h_lo[h], n - 1)
                        act.wait_ge(y_mm, n - 1)
                    act.activation(hp[:, n % 2, 0, HF * h:HF * h + HF, :],
                                   p_h[n % 2][h][:, 0:HF * T].rearrange("p (f t) -> p f t", f=HF), ACT.Gelu,
                                   scale=1.0 / SF).then_inc(h_hi[h], 1)
                    act.activation(hf[:, n % 2, h, :], p_h[n % 2][h][:, 0:HF * T], ACT.Gelu, scale=1.0 / SF
                                   ).then_inc(h_act[h], 1)

            def tokens(j):
                act.wait_ge(tokT_mm, j + 1)
                if j >= 2:
                    act.wait_ge(h_mm[1], routed_at(j - 2) + 1)
                act.activation(tokT[:, j % 2, :, :], p_k[:, 0:2 * T].bitcast(F16).rearrange("p (b n) -> p b n", b=4),
                               ACT.Copy).then_inc(tokT_ready, 1)

            def keep_result(t):
                b = t // TPI
                act.wait_ge(fin_mm, t + 1)
                if b >= 2 and t % TPI == 0:
                    act.wait_ge(out_stored[b % 2], 16 * (b // 2))
                act.activation(outc[:, b % 2, :, (t % TPI) * T:(t % TPI + 1) * T],
                               p_f[t % 2][0:CH, 0:2 * T].rearrange("p (k n) -> p k n", k=2), ACT.Copy
                               ).then_inc(fin_kept, 1)

            def last_expert(half):
                e = NE - 1
                c = slice(half * FF // 2, (half + 1) * FF // 2)
                act.activation(w1stage[:, :, c], w1stage[:, :, c], ACT.Copy, scale=SF).then_inc(last_scaled, 1)
                act.wait_ge(last_scaled, 2 * half + 1)
                act.activation(w1s[0:LC, e, BIAS, c], w1stage[0:LC, MIX, c], ACT.Copy)
                act.activation(w1s[:, e, HI:MIX + 1, c], w1stage[:, :, c], ACT.Copy).then_inc(last_hi, 1)
                r = slice(half * NF // 2, (half + 1) * NF // 2)
                act.activation(w2stage[:, r, :], w2stage[:, r, :], ACT.Copy, scale=SF).then_inc(last_scaled, 1)
                act.wait_ge(last_scaled, 2 * half + 2)
                act.activation(w2s[:, e, 0, r, :], w2stage[:, r, :], ACT.Copy).then_inc(last_hi, 1)

            act.wait_ge(ex_in, 1)
            act.activation(ex[:, :, :], ex[:, :, :], ACT.Exp).then_inc(ex_out, 1)
            for n in range(N + 2):
                j = next_routed(n)
                if j is not None:
                    tokens(j)
                if n == 0:
                    last_expert(0)
                if n < N:
                    hidden(n)
                if n == 2:
                    last_expert(1)
                for t in mixes(n - 1):
                    keep_result(t)

        @block.vector
        def _(dve):
            dve.memset(tok[:, :, 2 * C:XW], 0.0).then_inc(consts, 1)
            dve.tensor_scalar(ohc[:, :], pid[:, 0:1].to_broadcast([2 * ER, T]), 0.0, None, ALU.is_equal
                              ).then_inc(consts, 1)
            dve.wait_ge(consts, 1)
            for one in (0, 32):
                dve.memset(tok[:, :, 2 * C + one], 1.0).then_inc(consts, 1)

            links = [0]

            def link(ins):
                links[0] += 1
                ins.then_inc(chain, 1)
                dve.wait_ge(chain, links[0])

            def by_expert(column):
                return column.unsqueeze(2).to_broadcast([128, NT, NE])

            def over_tiles(row):
                return row.unsqueeze(1).to_broadcast([128, NT, NE])

            top, total, expert, slotf = (r16[:, i, :] for i in range(4))

            def choose_experts():
                link(dve.tensor_reduce(top, lg[:, :, :], AX, ALU.max))
                link(dve.tensor_tensor(lg[:, :, :], lg[:, :, :], by_expert(top), ALU.subtract))
                dve.tensor_copy(ex[:, :, :], lg[:, :, :]).then_inc(ex_in, 1)
                link(dve.tensor_scalar(cand[:, :, :], lg[:, :, :], 0.0, float(NE), ALU.is_lt, ALU.mult))
                link(dve.tensor_tensor(cand[:, :, :], cand[:, :, :], over_tiles(eio[:, :]), ALU.add))
                link(dve.tensor_reduce(expert, cand[:, :, :], AX, ALU.min))
                dve.tensor_tensor(oh[:, :, :], over_tiles(eio[:, :]), by_expert(expert), ALU.is_equal
                                  ).then_inc(oh_ready, 1)

            def probabilities():
                dve.wait_ge(ex_out, 1)
                link(dve.tensor_reduce(total, ex[:, :, :], AX, ALU.add))
                link(dve.reciprocal(pmax[:, :], total))
                link(dve.tensor_scalar(omp[:, :], pmax[:, :], -1.0 / SF, 1.0 / SF, ALU.mult, ALU.add))

            count, tiles, first, end = (cnt[:, i, :] for i in range(4))

            def slots():
                dve.wait_ge(rank_mm, 1)
                link(dve.tensor_copy(count, p_f[0][:, 0:NE]))
                above = big[:, 0:NE * NT].rearrange("p (e k) -> p e k", e=NE)
                link(dve.tensor_tensor(above, count.unsqueeze(2).to_broadcast([128, NE, NT]),
                                       kio[:, :].unsqueeze(1).to_broadcast([128, NE, NT]), ALU.is_gt))
                link(dve.tensor_reduce(tiles, above, AX, ALU.add))
                before = big[:, 0:NE * NE].rearrange("p (e k) -> p e k", e=NE)
                link(dve.tensor_tensor(before, tiles.unsqueeze(1).to_broadcast([128, NE, NE]), ltm[:, :, :], ALU.mult))
                link(dve.tensor_reduce(first, before, AX, ALU.add))
                link(dve.tensor_tensor(end, first, tiles, ALU.add))
                link(dve.tensor_scalar(first, first, float(T), None, ALU.mult))
                link(dve.tensor_tensor(cand[:, :, :], p_k[:, 0:NT * NE].rearrange("p (t e) -> p t e", e=NE),
                                       over_tiles(first), ALU.add))
                link(dve.tensor_tensor(cand[:, :, :], cand[:, :, :], oh[:, :, :], ALU.mult))
                link(dve.tensor_reduce(slotf, cand[:, :, :], AX, ALU.add))
                dve.tensor_copy(slot[:, :], slotf).then_inc(slots_ready, 1)

            def tile_experts():
                passed = big[0:2 * ER, 0:NR * NE].rearrange("p (j e) -> p j e", e=NE)
                link(dve.tensor_tensor(passed, end[0:2 * ER, :].unsqueeze(1).to_broadcast([2 * ER, NR, NE]),
                                       jio[:, :].unsqueeze(2).to_broadcast([2 * ER, NR, NE]), ALU.is_le))
                link(dve.tensor_reduce(ejf[:, 0, :], passed, AX, ALU.add))
                link(dve.tensor_scalar(ejf[:, 1, :], ejf[:, 0, :], float(NE - 1), None, ALU.min))
                link(dve.tensor_copy(etile[:, :], ejf[0:1, 1, :]))
                dve.tensor_scalar(ohe[:, :], ejf[:, 1, :], pid[:, 0:1], None, ALU.is_equal)

            def weights_1(j):
                e = dve.value_load(etile[0:1, j:j + 1], min_val=0, max_val=NE - 1)
                if j == 0:
                    dve.wait_ge(last_lo, 6)
                if j >= 2:
                    dve.wait_ge(h_mm[1], routed_at(j - 2) + 1)
                dve.tensor_copy(w1d[:, j % 2, :, :], w1s[:, e, :, :]).then_inc(w1_copied, 1)
                return e

            def weights_2(j, e):
                if j >= 2:
                    dve.wait_ge(y_mm, routed_at(j - 2) + 1)
                dve.tensor_copy(ohd[:, j % 2, :], ohe[:, j:j + 1].to_broadcast([2 * ER, T]))
                dve.tensor_copy(w2d[:, j % 2, :, :, :], w2s[:, e, :, :, :]).then_inc(w2_copied, 1)

            def hidden_lo(n):
                for h in range(2):
                    dve.wait_ge(h_act[h], n + 1)
                    if n >= 2:
                        dve.wait_ge(y_mm, n - 1)
                    dve.tensor_tensor(hp[:, n % 2, 1, HF * h:HF * h + HF, :],
                                      hf[:, n % 2, h, :].rearrange("p (f t) -> p f t", f=HF),
                                      hp[:, n % 2, 0, HF * h:HF * h + HF, :], ALU.subtract).then_inc(h_lo[h], 1)

            def keep_y(n):
                kind, i = TILES[n]
                dve.wait_ge(y_mm, n + 1)
                if kind == "common":
                    dve.scalar_tensor_tensor(out=x2[:, i, :], in0=p_y[n % 2][:, 0:C], scalar=omp[:, i:i + 1],
                                             in1=x2[:, i, :], op0=ALU.mult, op1=ALU.add).then_inc(y_kept, 1)
                else:
                    if i >= YB:
                        dve.wait_ge(y_stored[i % YB], 16 * (i // YB))
                    dve.tensor_scalar(yo[:, i % YB, :], p_y[n % 2][:, 0:C], 1.0 / SF, None, ALU.mult
                                      ).then_inc(y_kept, 1)

            def mix(t):
                dve.wait_ge(gathered[t % GB], 16 * (t // GB + 1))
                dve.wait_ge(y_kept, common_at(t) + 1)
                if t >= FB:
                    dve.wait_ge(fin_mm, t - FB + 1)
                dve.scalar_tensor_tensor(out=fin[:, t % FB, :], in0=sel[:, t % GB, :], scalar=pmax[:, t:t + 1],
                                         in1=x2[:, t, :], op0=ALU.mult, op1=ALU.add).then_inc(mixed, 1)

            choose_experts()
            probabilities()
            for n in range(N + 1):
                j = next_routed(n)
                if j is not None:
                    e = weights_1(j)
                if n == 0:
                    slots()
                if n < N:
                    hidden_lo(n)
                if n == 1:
                    tile_experts()
                if n >= 1:
                    keep_y(n - 1)
                if j is not None:
                    weights_2(j, e)
                for t in mixes(n):
                    mix(t)

        @block.tensor
        def _(pe):
            pe.wait_ge(consts, 4)

            def tokens(j):
                pe.wait_ge(tok_loaded[j % YB], 16 * (j // YB + 1))
                if j >= 1:
                    pe.wait_ge(tokT_ready, j)
                bank = p_k[:, 0:2 * T].bitcast(F16).rearrange("p (b n) -> p b n", b=4)
                packed_transposes(pe, bank, tok[:, j % YB, :], ident16).then_inc(tokT_mm, 1)

            def hidden(n):
                kind, i = TILES[n]
                if n >= 2:
                    for h in range(2):
                        pe.wait_ge(h_act[h], n - 1)
                if kind == "common":
                    w, xT = w1s[:, 0, :, :], xhT[:, i, :, :]
                else:
                    pe.wait_ge(w1_copied, i + 1)
                    pe.wait_ge(tokT_ready, i + 1)
                    w, xT = w1d[:, i % 2, :, :], tokT[:, i % 2, :, :]
                for f in range(NF):
                    for m, (a, b, rows) in enumerate(PACKED):
                        mm = pe.matmul(p_h[n % 2][f // HF][:, (f % HF) * T:(f % HF + 1) * T],
                                       w[0:rows, a, f * 128:(f + 1) * 128], xT[0:rows, b, :],
                                       start=(m == 0), stop=(m == len(PACKED) - 1))
                    if f % HF == HF - 1:
                        mm.then_inc(h_mm[f // HF], 1)
                    if n == 0 and f == HF - 1:
                        ranks()

            def outputs(n):
                kind, i = TILES[n]
                if n >= 2:
                    pe.wait_ge(y_kept, n - 1)
                if kind == "common":
                    w, chosen = w2s[:, 0, :, :, :], ohc[:, :]
                else:
                    pe.wait_ge(w2_copied, i + 1)
                    w, chosen = w2d[:, i % 2, :, :, :], ohd[:, i % 2, :]
                y = p_y[n % 2][:, 0:C]
                pe.matmul(y, chosen, b2s[:, :], start=True, stop=False)
                for f in range(NF):
                    if f % HF == 0:
                        pe.wait_ge(h_lo[f // HF], n + 1)
                    for m, (a, b) in enumerate(PASSES):
                        mm = pe.matmul(y, hp[:, n % 2, a, f, :], w[:, b, f, :], start=False,
                                       stop=(f == NF - 1 and m == 2))
                mm.then_inc(y_mm, 1)

            def ranks():
                pe.wait_ge(oh_ready, 1)
                flat = oh[:, :, :].rearrange("p t e -> p (t e)")
                pe.matmul(p_k[:, 0:NT * NE], tri[:, :], flat, start=True, stop=False, skip_group_check=True)
                for d in range(1, NT):
                    pe.matmul(p_k[:, d * NE:NT * NE], ones16[:, :], flat[:, 0:(NT - d) * NE], start=False,
                              stop=(d == NT - 1), skip_group_check=True)
                for t in range(NT):
                    mm = pe.matmul(p_f[0][:, 0:NE], ones16[:, :], oh[:, t, :], start=(t == 0), stop=(t == NT - 1))
                mm.then_inc(rank_mm, 1)

            def result_to_channels(t):
                pe.wait_ge(mixed, t + 1)
                if t >= 2:
                    pe.wait_ge(fin_kept, t - 1)
                elif t == 1:
                    pe.wait_ge(tokT_ready, NR)
                for k in range(2):
                    mm = pe.transpose(p_f[t % 2][0:CH, k * T:(k + 1) * T], fin[:, t % FB, k * CH:(k + 1) * CH],
                                      ident[:, :])
                mm.then_inc(fin_mm, 1)

            for n in range(N + 2):
                j = next_routed(n)
                if j is not None:
                    tokens(j)
                if n < N:
                    hidden(n)
                results = list(mixes(n - 1))
                if n < N:
                    for t in results[:2]:
                        result_to_channels(t)
                    results = results[2:]
                if 1 <= n <= N:
                    outputs(n - 1)
                for t in results:
                    result_to_channels(t)


_INS = ['x', 'L0_conv_Wq', 'L0_conv_Wk', 'L0_conv_Wv', 'L0_conv_Wo_w', 'L0_conv_Wo_b', 'L0_conv_rel_pos_bias',
        'L0_conv_rel_coords', 'L0_ffn_Ws', 'L0_ffn_bs', 'L0_ffn_W1', 'L0_ffn_b1', 'L0_ffn_W2', 'L0_ffn_b2']
_OUTS = [((B, C, IMG, IMG), 'float32')]


def kernel(**inputs):
    import numpy as _np
    import concourse.bacc as _bacc
    from concourse import mybir as _mybir
    from concourse.bass_utils import run_bass_kernel_spmd as _run

    nc = _bacc.Bacc("TRN2", target_bir_lowering=False, num_devices=1)
    arrays, args = {}, []
    for name in _INS:
        a = _np.ascontiguousarray(inputs[name])
        arrays[f"in_{name}_dram"] = a
        args.append(nc.dram_tensor(f"in_{name}_dram", a.shape, _mybir.dt.from_np(a.dtype), kind="ExternalInput").ap())
    for i, (shape, dtype) in enumerate(_OUTS):
        dt = _mybir.dt.from_np(_np.dtype(dtype))
        args.append(nc.dram_tensor(f"out_{i}_dram", shape, dt, kind="ExternalOutput").ap())
    build(nc, *args)
    r = _run(nc, [arrays], core_ids=[0])
    got = tuple(r.results[0][f"out_{i}_dram"] for i in range(len(_OUTS)))
    return got[0]
```
